# Optimizing a Trainium2 kernel written in Bass

```python
import numpy as np
import jax
import jax.numpy as jnp

def _softmax(x, axis=-1):
    return jax.nn.softmax(x, axis=axis)

def _gelu(x):
    return jax.nn.gelu(x, approximate=True)

def _silu(x):
    return jax.nn.silu(x)

def _sigmoid(x):
    return jax.nn.sigmoid(x)

def _layernorm(x, axis=-1, eps=1e-05):
    m = jnp.mean(x, axis=axis, keepdims=True)
    v = jnp.var(x, axis=axis, keepdims=True)
    return (x - m) / jnp.sqrt(v + eps)

def _scatter_add(tgt, idx, src, axis=0):
    return tgt.at[idx].add(src)

def _segment_sum(src, seg, n):
    return jax.ops.segment_sum(src, seg, n)
kernel_name = 'mk_conv_seq_d4_conv_nhwc768_r4_a6371a'

def setup_inputs(seed: int=0):
    np.random.seed(seed)
    _w = jnp.asarray

    def _rec_inputs():
        import jax
        import jax.numpy as jnp
        _gk = jax.random.key(seed)
        x = -0.0004039 + 1 * jax.random.normal(jax.random.fold_in(_gk, 1), (4, 16, 16, 192), jnp.float32)
        return x
    x = _rec_inputs()

    def _L0_conv_setup():
        import jax, jax.numpy as jnp
        import numpy as np
        B, H, W = (4, 16, 16)
        DIM, HEADS, HEAD = (192, 12, 16)
        WIN = 14
        MLP_DIM = 4 * DIM
        EPS = 1e-05

        def _ln(x, g, b):
            mu = jnp.mean(x, axis=-1, keepdims=True)
            var = jnp.mean(jnp.square(x - mu), axis=-1, keepdims=True)
            return (x - mu) * jax.lax.rsqrt(var + EPS) * g + b

        def _window_partition(x):
            Bb, Hh, Ww, C = x.shape
            pad_h = (WIN - Hh % WIN) % WIN
            pad_w = (WIN - Ww % WIN) % WIN
            x = jnp.pad(x, ((0, 0), (0, pad_h), (0, pad_w), (0, 0)))
            Hp, Wp = (Hh + pad_h, Ww + pad_w)
            x = x.reshape(Bb, Hp // WIN, WIN, Wp // WIN, WIN, C)
            win = x.transpose(0, 1, 3, 2, 4, 5).reshape(-1, WIN, WIN, C)
            return (win, (Hp, Wp))

        def _window_unpartition(win, pad_hw, hw):
            Hp, Wp = pad_hw
            Hh, Ww = hw
            Bb = win.shape[0] // (Hp * Wp // WIN // WIN)
            x = win.reshape(Bb, Hp // WIN, Wp // WIN, WIN, WIN, -1)
            x = x.transpose(0, 1, 3, 2, 4, 5).reshape(Bb, Hp, Wp, -1)
            return x[:, :Hh, :Ww, :]

        def _attention(xw, qkv_w, qkv_b, proj_w, proj_b, rel_pos_h, rel_pos_w):
            Bw = xw.shape[0]
            N = WIN * WIN
            qkv = xw.reshape(Bw, N, DIM) @ qkv_w + qkv_b
            qkv = qkv.reshape(Bw, N, 3, HEADS, HEAD)
            qkv = qkv.transpose(2, 0, 3, 1, 4).reshape(3, Bw * HEADS, N, HEAD)
            q, k, v = (qkv[0], qkv[1], qkv[2])
            scale = HEAD ** (-0.5)
            attn = jnp.einsum('bqc,bkc->bqk', q * scale, k)
            idx = jnp.arange(WIN)[:, None] - jnp.arange(WIN)[None, :] + (WIN - 1)
            Rh = rel_pos_h[idx]
            Rw = rel_pos_w[idx]
            r_q = q.reshape(-1, WIN, WIN, HEAD)
            rel_h = jnp.einsum('bhwc,hkc->bhwk', r_q, Rh)
            rel_w = jnp.einsum('bhwc,wkc->bhwk', r_q, Rw)
            attn = attn.reshape(-1, WIN, WIN, WIN, WIN) + rel_h[..., None] + rel_w[..., None, :]
            attn = jax.nn.softmax(attn.reshape(-1, N, N), axis=-1)
            out = attn @ v
            out = out.reshape(Bw, HEADS, WIN, WIN, HEAD).transpose(0, 2, 3, 1, 4)
            out = out.reshape(Bw, WIN, WIN, DIM)
            return out @ proj_w + proj_b
        key = jax.random.key(seed)
        ks = jax.random.split(key, 8)
        s = 0.02
        return {'x': jax.random.normal(ks[0], (B, H, W, DIM), jnp.float32), 'norm1_g': jnp.ones((DIM,), jnp.float32), 'norm1_b': jnp.zeros((DIM,), jnp.float32), 'qkv_w': jax.random.normal(ks[1], (DIM, 3 * DIM), jnp.float32) * s, 'qkv_b': jnp.zeros((3 * DIM,), jnp.float32), 'proj_w': jax.random.normal(ks[2], (DIM, DIM), jnp.float32) * s, 'proj_b': jnp.zeros((DIM,), jnp.float32), 'rel_pos_h': jax.random.normal(ks[3], (2 * WIN - 1, HEAD), jnp.float32) * s, 'rel_pos_w': jax.random.normal(ks[4], (2 * WIN - 1, HEAD), jnp.float32) * s, 'norm2_g': jnp.ones((DIM,), jnp.float32), 'norm2_b': jnp.zeros((DIM,), jnp.float32), 'mlp_w1': jax.random.normal(ks[5], (DIM, MLP_DIM), jnp.float32) * s, 'mlp_b1': jnp.zeros((MLP_DIM,), jnp.float32), 'mlp_w2': jax.random.normal(ks[6], (MLP_DIM, DIM), jnp.float32) * s, 'mlp_b2': jnp.zeros((DIM,), jnp.float32)}
    _L0_conv_all = _L0_conv_setup()
    _L0_conv_in = {k: v for k, v in _L0_conv_all.items() if k in ('norm1_g', 'norm1_b', 'qkv_w', 'qkv_b', 'proj_w', 'proj_b', 'rel_pos_h', 'rel_pos_w', 'norm2_g', 'norm2_b', 'mlp_w1', 'mlp_b1', 'mlp_w2', 'mlp_b2')}
    del _L0_conv_all

    def _L1_conv_setup():
        import jax, jax.numpy as jnp
        import numpy as np
        B, H, W, C = (8, 16, 16, 192)
        WIN = 16
        NH, HD = (12, 48)

        def _layer_norm(x, scale, offset, eps=1e-05):
            m = jnp.mean(x, axis=-1, keepdims=True)
            v = jnp.var(x, axis=-1, keepdims=True)
            return (x - m) * jax.lax.rsqrt(v + eps) * scale + offset
        key = jax.random.key(seed)
        ks = jax.random.split(key, 10)
        s = 0.02
        return {'x': jax.random.normal(ks[0], (B, H, W, C), jnp.float32), 'wq': jax.random.normal(ks[1], (C, NH * HD), jnp.float32) * s, 'bq': jnp.zeros((NH * HD,), jnp.float32), 'wk': jax.random.normal(ks[2], (C, NH * HD), jnp.float32) * s, 'bk': jnp.zeros((NH * HD,), jnp.float32), 'wv': jax.random.normal(ks[3], (C, NH * HD), jnp.float32) * s, 'bv': jnp.zeros((NH * HD,), jnp.float32), 'rel_pos_0': jax.random.normal(ks[4], (2 * WIN - 1, HD), jnp.float32) * s, 'rel_pos_1': jax.random.normal(ks[5], (2 * WIN - 1, HD), jnp.float32) * s, 'wo': jax.random.normal(ks[6], (NH * HD, C), jnp.float32) * s, 'bo': jnp.zeros((C,), jnp.float32), 'ln1_scale': jnp.ones((C,), jnp.float32), 'ln1_offset': jnp.zeros((C,), jnp.float32), 'ln2_scale': jnp.ones((C,), jnp.float32), 'ln2_offset': jnp.zeros((C,), jnp.float32), 'w1': jax.random.normal(ks[7], (C, 4 * C), jnp.float32) * s, 'b1': jnp.zeros((4 * C,), jnp.float32), 'w2': jax.random.normal(ks[8], (4 * C, C), jnp.float32) * s, 'b2': jnp.zeros((C,), jnp.float32)}
    _L1_conv_all = _L1_conv_setup()
    _L1_conv_in = {k: v for k, v in _L1_conv_all.items() if k in ('wq', 'bq', 'wk', 'bk', 'wv', 'bv', 'rel_pos_0', 'rel_pos_1', 'wo', 'bo', 'ln1_scale', 'ln1_offset', 'ln2_scale', 'ln2_offset', 'w1', 'b1', 'w2', 'b2')}
    del _L1_conv_all

    def _L2_conv_setup():
        import jax, jax.numpy as jnp
        import numpy as np
        B, H, W = (8, 16, 16)
        EMBED, HEADS, HEAD_DIM = (192, 12, 16)
        FF = 768
        WS = 14
        SCALE = HEAD_DIM ** (-0.5)
        EPS = 1e-06

        def layer_norm(x, g, b):
            m = jnp.mean(x, axis=-1, keepdims=True)
            v = jnp.mean(jnp.square(x - m), axis=-1, keepdims=True)
            return (x - m) * jax.lax.rsqrt(v + EPS) * g + b

        def window_partition(x):
            b, h, w, c = x.shape
            ph, pw = (-h % WS, -w % WS)
            x = jnp.pad(x, ((0, 0), (0, ph), (0, pw), (0, 0)))
            hp, wp = (h + ph, w + pw)
            x = x.reshape(b, hp // WS, WS, wp // WS, WS, c)
            x = x.transpose(0, 1, 3, 2, 4, 5).reshape(-1, WS, WS, c)
            return (x, (hp, wp))

        def window_unpartition(win, pad_hw, hw):
            hp, wp = pad_hw
            h, w = hw
            b = win.shape[0] // (hp // WS * (wp // WS))
            x = win.reshape(b, hp // WS, wp // WS, WS, WS, -1)
            x = x.transpose(0, 1, 3, 2, 4, 5).reshape(b, hp, wp, -1)
            return x[:, :h, :w, :]

        def attention(xw, w_qkv, b_qkv, w_proj, b_proj, rel_pos_h, rel_pos_w):
            bw, hs, ws_, c = xw.shape
            n = hs * ws_
            qkv = (xw.reshape(bw, n, c) @ w_qkv + b_qkv).reshape(bw, n, 3, HEADS, HEAD_DIM)
            q, k, v = jnp.moveaxis(qkv, 2, 0)
            q = q.transpose(0, 2, 1, 3)
            k = k.transpose(0, 2, 1, 3)
            v = v.transpose(0, 2, 1, 3)
            attn = jnp.einsum('bhnd,bhmd->bhnm', q * SCALE, k)
            idx = jnp.arange(WS)[:, None] - jnp.arange(WS)[None, :] + (WS - 1)
            Rh = rel_pos_h[idx]
            Rw = rel_pos_w[idx]
            r_q = q.reshape(bw, HEADS, WS, WS, HEAD_DIM)
            rel_h = jnp.einsum('bhpqd,pkd->bhpqk', r_q, Rh)
            rel_w = jnp.einsum('bhpqd,qkd->bhpqk', r_q, Rw)
            attn = attn.reshape(bw, HEADS, WS, WS, WS, WS)
            attn = attn + rel_h[..., :, None] + rel_w[..., None, :]
            attn = jax.nn.softmax(attn.reshape(bw, HEADS, n, n), axis=-1)
            out = jnp.einsum('bhnm,bhmd->bhnd', attn, v)
            out = out.transpose(0, 2, 1, 3).reshape(bw, hs, ws_, c)
            return out @ w_proj + b_proj
        key = jax.random.key(seed)
        ks = jax.random.split(key, 8)

        def n(k, shp, s=0.02):
            return jax.random.normal(k, shp, jnp.float32) * s
        return {'x': jax.random.normal(ks[0], (B, H, W, EMBED), jnp.float32), 'g1': jnp.ones((EMBED,), jnp.float32), 'beta1': jnp.zeros((EMBED,), jnp.float32), 'w_qkv': n(ks[1], (EMBED, 3 * EMBED)), 'b_qkv': jnp.zeros((3 * EMBED,), jnp.float32), 'w_proj': n(ks[2], (EMBED, EMBED)), 'b_proj': jnp.zeros((EMBED,), jnp.float32), 'rel_pos_h': n(ks[3], (2 * WS - 1, HEAD_DIM)), 'rel_pos_w': n(ks[4], (2 * WS - 1, HEAD_DIM)), 'g2': jnp.ones((EMBED,), jnp.float32), 'beta2': jnp.zeros((EMBED,), jnp.float32), 'w_fc1': n(ks[5], (EMBED, FF)), 'b_fc1': jnp.zeros((FF,), jnp.float32), 'w_fc2': n(ks[6], (FF, EMBED)), 'b_fc2': jnp.zeros((EMBED,), jnp.float32)}
    _L2_conv_all = _L2_conv_setup()
    _L2_conv_in = {k: v for k, v in _L2_conv_all.items() if k in ('g1', 'beta1', 'w_qkv', 'b_qkv', 'w_proj', 'b_proj', 'rel_pos_h', 'rel_pos_w', 'g2', 'beta2', 'w_fc1', 'b_fc1', 'w_fc2', 'b_fc2')}
    del _L2_conv_all

    def _L3_conv_setup():
        import jax, jax.numpy as jnp
        import numpy as np
        NUM_BLOCKS = 8
        SPARSITY = 0.01
        HARD_FRAC = 1.0
        HSF = 1
        SCALE = 0.02

        def _softshrink(v, lambd):
            return jnp.where(v > lambd, v - lambd, jnp.where(v < -lambd, v + lambd, jnp.zeros_like(v)))
        key = jax.random.key(seed)
        ks = jax.random.split(key, 5)
        B, H, W, C = (8, 32, 32, 192)
        bs = C // NUM_BLOCKS
        x = jax.random.normal(ks[0], (B, H, W, C), dtype=jnp.float32)
        w1 = SCALE * jax.random.normal(ks[1], (2, NUM_BLOCKS, bs, bs * HSF), dtype=jnp.float32)
        b1 = SCALE * jax.random.normal(ks[2], (2, NUM_BLOCKS, bs * HSF), dtype=jnp.float32)
        w2 = SCALE * jax.random.normal(ks[3], (2, NUM_BLOCKS, bs * HSF, bs), dtype=jnp.float32)
        b2 = SCALE * jax.random.normal(ks[4], (2, NUM_BLOCKS, bs), dtype=jnp.float32)
        return {'x': x, 'w1': w1, 'b1': b1, 'w2': w2, 'b2': b2}
    _L3_conv_all = _L3_conv_setup()
    _L3_conv_in = {k: v for k, v in _L3_conv_all.items() if k in ('w1', 'b1', 'w2', 'b2')}
    del _L3_conv_all
    return {'x': x, 'L0_conv_norm1_g': _L0_conv_in['norm1_g'], 'L0_conv_norm1_b': _L0_conv_in['norm1_b'], 'L0_conv_qkv_w': _L0_conv_in['qkv_w'], 'L0_conv_qkv_b': _L0_conv_in['qkv_b'], 'L0_conv_proj_w': _L0_conv_in['proj_w'], 'L0_conv_proj_b': _L0_conv_in['proj_b'], 'L0_conv_rel_pos_h': _L0_conv_in['rel_pos_h'], 'L0_conv_rel_pos_w': _L0_conv_in['rel_pos_w'], 'L0_conv_norm2_g': _L0_conv_in['norm2_g'], 'L0_conv_norm2_b': _L0_conv_in['norm2_b'], 'L0_conv_mlp_w1': _L0_conv_in['mlp_w1'], 'L0_conv_mlp_b1': _L0_conv_in['mlp_b1'], 'L0_conv_mlp_w2': _L0_conv_in['mlp_w2'], 'L0_conv_mlp_b2': _L0_conv_in['mlp_b2'], 'L1_conv_wq': _L1_conv_in['wq'], 'L1_conv_bq': _L1_conv_in['bq'], 'L1_conv_wk': _L1_conv_in['wk'], 'L1_conv_bk': _L1_conv_in['bk'], 'L1_conv_wv': _L1_conv_in['wv'], 'L1_conv_bv': _L1_conv_in['bv'], 'L1_conv_rel_pos_0': _L1_conv_in['rel_pos_0'], 'L1_conv_rel_pos_1': _L1_conv_in['rel_pos_1'], 'L1_conv_wo': _L1_conv_in['wo'], 'L1_conv_bo': _L1_conv_in['bo'], 'L1_conv_ln1_scale': _L1_conv_in['ln1_scale'], 'L1_conv_ln1_offset': _L1_conv_in['ln1_offset'], 'L1_conv_ln2_scale': _L1_conv_in['ln2_scale'], 'L1_conv_ln2_offset': _L1_conv_in['ln2_offset'], 'L1_conv_w1': _L1_conv_in['w1'], 'L1_conv_b1': _L1_conv_in['b1'], 'L1_conv_w2': _L1_conv_in['w2'], 'L1_conv_b2': _L1_conv_in['b2'], 'L2_conv_g1': _L2_conv_in['g1'], 'L2_conv_beta1': _L2_conv_in['beta1'], 'L2_conv_w_qkv': _L2_conv_in['w_qkv'], 'L2_conv_b_qkv': _L2_conv_in['b_qkv'], 'L2_conv_w_proj': _L2_conv_in['w_proj'], 'L2_conv_b_proj': _L2_conv_in['b_proj'], 'L2_conv_rel_pos_h': _L2_conv_in['rel_pos_h'], 'L2_conv_rel_pos_w': _L2_conv_in['rel_pos_w'], 'L2_conv_g2': _L2_conv_in['g2'], 'L2_conv_beta2': _L2_conv_in['beta2'], 'L2_conv_w_fc1': _L2_conv_in['w_fc1'], 'L2_conv_b_fc1': _L2_conv_in['b_fc1'], 'L2_conv_w_fc2': _L2_conv_in['w_fc2'], 'L2_conv_b_fc2': _L2_conv_in['b_fc2'], 'L3_conv_w1': _L3_conv_in['w1'], 'L3_conv_b1': _L3_conv_in['b1'], 'L3_conv_w2': _L3_conv_in['w2'], 'L3_conv_b2': _L3_conv_in['b2']}

def reference(x, L0_conv_norm1_g, L0_conv_norm1_b, L0_conv_qkv_w, L0_conv_qkv_b, L0_conv_proj_w, L0_conv_proj_b, L0_conv_rel_pos_h, L0_conv_rel_pos_w, L0_conv_norm2_g, L0_conv_norm2_b, L0_conv_mlp_w1, L0_conv_mlp_b1, L0_conv_mlp_w2, L0_conv_mlp_b2, L1_conv_wq, L1_conv_bq, L1_conv_wk, L1_conv_bk, L1_conv_wv, L1_conv_bv, L1_conv_rel_pos_0, L1_conv_rel_pos_1, L1_conv_wo, L1_conv_bo, L1_conv_ln1_scale, L1_conv_ln1_offset, L1_conv_ln2_scale, L1_conv_ln2_offset, L1_conv_w1, L1_conv_b1, L1_conv_w2, L1_conv_b2, L2_conv_g1, L2_conv_beta1, L2_conv_w_qkv, L2_conv_b_qkv, L2_conv_w_proj, L2_conv_b_proj, L2_conv_rel_pos_h, L2_conv_rel_pos_w, L2_conv_g2, L2_conv_beta2, L2_conv_w_fc1, L2_conv_b_fc1, L2_conv_w_fc2, L2_conv_b_fc2, L3_conv_w1, L3_conv_b1, L3_conv_w2, L3_conv_b2):
    import jax
    import jax.numpy as jnp

    def _L0_conv_ref(x, norm1_g, norm1_b, qkv_w, qkv_b, proj_w, proj_b, rel_pos_h, rel_pos_w, norm2_g, norm2_b, mlp_w1, mlp_b1, mlp_w2, mlp_b2):
        import jax, jax.numpy as jnp
        import numpy as np
        B, H, W = (4, 16, 16)
        DIM, HEADS, HEAD = (192, 12, 16)
        WIN = 14
        MLP_DIM = 4 * DIM
        EPS = 1e-05

        def _ln(x, g, b):
            mu = jnp.mean(x, axis=-1, keepdims=True)
            var = jnp.mean(jnp.square(x - mu), axis=-1, keepdims=True)
            return (x - mu) * jax.lax.rsqrt(var + EPS) * g + b

        def _window_partition(x):
            Bb, Hh, Ww, C = x.shape
            pad_h = (WIN - Hh % WIN) % WIN
            pad_w = (WIN - Ww % WIN) % WIN
            x = jnp.pad(x, ((0, 0), (0, pad_h), (0, pad_w), (0, 0)))
            Hp, Wp = (Hh + pad_h, Ww + pad_w)
            x = x.reshape(Bb, Hp // WIN, WIN, Wp // WIN, WIN, C)
            win = x.transpose(0, 1, 3, 2, 4, 5).reshape(-1, WIN, WIN, C)
            return (win, (Hp, Wp))

        def _window_unpartition(win, pad_hw, hw):
            Hp, Wp = pad_hw
            Hh, Ww = hw
            Bb = win.shape[0] // (Hp * Wp // WIN // WIN)
            x = win.reshape(Bb, Hp // WIN, Wp // WIN, WIN, WIN, -1)
            x = x.transpose(0, 1, 3, 2, 4, 5).reshape(Bb, Hp, Wp, -1)
            return x[:, :Hh, :Ww, :]

        def _attention(xw, qkv_w, qkv_b, proj_w, proj_b, rel_pos_h, rel_pos_w):
            Bw = xw.shape[0]
            N = WIN * WIN
            qkv = xw.reshape(Bw, N, DIM) @ qkv_w + qkv_b
            qkv = qkv.reshape(Bw, N, 3, HEADS, HEAD)
            qkv = qkv.transpose(2, 0, 3, 1, 4).reshape(3, Bw * HEADS, N, HEAD)
            q, k, v = (qkv[0], qkv[1], qkv[2])
            scale = HEAD ** (-0.5)
            attn = jnp.einsum('bqc,bkc->bqk', q * scale, k)
            idx = jnp.arange(WIN)[:, None] - jnp.arange(WIN)[None, :] + (WIN - 1)
            Rh = rel_pos_h[idx]
            Rw = rel_pos_w[idx]
            r_q = q.reshape(-1, WIN, WIN, HEAD)
            rel_h = jnp.einsum('bhwc,hkc->bhwk', r_q, Rh)
            rel_w = jnp.einsum('bhwc,wkc->bhwk', r_q, Rw)
            attn = attn.reshape(-1, WIN, WIN, WIN, WIN) + rel_h[..., None] + rel_w[..., None, :]
            attn = jax.nn.softmax(attn.reshape(-1, N, N), axis=-1)
            out = attn @ v
            out = out.reshape(Bw, HEADS, WIN, WIN, HEAD).transpose(0, 2, 3, 1, 4)
            out = out.reshape(Bw, WIN, WIN, DIM)
            return out @ proj_w + proj_b
        shortcut = x
        x = _ln(x, norm1_g, norm1_b)
        win, pad_hw = _window_partition(x)
        win = _attention(win, qkv_w, qkv_b, proj_w, proj_b, rel_pos_h, rel_pos_w)
        x = _window_unpartition(win, pad_hw, (H, W))
        x = shortcut + x
        y = _ln(x, norm2_g, norm2_b)
        y = jax.nn.gelu(y @ mlp_w1 + mlp_b1, approximate=False) @ mlp_w2 + mlp_b2
        return x + y

    def _L1_conv_ref(x, wq, bq, wk, bk, wv, bv, rel_pos_0, rel_pos_1, wo, bo, ln1_scale, ln1_offset, ln2_scale, ln2_offset, w1, b1, w2, b2):
        import jax, jax.numpy as jnp
        import numpy as np
        B, H, W, C = (8, 16, 16, 192)
        WIN = 16
        NH, HD = (12, 48)

        def _layer_norm(x, scale, offset, eps=1e-05):
            m = jnp.mean(x, axis=-1, keepdims=True)
            v = jnp.var(x, axis=-1, keepdims=True)
            return (x - m) * jax.lax.rsqrt(v + eps) * scale + offset
        b, h, w, c = x.shape
        wh = ww = WIN
        nH, nW = (h // wh, w // ww)
        T = wh * ww
        shortcut = x
        xn = _layer_norm(x, ln1_scale, ln1_offset)
        xw = xn.reshape(b, nH, wh, nW, ww, c).transpose(0, 1, 3, 2, 4, 5)
        xw = xw.reshape(b * nH * nW, T, c)
        q = (xw @ wq + bq).reshape(-1, T, NH, HD)
        k = (xw @ wk + bk).reshape(-1, T, NH, HD)
        v = (xw @ wv + bv).reshape(-1, T, NH, HD)
        logits = jnp.einsum('nthd,nThd->nhtT', q, k) / np.float32(np.sqrt(HD))
        coords = jnp.arange(WIN)[:, None] - jnp.arange(WIN)[None, :] + (WIN - 1)
        Rh = rel_pos_0[coords]
        Rw = rel_pos_1[coords]
        qg = q.reshape(-1, wh, ww, NH, HD)
        bias_h = jnp.einsum('nabhd,akd->nhabk', qg, Rh)
        bias_w = jnp.einsum('nabhd,bkd->nhabk', qg, Rw)
        logits = logits.reshape(-1, NH, wh, ww, wh, ww)
        logits = logits + bias_h[..., :, None] + bias_w[..., None, :]
        logits = logits.reshape(-1, NH, T, T)
        attn = jax.nn.softmax(logits, axis=-1)
        out = jnp.einsum('nhtT,nThd->nthd', attn, v).reshape(-1, T, NH * HD)
        out = out @ wo + bo
        out = out.reshape(b, nH, nW, wh, ww, c).transpose(0, 1, 3, 2, 4, 5)
        out = out.reshape(b, h, w, c)
        x2 = shortcut + out
        mlp_in = _layer_norm(x2, ln2_scale, ln2_offset)
        mlp = jax.nn.gelu(mlp_in @ w1 + b1) @ w2 + b2
        return x2 + mlp

    def _L2_conv_ref(x, g1, beta1, w_qkv, b_qkv, w_proj, b_proj, rel_pos_h, rel_pos_w, g2, beta2, w_fc1, b_fc1, w_fc2, b_fc2):
        import jax, jax.numpy as jnp
        import numpy as np
        B, H, W = (8, 16, 16)
        EMBED, HEADS, HEAD_DIM = (192, 12, 16)
        FF = 768
        WS = 14
        SCALE = HEAD_DIM ** (-0.5)
        EPS = 1e-06

        def layer_norm(x, g, b):
            m = jnp.mean(x, axis=-1, keepdims=True)
            v = jnp.mean(jnp.square(x - m), axis=-1, keepdims=True)
            return (x - m) * jax.lax.rsqrt(v + EPS) * g + b

        def window_partition(x):
            b, h, w, c = x.shape
            ph, pw = (-h % WS, -w % WS)
            x = jnp.pad(x, ((0, 0), (0, ph), (0, pw), (0, 0)))
            hp, wp = (h + ph, w + pw)
            x = x.reshape(b, hp // WS, WS, wp // WS, WS, c)
            x = x.transpose(0, 1, 3, 2, 4, 5).reshape(-1, WS, WS, c)
            return (x, (hp, wp))

        def window_unpartition(win, pad_hw, hw):
            hp, wp = pad_hw
            h, w = hw
            b = win.shape[0] // (hp // WS * (wp // WS))
            x = win.reshape(b, hp // WS, wp // WS, WS, WS, -1)
            x = x.transpose(0, 1, 3, 2, 4, 5).reshape(b, hp, wp, -1)
            return x[:, :h, :w, :]

        def attention(xw, w_qkv, b_qkv, w_proj, b_proj, rel_pos_h, rel_pos_w):
            bw, hs, ws_, c = xw.shape
            n = hs * ws_
            qkv = (xw.reshape(bw, n, c) @ w_qkv + b_qkv).reshape(bw, n, 3, HEADS, HEAD_DIM)
            q, k, v = jnp.moveaxis(qkv, 2, 0)
            q = q.transpose(0, 2, 1, 3)
            k = k.transpose(0, 2, 1, 3)
            v = v.transpose(0, 2, 1, 3)
            attn = jnp.einsum('bhnd,bhmd->bhnm', q * SCALE, k)
            idx = jnp.arange(WS)[:, None] - jnp.arange(WS)[None, :] + (WS - 1)
            Rh = rel_pos_h[idx]
            Rw = rel_pos_w[idx]
            r_q = q.reshape(bw, HEADS, WS, WS, HEAD_DIM)
            rel_h = jnp.einsum('bhpqd,pkd->bhpqk', r_q, Rh)
            rel_w = jnp.einsum('bhpqd,qkd->bhpqk', r_q, Rw)
            attn = attn.reshape(bw, HEADS, WS, WS, WS, WS)
            attn = attn + rel_h[..., :, None] + rel_w[..., None, :]
            attn = jax.nn.softmax(attn.reshape(bw, HEADS, n, n), axis=-1)
            out = jnp.einsum('bhnm,bhmd->bhnd', attn, v)
            out = out.transpose(0, 2, 1, 3).reshape(bw, hs, ws_, c)
            return out @ w_proj + b_proj
        shortcut = x
        h = layer_norm(x, g1, beta1)
        win, pad_hw = window_partition(h)
        a = attention(win, w_qkv, b_qkv, w_proj, b_proj, rel_pos_h, rel_pos_w)
        a = window_unpartition(a, pad_hw, (x.shape[1], x.shape[2]))
        x = shortcut + a
        h2 = layer_norm(x, g2, beta2)
        mlp = jax.nn.gelu(h2 @ w_fc1 + b_fc1, approximate=False) @ w_fc2 + b_fc2
        return x + mlp

    def _L3_conv_ref(x, w1, b1, w2, b2):
        import jax, jax.numpy as jnp
        import numpy as np
        NUM_BLOCKS = 8
        SPARSITY = 0.01
        HARD_FRAC = 1.0
        HSF = 1
        SCALE = 0.02

        def _softshrink(v, lambd):
            return jnp.where(v > lambd, v - lambd, jnp.where(v < -lambd, v + lambd, jnp.zeros_like(v)))
        B, H, W, C = x.shape
        bs = C // NUM_BLOCKS
        bias = x
        xf = jnp.fft.rfft2(x, axes=(1, 2), norm='ortho')
        Wf = W // 2 + 1
        xf = xf.reshape(B, H, Wf, NUM_BLOCKS, bs)
        total_modes = H // 2 + 1
        kept = int(total_modes * HARD_FRAC)
        h0 = total_modes - kept
        h1 = min(total_modes + kept, H)
        w1k = min(kept, Wf)
        xs = xf[:, h0:h1, :w1k]
        xr, xi = (jnp.real(xs), jnp.imag(xs))
        o1r = jax.nn.relu(jnp.einsum('bhwni,nio->bhwno', xr, w1[0]) - jnp.einsum('bhwni,nio->bhwno', xi, w1[1]) + b1[0])
        o1i = jax.nn.relu(jnp.einsum('bhwni,nio->bhwno', xi, w1[0]) + jnp.einsum('bhwni,nio->bhwno', xr, w1[1]) + b1[1])
        o2r = jnp.einsum('bhwno,noi->bhwni', o1r, w2[0]) - jnp.einsum('bhwno,noi->bhwni', o1i, w2[1]) + b2[0]
        o2i = jnp.einsum('bhwno,noi->bhwni', o1i, w2[0]) + jnp.einsum('bhwno,noi->bhwni', o1r, w2[1]) + b2[1]
        o2r = _softshrink(o2r, SPARSITY)
        o2i = _softshrink(o2i, SPARSITY)
        out = jnp.zeros((B, H, Wf, NUM_BLOCKS, bs), dtype=xf.dtype)
        out = out.at[:, h0:h1, :w1k].set(o2r + 1j * o2i)
        out = out.reshape(B, H, Wf, C)
        y = jnp.fft.irfft2(out, s=(H, W), axes=(1, 2), norm='ortho')
        return y + bias

    def _gn(v, G=32, eps=1e-05):
        B_, H_, W_, C_ = v.shape
        g = v.reshape(B_, H_, W_, G, C_ // G)
        m = jnp.mean(g, axis=(1, 2, 4), keepdims=True)
        s = jnp.var(g, axis=(1, 2, 4), keepdims=True)
        return ((g - m) / jnp.sqrt(s + eps)).reshape(v.shape)

    def _ln_c(v, eps=1e-06):
        m = jnp.mean(v, axis=-1, keepdims=True)
        s = jnp.var(v, axis=-1, keepdims=True)
        return (v - m) / jnp.sqrt(s + eps)

    def _ln_t(v, eps=1e-05):
        m = jnp.mean(v, axis=-1, keepdims=True)
        s = jnp.var(v, axis=-1, keepdims=True)
        return (v - m) / jnp.sqrt(s + eps)

    def _to_tokens(v):
        B_, H_, W_, C_ = v.shape
        return v.reshape(B_, H_ * W_, C_)

    def _from_tokens(t, like):
        return t.reshape(like.shape)
    x = _L0_conv_ref(x, L0_conv_norm1_g, L0_conv_norm1_b, L0_conv_qkv_w, L0_conv_qkv_b, L0_conv_proj_w, L0_conv_proj_b, L0_conv_rel_pos_h, L0_conv_rel_pos_w, L0_conv_norm2_g, L0_conv_norm2_b, L0_conv_mlp_w1, L0_conv_mlp_b1, L0_conv_mlp_w2, L0_conv_mlp_b2)
    x = _L1_conv_ref(x, L1_conv_wq, L1_conv_bq, L1_conv_wk, L1_conv_bk, L1_conv_wv, L1_conv_bv, L1_conv_rel_pos_0, L1_conv_rel_pos_1, L1_conv_wo, L1_conv_bo, L1_conv_ln1_scale, L1_conv_ln1_offset, L1_conv_ln2_scale, L1_conv_ln2_offset, L1_conv_w1, L1_conv_b1, L1_conv_w2, L1_conv_b2)
    x = _L2_conv_ref(x, L2_conv_g1, L2_conv_beta1, L2_conv_w_qkv, L2_conv_b_qkv, L2_conv_w_proj, L2_conv_b_proj, L2_conv_rel_pos_h, L2_conv_rel_pos_w, L2_conv_g2, L2_conv_beta2, L2_conv_w_fc1, L2_conv_b_fc1, L2_conv_w_fc2, L2_conv_b_fc2)
    x = _L3_conv_ref(x, L3_conv_w1, L3_conv_b1, L3_conv_w2, L3_conv_b2)
    return x

_drawn_inputs = setup_inputs


def setup_inputs(seed=0):
    import zlib

    import numpy as np

    out = dict(_drawn_inputs(seed))
    spreads = {'L0_conv_norm1_g': (1.0, 0.6),
     'L0_conv_norm1_b': (0.0, 0.8),
     'L0_conv_qkv_b': (0.0, 0.279),
     'L0_conv_proj_b': (0.0, 0.1),
     'L0_conv_norm2_g': (1.0, 0.6),
     'L0_conv_norm2_b': (0.0, 0.8),
     'L0_conv_mlp_b1': (0.0, 0.29),
     'L0_conv_mlp_b2': (0.0, 0.1),
     'L1_conv_bq': (0.0, 0.8),
     'L1_conv_bk': (0.0, 0.8),
     'L1_conv_bv': (0.0, 0.1),
     'L1_conv_bo': (0.0, 0.1),
     'L1_conv_ln1_scale': (1.0, 0.6),
     'L1_conv_ln1_offset': (0.0, 0.6),
     'L1_conv_ln2_scale': (1.0, 0.6),
     'L1_conv_ln2_offset': (0.0, 0.8),
     'L1_conv_b1': (0.0, 0.275),
     'L1_conv_b2': (0.0, 0.1),
     'L2_conv_g1': (1.0, 0.6),
     'L2_conv_beta1': (0.0, 0.8),
     'L2_conv_b_qkv': (0.0, 0.304),
     'L2_conv_b_proj': (0.0, 0.1),
     'L2_conv_g2': (1.0, 0.6),
     'L2_conv_beta2': (0.0, 0.8),
     'L2_conv_b_fc1': (0.0, 0.286),
     'L2_conv_b_fc2': (0.0, 0.1)}
    factors = {'L0_conv_qkv_w': 6.179,
     'L0_conv_rel_pos_h': 8.0,
     'L0_conv_rel_pos_w': 8.0,
     'L1_conv_wq': 8.0,
     'L1_conv_wk': 8.0,
     'L1_conv_rel_pos_0': 8.0,
     'L1_conv_rel_pos_1': 8.0,
     'L2_conv_w_qkv': 3.035,
     'L2_conv_rel_pos_h': 8.0,
     'L2_conv_rel_pos_w': 8.0,
     'L3_conv_w1': 7.138,
     'L3_conv_b1': 8.0,
     'L3_conv_w2': 5.942,
     'L3_conv_b2': 3.145}
    for name, (base, spread) in spreads.items():
        noise = np.random.default_rng([zlib.crc32(name.encode()), seed]).standard_normal(out[name].shape)
        drawn = base * np.exp(spread * noise) if base else spread * noise
        out[name] = jnp.asarray(drawn.astype(out[name].dtype))
    for name, factor in factors.items():
        out[name] = (out[name] * factor).astype(out[name].dtype)
    return out
```

```python
from contextlib import ExitStack

import numpy as np
import concourse.bass as bass
from concourse import mybir

F32 = mybir.dt.float32
F32R = mybir.dt.float32r
ALU = mybir.AluOpType
ACT = mybir.ActivationFunctionType
AX = mybir.AxisListType

NB, IMG, C = 4, 16, 192
TOK = IMG * IMG
NT = NB * TOK
TILES = NT // 128
CK = C // 2
HEADS, HALF = 12, 6
FF = 4 * C
FM = FF // 128
BIG = 1e30
EDGE = 14
STRIP_A = NB * IMG * 2
STRIP_B = NB * 2 * EDGE
NE = STRIP_A + STRIP_B
FREQ = IMG // 2 + 1
MODES = IMG * FREQ
MT = MODES // 2
NBLK, BS = 8, C // 8
SHRINK = 0.01


class Layer:

    def __init__(self, index, head_dim, window, eps, gelu):
        self.index, self.hd, self.win, self.eps, self.gelu = index, head_dim, window, eps, gelu
        self.split = head_dim == 16
        self.pads = IMG % window != 0
        self.dim = HEADS * head_dim
        self.per_chunk = CK // head_dim
        self.chunks = HEADS // self.per_chunk
        self.chunks_half = self.chunks // 2
        self.slot = 32 if head_dim == 16 else 64
        self.per_group = 128 // self.slot
        self.groups = HEADS // self.per_group
        self.rel = 2 * window - 1
        self.npad = window * window if self.pads else 0
        self.keys = NT + self.npad
        self.pc = self.npad // 2
        if self.split:
            h, w = head_dim, window
            self.q_rows = [("q_hi", 0, h), ("q_hi", h, h), ("q_lo", 2 * h, h)]
            r = 3 * h
            for part in ("rh_hi", "rw_hi", "rh_lo", "rw_lo"):
                self.q_rows.append((part, r, w))
                r += w
            self.k_rows = [("k_hi", 0, h), ("k_lo", h, h), ("k_hi", 2 * h, h)]
            self.const_row, self.mask_row, self.max_row = 3 * h, r, r + 5
            self.rows = r + 7
        else:
            h, w = head_dim, window
            self.q_rows = [("q", 0, h), ("rh", h, w), ("rw", h + w, w)]
            self.k_rows = [("k", 0, h)]
            self.const_row, self.max_row = h, h + 2 * w
            self.rows = h + 2 * w + 1


LAYERS = [Layer(0, 16, 14, 1e-5, ACT.Gelu), Layer(1, 48, 16, 1e-5, ACT.Gelu_apprx_tanh),
          Layer(2, 16, 14, 1e-6, ACT.Gelu)]


def key_constants(L):
    w, two = L.win, 2 if L.split else 1
    n = TOK + L.npad
    hot_h, hot_w = np.zeros((w, n), np.float32), np.zeros((w, n), np.float32)
    masks = np.zeros((5, n), np.float32)
    for kh in range(IMG):
        for kw in range(IMG):
            j = kh * IMG + kw
            hot_h[w - 1 - kh % w, j] = 1
            hot_w[w - 1 - kw % w, j] = 1
            masks[kh // w, j] = 1
            masks[2 + kw // w, j] = 1
    for p in range(L.npad):
        kh, kw = divmod(p, w)
        j = TOK + p
        hot_h[w - 1 - kh, j] = 1
        hot_w[w - 1 - kw, j] = 1
        real_h, real_w = kh < IMG - w, kw < IMG - w
        if real_h and real_w:
            masks[0, j] = masks[1, j] = 1
        elif real_h:
            masks[3, j] = 1
        elif real_w:
            masks[1, j] = 1
        else:
            masks[4, j] = 1
    parts = [hot_h, hot_w] * two + ([masks] if L.split else []) + [np.ones((two, n), np.float32)]
    return np.ascontiguousarray(np.concatenate(parts))


def query_masks():
    m = np.zeros((5, IMG, IMG), np.float32)
    low = np.arange(IMG) < EDGE
    m[0, ~low, :] = -BIG
    m[1, low, :] = -BIG
    m[2, :, ~low] = -BIG
    m[3, :, low] = -BIG
    m[4, :EDGE, :EDGE] = -BIG
    return m.reshape(5, TOK)


def fourier():
    pos = np.arange(IMG)
    h, w, kh, kw = np.meshgrid(pos, pos, pos, np.arange(FREQ), indexing="ij")
    ang = 2 * np.pi * ((h * kh + w * kw) % IMG) / IMG
    cos, sin = np.cos(ang).reshape(TOK, MODES) / IMG, np.sin(ang).reshape(TOK, MODES) / IMG
    weight = np.tile(np.where((np.arange(FREQ) == 0) | (np.arange(FREQ) == FREQ - 1), 1.0, 2.0), IMG)
    fwd = np.concatenate([cos, -sin], 1)
    inv = np.stack([(cos * weight).T, (-sin * weight).T])
    fwd = fwd.reshape(2, 128, 2 * MODES).transpose(1, 0, 2)
    inv = inv.reshape(2, 2, MT, TOK).transpose(2, 1, 0, 3)
    return np.ascontiguousarray(fwd, np.float32), np.ascontiguousarray(inv, np.float32)


class Count:

    def __init__(self, nc, ctx, name, per_layer, step=1):
        self.sem = ctx.enter_context(nc.semaphore(name))
        self.base = [sum(per_layer[:i]) for i in range(len(per_layer) + 1)]
        self.step = step

    def at(self, layer, i):
        return self.step * (self.base[layer] + i + 1)


def build(nc, io, out):
    ctx = ExitStack()
    with ctx:
        _build(nc, ctx, io, out)


def _build(nc, ctx, io, out):
    def sb(where, name, shape, dt=F32):
        return where.enter_context(nc.sbuf_tensor(name, shape, dt))

    def count(name, per_layer, step=1):
        return Count(nc, ctx, name, per_layer, step)

    X = sb(ctx, "X", [128, TILES, C])
    XN = sb(ctx, "XN", [128, TILES, C])
    XT = sb(ctx, "XT", [CK, 2, NT])
    IDN = sb(ctx, "IDN", [128, 128])
    SEL = {s: sb(ctx, f"SEL{s}", [128, 128]) for s in (32, 64)}
    STAT = sb(ctx, "STAT", [128, TILES, 6])
    MV = sb(ctx, "MV", [128, TILES, 2])
    STD = sb(ctx, "STD", [128, TILES])
    RSTD = sb(ctx, "RSTD", [128, TILES])
    EPS = sb(ctx, "EPS", [128, 2])
    PS = ctx.enter_context(nc.psum_tensor("PS", [128, 8, 512], F32))

    mem = []
    for L in LAYERS:
        n = L.index
        m = {}
        frame = ExitStack()
        m["WQKV"] = sb(frame, f"WQKV{n}", [CK, 2, 3 * L.dim])
        m["WP"] = sb(frame, f"WP{n}", [128, L.groups, C])
        m["W1"] = sb(frame, f"W1_{n}", [CK, 2, FF])
        m["W2"] = sb(frame, f"W2_{n}", [128, FM, C])
        m["COL"] = sb(frame, f"COL{n}", [128, 8 + 2 * L.chunks + FM])
        m["VB"] = sb(frame, f"VB{n}", [128, L.dim])
        m["B2"] = sb(frame, f"B2_{n}", [128, C])
        m["RB"] = sb(frame, f"RB{n}", [CK, 2, L.rel, L.per_chunk])
        attn = ExitStack()
        dt = F32R if L.split else F32
        m["QA"] = sb(attn, f"QA{n}", [L.rows, HALF, NT], dt)
        m["KA"] = sb(attn, f"KA{n}", [L.rows, HALF, L.keys], dt)
        rw = L.per_chunk * L.win
        bufs = 1 if L.split else 2
        m["q"] = [sb(attn, f"QD{n}_{i}", [CK, NT]) for i in range(bufs)]
        m["k"] = [sb(attn, f"KD{n}_{i}", [CK, L.keys]) for i in range(bufs)]
        if L.split:
            for part, p, f in (("q", CK, NT), ("k", CK, L.keys), ("rh", rw, NT), ("rw", rw, NT)):
                for half in ("hi", "lo"):
                    m[f"{part}_{half}"] = [sb(attn, f"{part}{half}{n}", [p, f], F32R)]
            m["KC32"] = sb(attn, f"KC32_{n}", [L.rows - L.const_row, TOK + L.npad])
            m["KC"] = sb(attn, f"KC{n}", [L.rows - L.const_row, TOK + L.npad], F32R)
            m["QM32"] = sb(attn, f"QM32_{n}", [5, TOK])
            m["QM"] = sb(attn, f"QM{n}", [5, TOK], F32R)
            m["BV"] = sb(attn, f"BV{n}", [L.pc, HEADS, L.slot])
            m["PP"] = sb(attn, f"PP{n}", [L.pc, 2, 2, NE])
            m["NRH"] = sb(attn, f"NRH{n}", [TILES, 2, 128], F32R)
            m["NRL"] = sb(attn, f"NRL{n}", [TILES, 2, 128], F32R)
        else:
            for part in ("rh", "rw"):
                m[part] = [sb(attn, f"{part}{n}_{i}", [rw, NT]) for i in range(bufs)]
        m["V"] = sb(attn, f"V{n}", [128, TILES, HEADS, L.slot])
        m["OT"] = sb(attn, f"OT{n}", [128, L.groups, NT])
        m["OS"] = sb(attn, f"OS{n}", [128, 2, 512])
        m["RC"] = sb(attn, f"RC{n}", [128, 512])
        m["PT"] = sb(attn, f"PT{n}", [128, 2, 2, NT])
        m["NM"] = sb(attn, f"NM{n}", [128, 2, TILES])
        m["NR"] = sb(attn, f"NR{n}", [TILES, 2, 128])
        attn.close()
        m["HT"] = sb(frame, f"HT{n}", [128, FM, NT])
        frame.close()
        mem.append(m)
    spectral = ExitStack()
    FW = sb(spectral, "FW", [128, 2, 2 * MODES])
    GI = sb(spectral, "GI", [MT, 2, 2, TOK])
    WS = sb(spectral, "WS", [CK, 2, 2, 2, CK])
    W1N = sb(spectral, "W1N", [CK, 2, CK])
    W2S = sb(spectral, "W2S", [CK, 2, 2, 2, CK])
    SB1 = sb(spectral, "SB1", [CK, 2, 2])
    SB2 = sb(spectral, "SB2", [MT, 2, 2, CK])
    XF = sb(spectral, "XF", [CK, 2, 2, NB * MODES])
    O1 = sb(spectral, "O1", [CK, 2, 2, NB * MODES])
    O2 = sb(spectral, "O2", [MT, 2, NB, 2, 2, CK])
    SH = sb(spectral, "SH", [MT, 2, 2, 2 * C])
    Y = sb(spectral, "Y", [128, TILES, C])
    spectral.close()

    A3 = lambda f: [f(L) for L in LAYERS] + [0]
    const_in = count("const_in", [4, 0, 0, 0], 16)
    x_in = count("x_in", [1, 0, 0, 0], 16)
    loads_of = [10 if L.split else 8 for L in LAYERS] + [5]
    weights_in = count("weights_in", loads_of, 16)
    const_rows = A3(lambda L: HALF * (3 if L.split else 1))
    aug_const = count("aug_const", const_rows, 16)
    consts_cast = count("consts_cast", A3(lambda L: 2 if L.split else 0))
    setup_done = count("setup_done", A3(lambda L: 2 if L.pads else 1)[:3] + [3])
    mean_var = count("mean_var", [2, 2, 2, 0])
    std_done = count("std_done", [2, 2, 2, 0])
    xn_done = count("xn_done", [2 * TILES] * 3 + [0])
    xt_psum = count("xt_psum", [8, 8, 8, 0])
    xt_done = count("xt_done", [8, 8, 8, 0])
    v_psum = count("v_psum", [TILES] * 3 + [0])
    v_done = count("v_done", [TILES] * 3 + [0])
    qk_psum = count("qk_psum", A3(lambda L: 4 * L.chunks))
    q_done = count("q_done", A3(lambda L: 2 * L.chunks))
    k_done = count("k_done", A3(lambda L: 2 * L.chunks))
    rel_psum = count("rel_psum", A3(lambda L: 4 * L.chunks))
    rh_done = count("rh_done", A3(lambda L: 2 * L.chunks))
    rw_done = count("rw_done", A3(lambda L: 2 * L.chunks))
    rh_lo_done = count("rh_lo_done", A3(lambda L: 2 * L.chunks if L.split else 0))
    rw_hi_done = count("rw_hi_done", A3(lambda L: 2 * L.chunks if L.split else 0))
    split_hi = count("split_hi", A3(lambda L: 2 * L.chunks if L.split else 0))
    split_done = count("split_done", A3(lambda L: 2 * L.chunks if L.split else 0))

    def aug_steps(L):
        return L.per_chunk * (len(L.q_rows) + len(L.k_rows))
    aug_in = [count(f"aug_in{p}", [L.chunks // 2 * aug_steps(L) for L in LAYERS] + [0], 16) for p in (0, 1)]

    def aug_at(L, c):
        return aug_in[c % 2].sem, aug_in[c % 2].at(L.index, (c // 2 + 1) * aug_steps(L) - 1)

    max_psum = count("max_psum", A3(lambda L: HEADS * TILES))
    max_done = count("max_done", A3(lambda L: HEADS * TILES))
    maxT_psum = count("maxT_psum", A3(lambda L: HEADS))
    maxT_done = count("maxT_done", A3(lambda L: HEADS))
    max_row_in = [count(f"max_row_in{p}", A3(lambda L: HEADS // 2 * (2 if L.split else 1)), 16) for p in (0, 1)]

    def max_row_at(L, h):
        two = 2 if L.split else 1
        return max_row_in[h % 2].sem, max_row_in[h % 2].at(L.index, (h // 2 + 1) * two - 1)

    score_units = A3(lambda L: HEADS * (5 if L.pads else 4))
    scores_psum = count("scores_psum", score_units)
    probs_done = count("probs_done", score_units)
    pv_done = count("pv_done", A3(lambda L: HEADS))
    o_copied = count("o_copied", A3(lambda L: 2 * L.groups))
    sums_psum = count("sums_psum", A3(lambda L: 2 * L.groups))
    sums_inv = count("sums_inv", A3(lambda L: 2 * L.groups))
    o_done = count("o_done", A3(lambda L: 2 * L.groups))
    proj_psum = count("proj_psum", [TILES] * 3 + [0])
    x_mid = count("x_mid", [TILES] * 3 + [0])
    x_biased = count("x_biased", [1] * 3 + [0])
    up_psum = count("up_psum", [2 * FM] * 3 + [0])
    gelu_done = count("gelu_done", [2 * FM] * 3 + [0])
    down_psum = count("down_psum", [TILES] * 3 + [0])
    x_end = count("x_end", [TILES] * 3 + [0])
    fwd_psum = count("fwd_psum", [0, 0, 0, 8])
    fwd_done = count("fwd_done", [0, 0, 0, 8])
    s1_psum = count("s1_psum", [0, 0, 0, 8])
    s1_done = count("s1_done", [0, 0, 0, 8])
    s2_psum = count("s2_psum", [0, 0, 0, 8])
    s2_biased = count("s2_biased", [0, 0, 0, 8])
    s2_clamped = count("s2_clamped", [0, 0, 0, 8])
    s2_done = count("s2_done", [0, 0, 0, 8])
    inv_psum = count("inv_psum", [0, 0, 0, TILES])
    y_done = count("y_done", [0, 0, 0, TILES])
    y_out = count("y_out", [0, 0, 0, 2], 16)

    dve_step = ctx.enter_context(nc.semaphore("dve_step"))

    MAX_BANK, SCORE_BANK, TR_BANK, O_BANK = (0, 1), (2, 3, 4), 5, (6, 7)

    def chunk_of(L, h):
        return h // L.per_chunk

    def units(L):
        return 5 if L.pads else 4

    def head_order(L, half):
        hs = list(range(half * HALF, half * HALF + HALF))
        yield "max", hs[0]
        yield "maxT", hs[0]
        yield "max", hs[1]
        pending = None
        for j, h in enumerate(hs):
            if j + 1 < HALF:
                yield "maxT", hs[j + 1]
            yield "scores", h
            if pending is not None:
                yield "norm", pending
                pending = None
            if j + 2 < HALF:
                yield "max", hs[j + 2]
            yield "pv", h
            if (h + 1) % L.per_group == 0:
                pending = h // L.per_group
        if pending is not None:
            yield "norm", pending

    def order_of(L):
        return list(head_order(L, 0)) + list(head_order(L, 1))

    def norms_before(L, h):
        steps = order_of(L)
        return sum(step == "norm" for step, _ in steps[:steps.index(("maxT", h))])

    def maxT_before_norm(L, g):
        steps = order_of(L)
        return max(h for step, h in steps[:steps.index(("norm", g))] if step == "maxT")

    block = ctx.enter_context(nc.Block())

    def raw(ap):
        return ap.bitcast(F32) if ap.dtype == F32R else ap

    @block.sync
    def _(sp):
        sp.dma_start(X[:, :, :], io["x"].rearrange("(t p) c -> p t c", p=128)).then_inc(x_in.sem, 16)
        for n, L in enumerate(LAYERS):
            m = mem[n]
            if n:
                sp.wait_ge(x_end.sem, x_end.at(n - 1, TILES - 1))
            loads = [(m["COL"][:, :], io[f"col{n}"]), (m["WQKV"][:, :, :], io[f"wqkv{n}"]),
                     (m["RB"][:, :, :, :], io[f"rb{n}"]),
                     (m["VB"][:, :], io[f"vb{n}"].partition_broadcast(128)),
                     (m["B2"][:, :], io[f"b2_{n}"].partition_broadcast(128)),
                     (m["WP"][:, :, :], io[f"wp{n}"]), (m["W1"][:, :, :], io[f"w1_{n}"]),
                     (m["W2"][:, :, :], io[f"w2_{n}"])]
            if L.split:
                loads += [(m["KC32"][:, :], io[f"kc{n}"]), (m["QM32"][:, :], io["qm"])]
            if n == 0:
                for dst, src in ((IDN[:, :], io["idn"]), (SEL[32][:, :], io["sel32"]),
                                 (SEL[64][:, :], io["sel64"]), (EPS[:, :], io["eps"])):
                    sp.dma_start(dst, src).then_inc(const_in.sem, 16)
            for dst, src in loads:
                sp.dma_start(dst, src).then_inc(weights_in.sem, 16)
            rows = L.rows - L.const_row
            if L.split:
                sp.wait_ge(consts_cast.sem, consts_cast.at(n, 1))

            for h in range(HALF):
                kdst = raw(m["KA"][L.const_row:L.rows, h, :])
                ksrc = raw(m["KC"][:, :]) if L.split else io[f"kc{n}"]
                sp.dma_start(kdst[:, 0:NT].rearrange("r (b t) -> r b t", b=NB),
                             ksrc[:, 0:TOK].unsqueeze(1).broadcast_to([rows, NB, TOK])).then_inc(aug_const.sem, 16)
                if L.split:
                    sp.dma_start(kdst[:, NT:], ksrc[:, TOK:]).then_inc(aug_const.sem, 16)
                    sp.dma_start(raw(m["QA"][L.mask_row:L.mask_row + 5, h, :]).rearrange("r (b t) -> r b t", b=NB),
                                 raw(m["QM"][:, :]).unsqueeze(1).broadcast_to([5, NB, TOK])).then_inc(aug_const.sem, 16)
            for half in range(2):
                for c in range(half * L.chunks_half, (half + 1) * L.chunks_half):
                    buf = c % len(m["q"])
                    if half:
                        sp.wait_ge(pv_done.sem, pv_done.at(n, HALF - 1))
                    if L.split:
                        sp.wait_ge(split_done.sem, split_done.at(n, 2 * c + 1))
                        sp.wait_ge(rh_lo_done.sem, rh_lo_done.at(n, 2 * c + 1))
                    else:
                        sp.wait_ge(q_done.sem, q_done.at(n, 2 * c + 1))
                        sp.wait_ge(k_done.sem, k_done.at(n, 2 * c + 1))
                        sp.wait_ge(rh_done.sem, rh_done.at(n, 2 * c + 1))
                    sp.wait_ge(rw_done.sem, rw_done.at(n, 2 * c + 1))
                    for i in range(L.per_chunk):
                        s = (c * L.per_chunk + i) % HALF
                        for dst, parts in ((m["QA"], L.q_rows), (m["KA"], L.k_rows)):
                            for part, row, k in parts:
                                src = m[part][buf][i::L.per_chunk, :] if part[0] == "r" else \
                                    m[part][buf][i * k:(i + 1) * k, :]
                                sp.dma_start(raw(dst[row:row + k, s, :]), raw(src))\
                                    .then_inc(aug_in[c % 2].sem, 16)
                for h in range(half * HALF, half * HALF + HALF):
                    s, p = h % HALF, h % 2
                    sp.wait_ge(maxT_done.sem, maxT_done.at(n, h))
                    parts = (m["NRH"], m["NRL"]) if L.split else (m["NR"],)
                    for r, part in enumerate(parts):
                        sp.dma_start(raw(m["QA"][L.max_row + r:L.max_row + r + 1, s, :]), raw(part[:, p, :]))\
                            .then_inc(max_row_in[p].sem, 16)
        sp.wait_ge(x_end.sem, x_end.at(2, TILES - 1))
        loads = [(FW[:, :, :], io["fwd"]), (GI[:, :, :, :], io["inv"]), (WS[:, :, :, :, :], io["ws"]),
                 (SB1[:, :, :], io["sb1"]),
                 (SB2[:, :, :, :], io["sb2"].partition_broadcast(MT))]
        for dst, src in loads:
            sp.dma_start(dst, src).then_inc(weights_in.sem, 16)
        for half in range(2):
            t = TILES // 2
            sp.wait_ge(y_done.sem, y_done.at(3, (half + 1) * t - 1))
            sp.dma_start(out[half * t * 128:(half + 1) * t * 128, :].rearrange("(t p) c -> p t c", p=128),
                         Y[:, half * t:(half + 1) * t, :]).then_inc(y_out.sem, 16)
        sp.wait_ge(y_out.sem, y_out.at(3, 1))

    @block.gpsimd
    def _(pool):
        for n, L in enumerate(LAYERS):
            m = mem[n]
            if n:
                pool.wait_ge(x_end.sem, x_end.at(n - 1, TILES - 1))
            nc.gpsimd.memset(m["V"][:, :, :, L.hd + 1:], 0.0)
            nc.gpsimd.memset(m["V"][:, :, :, L.hd:L.hd + 1], 1.0).then_inc(setup_done.sem, 1)
            pool.wait_ge(weights_in.sem, weights_in.at(n, loads_of[n] - 1))
            if L.pads:
                nc.gpsimd.memset(m["BV"][:, :, L.hd + 1:], 0.0)
                nc.gpsimd.memset(m["BV"][:, :, L.hd:L.hd + 1], 1.0)
                nc.gpsimd.tensor_copy(m["BV"][:, :, 0:L.hd],
                                      m["VB"][0:L.pc, :].rearrange("p (h d) -> p h d", h=HEADS))\
                    .then_inc(setup_done.sem, 1)
                nc.gpsimd.tensor_copy(m["KC"][:, :], m["KC32"][:, :]).then_inc(consts_cast.sem, 1)
                nc.gpsimd.tensor_copy(m["QM"][:, :], m["QM32"][:, :]).then_inc(consts_cast.sem, 1)
            if L.split:
                for c in range(L.chunks):
                    if c:
                        pool.wait_ge(*aug_at(L, c - 1))
                    for i, (part, done) in enumerate((("q", q_done), ("k", k_done))):
                        pool.wait_ge(done.sem, done.at(n, 2 * c + 1))
                        hi, lo, src = m[f"{part}_hi"][0], m[f"{part}_lo"][0], m[part][0]
                        nc.gpsimd.tensor_copy(hi[:, :], src[:, :]).then_inc(split_hi.sem, 1)
                        pool.wait_ge(split_hi.sem, split_hi.at(n, 2 * c + i))
                        nc.gpsimd.tensor_tensor(lo[:, :], src[:, :], hi[:, :].bitcast(F32), ALU.subtract)\
                            .then_inc(split_done.sem, 1)
            for t in range(TILES):
                pool.wait_ge(xn_done.sem, xn_done.at(n, TILES + t))
                ins = nc.gpsimd.tensor_tensor(X[:, t, :], X[:, t, :], m["B2"][:, :], ALU.add)
            ins.then_inc(x_biased.sem, 1)
        pool.wait_ge(weights_in.sem, weights_in.at(3, loads_of[3] - 1))
        nc.gpsimd.tensor_scalar(W1N[:, :, :], WS[:, 0, :, 1, :], -1.0, None, ALU.mult).then_inc(setup_done.sem, 1)
        nc.gpsimd.tensor_copy(W2S[:, :, 0, :, :], WS[:, 1, :, :, :])
        nc.gpsimd.tensor_copy(W2S[:, :, 1, 1, :], WS[:, 1, :, 0, :]).then_inc(setup_done.sem, 1)
        nc.gpsimd.tensor_scalar(W2S[:, :, 1, 0, :], WS[:, 1, :, 1, :], -1.0, None, ALU.mult)\
            .then_inc(setup_done.sem, 1)
        for u in range(8):
            pool.wait_ge(s2_biased.sem, s2_biased.at(3, u))
            nc.gpsimd.tensor_scalar(SH[:, 1, u % 2, :], SH[:, 0, u % 2, :], SHRINK, -SHRINK, ALU.min, ALU.max)\
                .then_inc(s2_clamped.sem, 1)

    @block.scalar
    def _(act):
        def norm_inputs(L, s):
            n = L.index
            act.wait_ge(mean_var.sem, mean_var.at(n, s))
            nc.scalar.activation(STD[:, :], MV[:, :, 1], ACT.Sqrt,
                                 bias=EPS[:, (1 if L.eps == 1e-6 else 0):(2 if L.eps == 1e-6 else 1)])\
                .then_inc(std_done.sem, 1)
            g = mem[n]["COL"][0:CK, 4 * s:4 * s + 4]
            for u in range(4):
                k = u % 2
                act.wait_ge(xt_psum.sem, xt_psum.at(n, 4 * s + u))
                nc.scalar.activation(XT[:, k, (u // 2) * 512:(u // 2 + 1) * 512], PS[0:CK, u, :], ACT.Identity,
                                     scale=g[:, k:k + 1], bias=g[:, 2 + k:3 + k]).then_inc(xt_done.sem, 1)

        act.wait_ge(const_in.sem, 4 * 16)
        for n, L in enumerate(LAYERS):
            m = mem[n]
            act.wait_ge(weights_in.sem, weights_in.at(n, loads_of[n] - 1))
            norm_inputs(L, 0)
            rows = L.per_chunk * L.win
            for half in range(2):
                for c in range(half * L.chunks_half, (half + 1) * L.chunks_half):
                    bufs = len(m["q"])
                    if c >= bufs:
                        act.wait_ge(*aug_at(L, c - bufs))
                    for u in range(2):
                        act.wait_ge(qk_psum.sem, qk_psum.at(n, 4 * c + u))
                        nc.scalar.activation(m["q"][c % bufs][:, u * 512:(u + 1) * 512], PS[0:CK, u, :],
                                             ACT.Identity, bias=m["COL"][0:CK, 8 + c:9 + c])\
                            .then_inc(q_done.sem, 1)
                    dst = (m["rh_hi"] if L.split else m["rh"])[c % bufs]
                    for u in range(2):
                        act.wait_ge(rel_psum.sem, rel_psum.at(n, 4 * c + u))
                        nc.scalar.activation(
                            dst[:, :].rearrange("r (b y x) -> r b y x", b=NB, y=IMG)[:, :, 8 * u:8 * u + 8, :],
                            PS[0:rows, 4 + u, :].rearrange("r (y b x) -> r b y x", b=NB, y=8), ACT.Copy)\
                            .then_inc(rh_done.sem, 1)
                ot = 0
                for step, h in head_order(L, half):
                    if step == "scores":
                        if h >= 2:
                            act.wait_ge(pv_done.sem, pv_done.at(n, h - 2))
                        for u in range(4):
                            j = units(L) * h + u
                            act.wait_ge(scores_psum.sem, scores_psum.at(n, j))
                            nc.scalar.activation(m["PT"][:, h % 2, u % 2, (u // 2) * 512:(u // 2 + 1) * 512],
                                                 PS[:, SCORE_BANK[j % 3], :], ACT.Exp).then_inc(probs_done.sem, 1)
                        if L.pads:
                            j = units(L) * h + 4
                            act.wait_ge(scores_psum.sem, scores_psum.at(n, j))
                            nc.scalar.activation(m["PP"][:, h % 2, :, :],
                                                 PS[0:L.pc, SCORE_BANK[j % 3], 0:2 * NE], ACT.Exp)\
                                .then_inc(probs_done.sem, 1)
                    if step == "pv" and (h + 1) % L.per_group == 0:
                        g = h // L.per_group
                        act.wait_ge(pv_done.sem, pv_done.at(n, h))
                        if g:
                            act.wait_ge(o_done.sem, o_done.at(n, 2 * g - 1))
                        for u in range(2):
                            nc.scalar.activation(m["OS"][:, u, :], PS[:, O_BANK[u], :], ACT.Copy)\
                                .then_inc(o_copied.sem, 1)
            norm_inputs(L, 1)
            for j in range(2 * FM):
                act.wait_ge(up_psum.sem, up_psum.at(n, j))
                nc.scalar.activation(m["HT"][:, j // 2, (j % 2) * 512:(j % 2 + 1) * 512], PS[:, j % 4, :], L.gelu,
                                     bias=m["COL"][:, 8 + 2 * L.chunks + j // 2:9 + 2 * L.chunks + j // 2])\
                    .then_inc(gelu_done.sem, 1)
        act.wait_ge(weights_in.sem, weights_in.at(3, loads_of[3] - 1))
        for u in range(0, 8, 2):
            b, cc = divmod(u, 2)
            act.wait_ge(fwd_psum.sem, fwd_psum.at(3, u))
            nc.scalar.activation(XF[:, cc, :, b * MODES:(b + 1) * MODES],
                                 PS[0:CK, u, 0:2 * MODES].rearrange("p (r m) -> p r m", r=2), ACT.Copy)\
                .then_inc(fwd_done.sem, 1)
        for u in range(8):
            cc, r, half = u // 4, u // 2 % 2, u % 2
            act.wait_ge(s1_psum.sem, s1_psum.at(3, u))
            nc.scalar.activation(O1[:, cc, r, half * 2 * MODES:(half + 1) * 2 * MODES], PS[0:CK, u, 0:2 * MODES],
                                 ACT.Relu, bias=SB1[:, cc, r:r + 1]).then_inc(s1_done.sem, 1)

    @block.vector
    def _(dve):
        steps = [0]

        def link(ins):
            steps[0] += 1
            ins.then_inc(dve_step, 1)
            dve.wait_ge(dve_step, steps[0])

        def norm_stats(L, s):
            n = L.index
            if s == 1:
                for t in range(TILES):
                    dve.wait_ge(proj_psum.sem, proj_psum.at(n, t))
                    link(nc.vector.tensor_tensor(X[:, t, :], X[:, t, :], PS[:, t % 4, 0:C], ALU.add))
                    nc.vector.bn_stats(STAT[:, t, :], X[:, t, :]).then_inc(x_mid.sem, 1)
                dve.wait_ge(x_mid.sem, x_mid.at(n, TILES - 1))
            else:
                for t in range(TILES):
                    if n:
                        dve.wait_ge(x_end.sem, x_end.at(n - 1, t))
                    ins = nc.vector.bn_stats(STAT[:, t, :], X[:, t, :])
                link(ins)
            for t in range(TILES):
                ins = nc.vector.bn_aggr(MV[:, t, :], STAT[:, t, :])
            ins.then_inc(mean_var.sem, 1)
            dve.wait_ge(std_done.sem, std_done.at(n, s))
            link(nc.vector.reciprocal(RSTD[:, :], STD[:, :]))
            if 2 * n + s:
                dve.wait_ge(xt_psum.sem, xt_psum.at(n, 4 * s - 1))
            for t in range(TILES):
                nc.vector.tensor_scalar(XN[:, t, :], X[:, t, :], MV[:, t, 0:1], RSTD[:, t:t + 1],
                                        ALU.subtract, ALU.mult).then_inc(xn_done.sem, 1)

        dve.wait_ge(x_in.sem, 16)
        for n, L in enumerate(LAYERS):
            m = mem[n]
            norm_stats(L, 0)
            dve.wait_ge(weights_in.sem, weights_in.at(n, loads_of[n] - 1))
            dve.wait_ge(setup_done.sem, setup_done.at(n, 0))
            for t in range(TILES):
                dve.wait_ge(v_psum.sem, v_psum.at(n, t))
                bank, nh = 4 + 2 * (t % 2), HEADS if L.hd == 16 else HALF
                for g in range(HEADS // nh):
                    ins = nc.vector.tensor_tensor(
                        m["V"][:, t, g * nh:(g + 1) * nh, 0:L.hd],
                        PS[:, bank + g, 0:nh * L.hd].rearrange("p (h d) -> p h d", h=nh),
                        m["VB"][:, g * nh * L.hd:(g + 1) * nh * L.hd].rearrange("p (h d) -> p h d", h=nh), ALU.add)
                ins.then_inc(v_done.sem, 1)
            rows = L.per_chunk * L.win
            for half in range(2):
                for c in range(half * L.chunks_half, (half + 1) * L.chunks_half):
                    bufs = len(m["q"])
                    if c >= bufs:
                        dve.wait_ge(*aug_at(L, c - bufs))
                    kd = m["k"][c % bufs]
                    bk = m["COL"][0:CK, 8 + L.chunks + c:9 + L.chunks + c]
                    if L.pads:
                        nc.vector.tensor_scalar(kd[:, NT:], bk.broadcast_to([CK, L.npad]), L.hd ** -0.5, None,
                                                ALU.mult)
                    for u in range(2):
                        dve.wait_ge(qk_psum.sem, qk_psum.at(n, 4 * c + 2 + u))
                        nc.vector.tensor_scalar(kd[:, u * 512:(u + 1) * 512], PS[0:CK, 2 + u, :], bk,
                                                L.hd ** -0.5, ALU.add, ALU.mult).then_inc(k_done.sem, 1)
                    if L.split:
                        for u in range(2):
                            dve.wait_ge(rh_done.sem, rh_done.at(n, 2 * c + u))
                            view = "r (b y x) -> r b y x"
                            y = slice(8 * u, 8 * u + 8)
                            nc.vector.tensor_tensor(
                                m["rh_lo"][0][:, :].rearrange(view, b=NB, y=IMG)[:, :, y, :],
                                PS[0:rows, 4 + u, :].rearrange("r (y b x) -> r b y x", b=NB, y=8),
                                m["rh_hi"][0][:, :].bitcast(F32).rearrange(view, b=NB, y=IMG)[:, :, y, :],
                                ALU.subtract).then_inc(rh_lo_done.sem, 1)
                    for u in range(2):
                        dve.wait_ge(rel_psum.sem, rel_psum.at(n, 4 * c + 2 + u))
                        x = slice(8 * u, 8 * u + 8)
                        view = "r (b y x) -> r b y x"
                        src = PS[0:rows, u, :].rearrange("r (x b y) -> r b y x", b=NB, x=8)
                        if L.split:
                            hi = m["rw_hi"][0][:, :].rearrange(view, b=NB, y=IMG)[:, :, :, x]
                            hi32 = m["rw_hi"][0][:, :].bitcast(F32).rearrange(view, b=NB, y=IMG)[:, :, :, x]
                            lo = m["rw_lo"][0][:, :].rearrange(view, b=NB, y=IMG)[:, :, :, x]
                            nc.vector.tensor_copy(hi, src).then_inc(rw_hi_done.sem, 1)
                            dve.wait_ge(rw_hi_done.sem, rw_hi_done.at(n, 2 * c + u))
                            nc.vector.tensor_tensor(lo, src, hi32, ALU.subtract).then_inc(rw_done.sem, 1)
                        else:
                            dst = m["rw"][c % bufs][:, :].rearrange(view, b=NB, y=IMG)[:, :, :, x]
                            nc.vector.tensor_copy(dst, src).then_inc(rw_done.sem, 1)
                for step, h in head_order(L, half):
                    if step == "max":
                        if h >= 2:
                            dve.wait_ge(maxT_psum.sem, maxT_psum.at(n, h - 2))
                        for i in range(TILES):
                            j = TILES * h + i
                            dve.wait_ge(max_psum.sem, max_psum.at(n, j))
                            wide = TOK + L.npad
                            nc.vector.tensor_reduce(m["NM"][:, h % 2, i:i + 1], PS[:, MAX_BANK[j % 2], 0:wide],
                                                    AX.X, ALU.max, negate=True).then_inc(max_done.sem, 1)
                    if step == "maxT":
                        dve.wait_ge(maxT_psum.sem, maxT_psum.at(n, h))
                        if h >= 2:
                            dve.wait_ge(*max_row_at(L, h - 2))
                        src = PS[0:TILES, TR_BANK, 0:128]
                        if L.split:
                            hi, lo = m["NRH"][:, h % 2, :], m["NRL"][:, h % 2, :]
                            link(nc.vector.tensor_copy(hi, src))
                            nc.vector.tensor_tensor(lo, src, m["NRH"][:, h % 2, :].bitcast(F32), ALU.subtract)\
                                .then_inc(maxT_done.sem, 1)
                        else:
                            nc.vector.tensor_copy(m["NR"][:, h % 2, :], src).then_inc(maxT_done.sem, 1)
                    if step == "norm":
                        g = h
                        for u in range(2):
                            dve.wait_ge(sums_psum.sem, sums_psum.at(n, 2 * g + u))
                            if 2 * g + u:
                                dve.wait_ge(o_done.sem, o_done.at(n, 2 * g + u - 1))
                            nc.vector.reciprocal(m["RC"][:, :], PS[:, TR_BANK, :]).then_inc(sums_inv.sem, 1)
                            dve.wait_ge(sums_inv.sem, sums_inv.at(n, 2 * g + u))
                            nc.vector.tensor_tensor(m["OT"][:, g, u * 512:(u + 1) * 512], m["OS"][:, u, :],
                                                    m["RC"][:, :], ALU.mult).then_inc(o_done.sem, 1)
            norm_stats(L, 1)
            dve.wait_ge(x_biased.sem, x_biased.at(n, 0))
            for t in range(TILES):
                dve.wait_ge(down_psum.sem, down_psum.at(n, t))
                nc.vector.tensor_tensor(X[:, t, :], X[:, t, :], PS[:, 4 + t % 4, 0:C], ALU.add)\
                    .then_inc(x_end.sem, 1)
        dve.wait_ge(weights_in.sem, weights_in.at(3, loads_of[3] - 1))
        for u in range(1, 8, 2):
            b, cc = divmod(u, 2)
            dve.wait_ge(fwd_psum.sem, fwd_psum.at(3, u))
            nc.vector.tensor_copy(XF[:, cc, :, b * MODES:(b + 1) * MODES],
                                  PS[0:CK, u, 0:2 * MODES].rearrange("p (r m) -> p r m", r=2))\
                .then_inc(fwd_done.sem, 1)
        for u in range(8):
            b, mt = divmod(u, 2)
            dve.wait_ge(s2_psum.sem, s2_psum.at(3, u))
            if u >= 2:
                dve.wait_ge(s2_done.sem, s2_done.at(3, u - 2))
                dve.wait_ge(s2_clamped.sem, s2_clamped.at(3, u - 2))
            nc.vector.tensor_tensor(SH[:, 0, u % 2, :], PS[0:MT, u, 0:2 * C],
                                    SB2[:, :, :, :].rearrange("p a b c -> p (a b c)"), ALU.add)\
                .then_inc(s2_biased.sem, 1)
            if u:
                shrink(nc, dve, s2_clamped, s2_done, O2, SH, u - 1)
        shrink(nc, dve, s2_clamped, s2_done, O2, SH, 7)
        for t in range(TILES):
            dve.wait_ge(inv_psum.sem, inv_psum.at(3, t))
            nc.vector.tensor_tensor(Y[:, t, :], X[:, t, :], PS[:, t, 0:C], ALU.add).then_inc(y_done.sem, 1)

    @block.tensor
    def _(pe):
        def mm(dst, lhsT, rhs, start, stop, loose=False):
            return nc.tensor.matmul(dst, lhsT, rhs, start=start, stop=stop, skip_group_check=loose)

        def transposes(L, s):
            n = L.index
            for u in range(4):
                k = u % 2
                for i in range(4):
                    t = 4 * (u // 2) + i
                    pe.wait_ge(xn_done.sem, xn_done.at(n, TILES * s + t))
                    last = nc.tensor.transpose(PS[0:CK, u, i * 128:(i + 1) * 128],
                                               XN[:, t, k * CK:(k + 1) * CK], IDN[:, :])
                last.then_inc(xt_psum.sem, 1)

        pe.wait_ge(const_in.sem, 4 * 16)
        for n, L in enumerate(LAYERS):
            m = mem[n]
            D = L.dim
            transposes(L, 0)
            pe.wait_ge(weights_in.sem, weights_in.at(n, loads_of[n] - 1))
            for t in range(TILES):
                pe.wait_ge(xt_done.sem, xt_done.at(n, 2 * (t // 4) + 1))
                if t >= 2:
                    pe.wait_ge(v_done.sem, v_done.at(n, t - 2))
                elif n:
                    pe.wait_ge(x_end.sem, x_end.at(n - 1, TILES - 1))
                wide = min(D, 288)
                for g in range(D // wide):
                    for k in range(2):
                        last = mm(PS[:, 4 + 2 * (t % 2) + g, 0:wide], XT[:, k, t * 128:(t + 1) * 128],
                                  m["WQKV"][:, k, 2 * D + g * wide:2 * D + (g + 1) * wide], k == 0, k == 1)
                last.then_inc(v_psum.sem, 1)
            for half in range(2):
                for c in range(half * L.chunks_half, (half + 1) * L.chunks_half):
                    bufs = len(m["q"])
                    if c:
                        pe.wait_ge(rw_done.sem, rw_done.at(n, 2 * c - 1))
                        pe.wait_ge(k_done.sem, k_done.at(n, 2 * c - 1))
                    if half and c == L.chunks_half:
                        pe.wait_ge(max_done.sem, max_done.at(n, TILES * HALF - 1))
                        pe.wait_ge(probs_done.sem, probs_done.at(n, units(L) * HALF - 1))
                    for part in range(2):
                        for u in range(2):
                            for k in range(2):
                                last = mm(PS[0:CK, 2 * part + u, :],
                                          m["WQKV"][:, k, part * D + c * CK:part * D + (c + 1) * CK],
                                          XT[:, k, u * 512:(u + 1) * 512], k == 0, k == 1)
                            last.then_inc(qk_psum.sem, 1)
                    pe.wait_ge(q_done.sem, q_done.at(n, 2 * c + 1))
                    pe.wait_ge(v_done.sem, v_done.at(n, TILES - 1))
                    if c:
                        pe.wait_ge(rh_done.sem, rh_done.at(n, 2 * c - 1))
                        if L.split:
                            pe.wait_ge(rh_lo_done.sem, rh_lo_done.at(n, 2 * c - 1))
                    if half and c == L.chunks_half:
                        g = HALF // L.per_group
                        pe.wait_ge(sums_inv.sem, sums_inv.at(n, 2 * g - 1))
                        pe.wait_ge(maxT_done.sem, maxT_done.at(n, HALF - 1))
                    rows = L.per_chunk * L.win
                    qd = m["q"][c % bufs][:, :].rearrange("r (b y x) -> r b y x", b=NB, y=IMG)
                    for axis in range(2):
                        for i in range(IMG):
                            bank = (4 if axis == 0 else 0) + i // 8
                            rhs = qd[:, :, i, :] if axis == 0 else qd[:, :, :, i]
                            last = mm(PS[0:rows, bank, (i % 8) * 64:(i % 8 + 1) * 64],
                                      m["RB"][:, axis, i % L.win:i % L.win + L.win, :], rhs, True, True)
                            if i % 8 == 7:
                                last.then_inc(rel_psum.sem, 1)
                for step, h in head_order(L, half):
                    s, c = h % HALF, chunk_of(L, h)
                    if step == "max":
                        pe.wait_ge(*aug_at(L, c))
                        pe.wait_ge(aug_const.sem, aug_const.at(n, const_rows[n] - 1))
                        if h % HALF == 0:
                            pe.wait_ge(rw_done.sem, rw_done.at(n, 2 * (half + 1) * L.chunks_half - 1))
                            pe.wait_ge(k_done.sem, k_done.at(n, 2 * (half + 1) * L.chunks_half - 1))
                            pe.wait_ge(rh_done.sem, rh_done.at(n, 2 * (half + 1) * L.chunks_half - 1))
                            if L.split:
                                pe.wait_ge(rh_lo_done.sem,
                                           rh_lo_done.at(n, 2 * (half + 1) * L.chunks_half - 1))
                        for i in range(TILES):
                            j = TILES * h + i
                            if j >= 2:
                                pe.wait_ge(max_done.sem, max_done.at(n, j - 2))
                            bank, b = MAX_BANK[j % 2], i // 2
                            q = m["QA"][0:L.max_row, s, i * 128:(i + 1) * 128]
                            last = mm(PS[:, bank, 0:TOK], q, m["KA"][0:L.max_row, s, b * TOK:(b + 1) * TOK],
                                      True, True)
                            if L.pads:
                                last = mm(PS[:, bank, TOK:TOK + L.npad], q, m["KA"][0:L.max_row, s, NT:], True, True)
                            last.then_inc(max_psum.sem, 1)
                    elif step == "maxT":
                        pe.wait_ge(max_done.sem, max_done.at(n, TILES * h + TILES - 1))
                        if h:
                            pe.wait_ge(maxT_done.sem, maxT_done.at(n, h - 1))
                        done_groups = norms_before(L, h)
                        if done_groups:
                            pe.wait_ge(sums_inv.sem, sums_inv.at(n, 2 * done_groups - 1))
                        nc.tensor.transpose(PS[0:TILES, TR_BANK, 0:128], m["NM"][:, h % 2, :], IDN[:, :])\
                            .then_inc(maxT_psum.sem, 1)
                    elif step == "scores":
                        pe.wait_ge(*max_row_at(L, h))
                        for u in range(4):
                            j = units(L) * h + u
                            if j >= 3:
                                pe.wait_ge(probs_done.sem, probs_done.at(n, j - 3))
                            for b in (2 * (u // 2), 2 * (u // 2) + 1):
                                k0 = b * TOK + (u % 2) * 128
                                last = mm(PS[:, SCORE_BANK[j % 3], (b % 2) * TOK:(b % 2 + 1) * TOK],
                                          m["KA"][:, s, k0:k0 + 128], m["QA"][:, s, b * TOK:(b + 1) * TOK],
                                          True, True)
                            last.then_inc(scores_psum.sem, 1)
                        if L.pads:
                            j = units(L) * h + 4
                            pe.wait_ge(probs_done.sem, probs_done.at(n, j - 3))
                            q = m["QA"][:, s, :].rearrange("r (b y x) -> r b y x", b=NB, y=IMG)
                            for pc in range(2):
                                k = m["KA"][:, s, NT + pc * L.pc:NT + (pc + 1) * L.pc]
                                dst = PS[0:L.pc, SCORE_BANK[j % 3], pc * NE:(pc + 1) * NE]
                                mm(dst[:, 0:STRIP_A], k, q[:, :, :, EDGE:], True, True)
                                last = mm(dst[:, STRIP_A:], k, q[:, :, EDGE:, 0:EDGE], True, True)
                            last.then_inc(scores_psum.sem, 1)
                    elif step == "pv":
                        r0 = (h % L.per_group) * L.slot
                        g = h // L.per_group
                        if h % L.per_group == 0 and g:
                            pe.wait_ge(o_copied.sem, o_copied.at(n, 2 * g - 1))
                        pe.wait_ge(probs_done.sem, probs_done.at(n, units(L) * (h + 1) - 1))
                        for u in range(2):
                            o = PS[r0:r0 + L.slot, O_BANK[u], :]
                            for b in (2 * u, 2 * u + 1):
                                for kc in range(2):
                                    last = mm(o[:, (b % 2) * TOK:(b % 2 + 1) * TOK], m["V"][:, 2 * b + kc, h, :],
                                              m["PT"][:, h % 2, kc, b * TOK:(b + 1) * TOK],
                                              b % 2 == 0 and kc == 0, kc == 1, True)
                            if L.pads:
                                oe = o.rearrange("r (b y x) -> r b y x", b=2, y=IMG)
                                for pc in range(2):
                                    p = m["PP"][:, h % 2, pc, :]
                                    na, nb = STRIP_A // 2, STRIP_B // 2
                                    for b in range(2):
                                        pa = p[:, u * na + b * na // 2:u * na + (b + 1) * na // 2]
                                        pb = p[:, STRIP_A + u * nb + b * nb // 2:STRIP_A + u * nb + (b + 1) * nb // 2]
                                        mm(oe[:, b, :, EDGE:], m["BV"][:, h, :],
                                           pa.rearrange("p (y x) -> p y x", y=IMG), False, False, True)
                                        last = mm(oe[:, b, EDGE:, 0:EDGE], m["BV"][:, h, :],
                                                  pb.rearrange("p (y x) -> p y x", y=2), False, True, True)
                        last.then_inc(pv_done.sem, 1)
                    elif step == "norm":
                        g = h
                        for u in range(2):
                            pe.wait_ge(o_copied.sem, o_copied.at(n, 2 * g + u))
                            if 2 * g + u:
                                pe.wait_ge(sums_inv.sem, sums_inv.at(n, 2 * g + u - 1))
                            pe.wait_ge(maxT_done.sem, maxT_done.at(n, maxT_before_norm(L, g)))
                            mm(PS[:, TR_BANK, :], SEL[L.slot][:, :], m["OS"][:, u, :], True, True)\
                                .then_inc(sums_psum.sem, 1)
            for t in range(TILES):
                pe.wait_ge(o_done.sem, o_done.at(n, 2 * L.groups - (1 if t >= TILES // 2 else 2)))
                if t == 0:
                    pe.wait_ge(probs_done.sem, probs_done.at(n, units(L) * HEADS - 1))
                    pe.wait_ge(max_done.sem, max_done.at(n, TILES * HEADS - 1))
                if t >= 4:
                    pe.wait_ge(x_mid.sem, x_mid.at(n, t - 4))
                for g in range(L.groups):
                    last = mm(PS[:, t % 4, 0:C], m["OT"][:, g, t * 128:(t + 1) * 128], m["WP"][:, g, :],
                              g == 0, g == L.groups - 1)
                last.then_inc(proj_psum.sem, 1)
            pe.wait_ge(x_mid.sem, x_mid.at(n, TILES - 1))
            transposes(L, 1)
            for j in range(2 * FM):
                pe.wait_ge(xt_done.sem, xt_done.at(n, 7))
                if j >= 4:
                    pe.wait_ge(gelu_done.sem, gelu_done.at(n, j - 4))
                for k in range(2):
                    last = mm(PS[:, j % 4, :], m["W1"][:, k, (j // 2) * 128:(j // 2 + 1) * 128],
                              XT[:, k, (j % 2) * 512:(j % 2 + 1) * 512], k == 0, k == 1)
                last.then_inc(up_psum.sem, 1)
            for t in range(TILES):
                pe.wait_ge(gelu_done.sem, gelu_done.at(n, 2 * FM - (1 if t >= TILES // 2 else 2)))
                if t >= 4:
                    pe.wait_ge(x_end.sem, x_end.at(n, t - 4))
                for g in range(FM):
                    last = mm(PS[:, 4 + t % 4, 0:C], m["HT"][:, g, t * 128:(t + 1) * 128], m["W2"][:, g, :],
                              g == 0, g == FM - 1)
                last.then_inc(down_psum.sem, 1)
        pe.wait_ge(weights_in.sem, weights_in.at(3, loads_of[3] - 1))
        pe.wait_ge(x_end.sem, x_end.at(2, TILES - 1))
        for u in range(8):
            b, cc = divmod(u, 2)
            for kt in range(2):
                last = mm(PS[0:CK, u, 0:2 * MODES], X[:, 2 * b + kt, cc * CK:(cc + 1) * CK], FW[:, kt, :],
                          kt == 0, kt == 1)
            last.then_inc(fwd_psum.sem, 1)
        pe.wait_ge(fwd_done.sem, fwd_done.at(3, 7))
        pe.wait_ge(setup_done.sem, setup_done.at(3, 2))
        for u in range(8):
            cc, r, half = u // 4, u // 2 % 2, u % 2
            cols = slice(half * 2 * MODES, (half + 1) * 2 * MODES)
            own, other = (WS[:, 0, cc, 0, :], W1N[:, cc, :] if r == 0 else WS[:, 0, cc, 1, :])
            mm(PS[0:CK, u, 0:2 * MODES], own, XF[:, cc, r, cols], True, False)
            mm(PS[0:CK, u, 0:2 * MODES], other, XF[:, cc, 1 - r, cols], False, True).then_inc(s1_psum.sem, 1)
        pe.wait_ge(s1_done.sem, s1_done.at(3, 7))
        for u in range(8):
            b, mt = divmod(u, 2)
            for cc in range(2):
                for r in range(2):
                    m0 = b * MODES + mt * MT
                    last = mm(PS[0:MT, u, cc * C:(cc + 1) * C], O1[:, cc, r, m0:m0 + MT],
                              W2S[:, cc, r, :, :], r == 0, r == 1)
            last.then_inc(s2_psum.sem, 1)
        for t in range(TILES):
            b, half = divmod(t, 2)
            pe.wait_ge(s2_done.sem, s2_done.at(3, 2 * b + 1))
            pe.wait_ge(s2_biased.sem, s2_biased.at(3, 7))
            for i in range(4):
                mt, r = divmod(i, 2)
                last = mm(PS[:, t, 0:C], GI[:, mt, r, half * 128:(half + 1) * 128],
                          O2[:, mt, b, r, :, :], i == 0, i == 3)
            last.then_inc(inv_psum.sem, 1)


def shrink(nc, dve, clamped, done, O2, SH, u):
    b, mt = divmod(u, 2)
    dve.wait_ge(clamped.sem, clamped.at(3, u))
    view = "p (c r k) -> p r c k"
    nc.vector.tensor_tensor(O2[:, mt, b, :, :, :], SH[:, 0, u % 2, :].rearrange(view, c=2, r=2),
                            SH[:, 1, u % 2, :].rearrange(view, c=2, r=2), ALU.subtract).then_inc(done.sem, 1)


def _pack(inputs):
    def f(name):
        return np.asarray(inputs[name])

    def cols(v, parts):
        return v.reshape(-1, parts).T

    def rows(w, parts):
        return w.reshape(-1, parts, w.shape[-1]).transpose(1, 0, 2)

    names = [("L0_conv_", "norm1_g norm1_b norm2_g norm2_b rel_pos_h rel_pos_w proj_w proj_b mlp_w1 mlp_b1 mlp_w2 mlp_b2"),
             ("L1_conv_", "ln1_scale ln1_offset ln2_scale ln2_offset rel_pos_0 rel_pos_1 wo bo w1 b1 w2 b2"),
             ("L2_conv_", "g1 beta1 g2 beta2 rel_pos_h rel_pos_w w_proj b_proj w_fc1 b_fc1 w_fc2 b_fc2")]
    arrays = {"x": f("x").reshape(NT, C)}
    for L, (prefix, keys) in zip(LAYERS, names):
        n = L.index
        g1, o1, g2, o2, rh, rw, wp, bp, w1, b1, w2, b2 = (f(prefix + k) for k in keys.split())
        if n == 1:
            wqkv = np.concatenate([f(prefix + k) for k in ("wq", "wk", "wv")], 1)
            bqkv = np.concatenate([f(prefix + k) for k in ("bq", "bk", "bv")])
        else:
            wqkv, bqkv = (f(prefix + k) for k in (("qkv_w", "qkv_b") if n == 0 else ("w_qkv", "b_qkv")))
        col = np.zeros((128, 8 + 2 * L.chunks + FM), np.float32)
        at = 0
        for v, parts in ((g1, CK), (o1, CK), (g2, CK), (o2, CK), (bqkv[:2 * L.dim], CK), (b1, 128)):
            c = cols(v, parts)
            col[:parts, at:at + c.shape[1]] = c
            at += c.shape[1]
        place = np.zeros((L.per_group, L.slot, L.groups, C), np.float32)
        place[:, :L.hd] = wp.reshape(L.groups, L.per_group, L.hd, C).transpose(1, 2, 0, 3)
        place[0, L.hd, 0] = bp
        rb = np.zeros((L.per_chunk, L.hd, 2, L.rel, L.per_chunk), np.float32)
        for i in range(L.per_chunk):
            rb[i, :, 0, :, i] = rh.T
            rb[i, :, 1, :, i] = rw.T
        arrays |= {f"col{n}": col, f"wqkv{n}": rows(wqkv, CK), f"wp{n}": place.reshape(128, L.groups, C),
                   f"rb{n}": rb.reshape(CK, 2, L.rel, L.per_chunk), f"w1_{n}": rows(w1, CK),
                   f"w2_{n}": rows(w2, 128), f"vb{n}": bqkv[2 * L.dim:], f"b2_{n}": b2,
                   f"kc{n}": key_constants(L)}
    arrays["qm"] = query_masks()
    arrays["idn"] = np.eye(128, dtype=np.float32)
    for slot, row in ((32, 16), (64, 48)):
        sel = np.zeros((128, 128), np.float32)
        for p in range(128):
            sel[p // slot * slot + row, p] = 1
        arrays[f"sel{slot}"] = sel
    arrays["eps"] = np.tile(np.array([1e-5, 1e-6], np.float32), (128, 1))
    arrays["fwd"], arrays["inv"] = fourier()
    per = CK // BS
    ws = np.zeros((per, BS, 2, 2, 2, per, BS), np.float32)
    for layer, name in enumerate(("w1", "w2")):
        w = f("L3_conv_" + name).reshape(2, 2, per, BS, BS)
        for i in range(per):
            ws[i, :, layer, :, :, i] = w[:, :, i].transpose(2, 1, 0, 3)
    arrays["ws"] = ws.reshape(CK, 2, 2, 2, CK)
    arrays["sb1"] = f("L3_conv_b1").reshape(2, 2, CK).transpose(2, 1, 0)
    arrays["sb2"] = f("L3_conv_b2").reshape(2, 2, CK).transpose(1, 0, 2)
    return {k: np.ascontiguousarray(v) for k, v in arrays.items()}


def kernel(**inputs):
    import concourse.bacc as _bacc
    from concourse.bass_utils import run_bass_kernel_spmd as _run

    nc = _bacc.Bacc("TRN2", target_bir_lowering=False, num_devices=1)
    arrays = _pack(inputs)
    io = {k: nc.dram_tensor(f"in_{k}", v.shape, F32, kind="ExternalInput").ap() for k, v in arrays.items()}
    out = nc.dram_tensor("out_y", (NT, C), F32, kind="ExternalOutput").ap()
    build(nc, io, out)
    r = _run(nc, [{f"in_{k}": v for k, v in arrays.items()}], core_ids=[0])
    return r.results[0]["out_y"].reshape(NB, IMG, IMG, C)
```

```python
from contextlib import ExitStack

import numpy as np
import concourse.bass as bass
from concourse import mybir

F32 = mybir.dt.float32
F32R = mybir.dt.float32r
ALU = mybir.AluOpType
ACT = mybir.ActivationFunctionType
AX = mybir.AxisListType

NB, IMG, C = 4, 16, 192
TOK = IMG * IMG
NT = NB * TOK
TILES = NT // 128
CK = C // 2
HEADS, HALF = 12, 6
FF = 4 * C
FM = FF // 128
BIG = 1e30
EDGE = 14
STRIP_A = NB * IMG * 2
STRIP_B = NB * 2 * EDGE
NE = STRIP_A + STRIP_B
FREQ = IMG // 2 + 1
MODES = IMG * FREQ
MT = MODES // 2
NBLK, BS = 8, C // 8
SHRINK = 0.01


class Layer:

    def __init__(self, index, head_dim, window, eps, gelu):
        self.index, self.hd, self.win, self.eps, self.gelu = index, head_dim, window, eps, gelu
        self.split = head_dim == 16
        self.pads = IMG % window != 0
        self.dim = HEADS * head_dim
        self.scale = head_dim ** -0.5
        self.per_chunk = CK // head_dim
        self.chunks = HEADS // self.per_chunk
        self.bufs = 1 if self.split else 2
        self.slot = 32 if head_dim == 16 else 64
        self.vcol = 32 if head_dim == 16 else 52
        self.per_group = 128 // self.slot
        self.groups = HEADS // self.per_group
        self.rel = 2 * window - 1
        self.npad = window * window if self.pads else 0
        self.pad_cols = TOK if self.pads else 0
        self.keys = NT + self.pad_cols
        self.pc = self.npad // 2
        parts = 2 if self.split else 1
        self.rel_row = 3 * head_dim if self.split else head_dim
        self.mask_row = self.rel_row + 2 * parts * window
        self.max_row = self.mask_row + (5 if self.pads else 0)
        self.rows = self.max_row + parts
        self.aug_dmas = 5 if self.split else 3
        self.units = 5 if self.pads else 4
        self.per_pair = 4 if self.split else 8


LAYERS = [Layer(0, 16, 14, 1e-5, ACT.Gelu), Layer(1, 48, 16, 1e-5, ACT.Gelu_apprx_tanh),
          Layer(2, 16, 14, 1e-6, ACT.Gelu)]


def key_constants(L):
    w, parts = L.win, 2 if L.split else 1
    n = TOK + L.pad_cols
    hot = np.zeros((w, parts, 2, n), np.float32)
    masks = np.zeros((5 if L.pads else 0, n), np.float32)
    ones = np.ones((parts, n), np.float32)
    for kh in range(IMG):
        for kw in range(IMG):
            j = kh * IMG + kw
            hot[w - 1 - kh % w, :, 0, j] = 1
            hot[w - 1 - kw % w, :, 1, j] = 1
            if L.pads:
                masks[kh // w, j] = 1
                masks[2 + kw // w, j] = 1
    for p in range(L.npad):
        kh, kw = divmod(p, w)
        j = TOK + p
        hot[w - 1 - kh, :, 0, j] = 1
        hot[w - 1 - kw, :, 1, j] = 1
        real_h, real_w = kh < IMG - w, kw < IMG - w
        if real_h and real_w:
            masks[0, j] = masks[1, j] = 1
        elif real_h:
            masks[3, j] = 1
        elif real_w:
            masks[1, j] = 1
        else:
            masks[4, j] = 1
    return np.ascontiguousarray(np.concatenate([hot.reshape(-1, n), masks, ones]))


def query_masks():
    m = np.zeros((5, IMG, IMG), np.float32)
    low = np.arange(IMG) < EDGE
    m[0, ~low, :] = -BIG
    m[1, low, :] = -BIG
    m[2, :, ~low] = -BIG
    m[3, :, low] = -BIG
    m[4, :EDGE, :EDGE] = -BIG
    return m.reshape(5, TOK)


def fourier():
    pos = np.arange(IMG)
    h, w, kh, kw = np.meshgrid(pos, pos, pos, np.arange(FREQ), indexing="ij")
    ang = 2 * np.pi * ((h * kh + w * kw) % IMG) / IMG
    cos, sin = np.cos(ang).reshape(TOK, MODES) / IMG, np.sin(ang).reshape(TOK, MODES) / IMG
    weight = np.tile(np.where((np.arange(FREQ) == 0) | (np.arange(FREQ) == FREQ - 1), 1.0, 2.0), IMG)
    fwd = np.concatenate([cos, -sin], 1)
    inv = np.stack([(cos * weight).T, (-sin * weight).T])
    fwd = fwd.reshape(2, 128, 2 * MODES).transpose(1, 0, 2)
    inv = inv.reshape(2, 2, MT, TOK).transpose(2, 1, 0, 3)
    return np.ascontiguousarray(fwd, np.float32), np.ascontiguousarray(inv, np.float32)


class Count:

    def __init__(self, nc, ctx, name, per_layer, step=1):
        self.sem = ctx.enter_context(nc.semaphore(name))
        self.base = [sum(per_layer[:i]) for i in range(len(per_layer) + 1)]
        self.step = step

    def at(self, layer, i):
        return self.sem, self.step * (self.base[layer] + i + 1)


RING = 6
MAX_BANK, SCORE_BANK, TR_BANK, O_BANK = (0, 1), (2, 3, 4), 5, (6, 7)


def alternate(main, extra):
    taken = 0
    for i, step in enumerate(main):
        yield step, False
        while taken * len(main) < (i + 1) * len(extra):
            yield extra[taken], True
            taken += 1


def spread(main, extra):
    return [step for step, _ in alternate(main, extra)] if main else extra


def attention_steps(L):
    n = L.index
    out = []

    def chunk_units(c):
        return [(kind, c, u) for kind in ("q", "k", "rh", "rw") for u in range(2)]

    if n == 0:
        out.append(("ln", 0, 0, 0))
    upfront = 1 if L.split else 2
    early = [("q", 0, 0), ("k", 0, 0)]
    out += [(*unit, 4 + k) for k, unit in enumerate(early)]
    out.append(("ln", 0, 1, 2))
    bank = 0
    for c in range(upfront):
        for unit in chunk_units(c):
            if unit not in early:
                out.append((*unit, bank))
                bank = (bank + 1) % 4
        out += [("aug", h, 0, 0) for h in range(c * L.per_chunk, (c + 1) * L.per_chunk)]
    out += [("v", t, 0, 4 + 2 * (t % 2)) for t in range(TILES)]
    units = [unit for c in range(upfront, L.chunks) for unit in chunk_units(c)]
    if L.split:
        out += [(*units.pop(0), k) for k in range(4)]
    for h in range(2):
        out += [("max", h, k, 0) for k in range(4)] + [("maxT", h, 0, 0)]
    waiting = list(range(upfront * L.per_chunk, HEADS))
    ready, scored = upfront * L.per_chunk, 0

    def lay_out_heads():
        while waiting and waiting[0] < ready and waiting[0] - RING < scored:
            out.append(("aug", waiting.pop(0), 0, 0))

    finished = []
    for h in range(0, HEADS, 2):
        main = [("scores", a, k, 0) for a in (h, h + 1) for k in range(L.units)]
        main += [("pv", h, k, 0) for k in range(L.units if L.pads else NB)]
        maxima = []
        if h + 2 < HEADS:
            for a in (h + 2, h + 3):
                maxima += [("max", a, k, 0) for k in range(4)] + [("maxT", a, 0, 0)]
        mine, units = units[:L.per_pair], units[L.per_pair:]
        extra = [(*unit, TR_BANK) for unit in mine]
        fill = spread(maxima[:6], extra) + maxima[6:]
        for k, part in enumerate(finished):
            fill.insert(min(1 + 3 * k, len(fill)), part)
        for step, filled in alternate(main, fill):
            if not filled:
                out.append(step)
                if step[0] == "scores" and step[2] == L.units - 1:
                    scored = step[1] + 1
                    lay_out_heads()
            else:
                out.append(step)
                if step[0] == "rw" and step[2] == 1:
                    ready = (step[1] + 1) * L.per_chunk
                    lay_out_heads()
        if (h + 2) % L.per_group == 0:
            g = h // L.per_group
            out.append(("copy_o", g, 0, 0))
            out.append(("sums", g, 0, 0))
            finished = [("inverse", g, 0, 0), ("divide", g, 0, 0)]
        else:
            finished = []
    out += finished
    assert not units and not waiting
    out += [("proj", t, 0, t) for t in range(TILES)]
    out += [("proj", t, 1, t) for t in range(4)] + [("ln", 1, 0, 0)]
    out += [("proj", t, 1, t) for t in range(4, TILES)] + [("ln", 1, 1, 2)]
    out += [("up", m, 0, m % 4) for m in range(FM)]
    out += [("down", t, 0, 4 + t % 4) for t in range(4)]
    out += [("up", m, 1, (m + 2) % 4) for m in range(FM)]
    if n + 1 < len(LAYERS):
        out.append(("next_ln", 0, 0, 0))
    out += [("down", t, 0, 4 + t % 4) for t in range(4, TILES)]
    return out


def all_steps():
    for L in LAYERS:
        for step, i, u, bank in attention_steps(L):
            if step == "next_ln":
                yield LAYERS[L.index + 1], "ln", i, u, bank
            else:
                yield L, step, i, u, bank


def build(nc, io, out):
    with ExitStack() as ctx:
        _build(nc, ctx, io, out)


def _build(nc, ctx, io, out):
    def sb(where, name, shape, dt=F32):
        return where.enter_context(nc.sbuf_tensor(name, shape, dt))

    def count(name, per_layer, step=1):
        return Count(nc, ctx, name, per_layer, step)

    X = sb(ctx, "X", [128, TILES, C])
    XN = sb(ctx, "XN", [128, TILES, C])
    XT = sb(ctx, "XT", [CK, 2, NT])
    IDN = sb(ctx, "IDN", [128, 128])
    STAT = sb(ctx, "STAT", [128, TILES, 6])
    MV = sb(ctx, "MV", [128, TILES, 2])
    STD = sb(ctx, "STD", [128, TILES])
    RSTD = sb(ctx, "RSTD", [128, TILES])
    EPS = sb(ctx, "EPS", [128, 2])
    WQKV = sb(ctx, "WQKV", [CK, 2, 3 * max(L.dim for L in LAYERS)])
    COL = [sb(ctx, f"COL{L.index}", [128, 8 + 2 * L.chunks + FM]) for L in LAYERS]
    SKB = [sb(ctx, f"SKB{L.index}", [CK, L.chunks]) for L in LAYERS]
    VB = [sb(ctx, f"VB{L.index}", [128, L.dim]) for L in LAYERS]
    B2 = [sb(ctx, f"B2_{L.index}", [128, C]) for L in LAYERS]
    RB = [sb(ctx, f"RB{L.index}", [CK, 2, L.rel, L.per_chunk]) for L in LAYERS]
    PS = ctx.enter_context(nc.psum_tensor("PS", [128, 8, 512], F32))

    mem = []
    for L in LAYERS:
        n = L.index
        m = {}
        frame = ExitStack()
        m["WP"] = sb(frame, f"WP{n}", [128, L.groups, C])
        attn = ExitStack()
        dt = F32R if L.split else F32
        m["QA"] = sb(attn, f"QA{n}", [L.rows, RING, NT], dt)
        m["KA"] = sb(attn, f"KA{n}", [L.rows, RING, L.keys], dt)
        rw = L.per_chunk * L.win
        m["q"] = [sb(attn, f"QD{n}_{i}", [CK, NT]) for i in range(L.bufs)]
        m["k"] = [sb(attn, f"KD{n}_{i}", [CK, L.keys]) for i in range(L.bufs)]
        if L.split:
            m["QHL"] = sb(attn, f"QHL{n}", [CK, 2, NT], F32R)
            m["KHL"] = sb(attn, f"KHL{n}", [CK, 2, L.keys], F32R)
            m["REL"] = [sb(attn, f"REL{n}", [rw, 4, NT], F32R)]
            m["KC32"] = sb(attn, f"KC32_{n}", [L.rows - L.rel_row, TOK + L.pad_cols])
            m["KC"] = sb(attn, f"KC{n}", [L.rows - L.rel_row, TOK + L.pad_cols], F32R)
            m["QM32"] = sb(attn, f"QM32_{n}", [5, TOK])
            m["QM"] = sb(attn, f"QM{n}", [5, TOK], F32R)
            m["BV"] = sb(attn, f"BV{n}", [L.pc, HEADS, L.slot])
            m["PP"] = sb(attn, f"PP{n}", [L.pc, 2, 2, NE])
            m["NRH"] = sb(attn, f"NRH{n}", [TILES, 2, 128], F32R)
            m["NRL"] = sb(attn, f"NRL{n}", [TILES, 2, 128], F32R)
        else:
            m["REL"] = [sb(attn, f"REL{n}_{i}", [rw, 2, NT]) for i in range(L.bufs)]
            m["NR"] = sb(attn, f"NR{n}", [TILES, 2, 128])
        m["V"] = sb(attn, f"V{n}", [128, TILES, HEADS * L.vcol + L.slot - L.vcol])
        m["OT"] = sb(attn, f"OT{n}", [128, L.groups, NT])
        m["OS"] = sb(attn, f"OS{n}", [128, 2, 512])
        m["SUMS"] = sb(attn, f"SUMS{n}", [128, 2, L.per_group * NT // 128])
        m["PT"] = sb(attn, f"PT{n}", [128, 2, 2, NT])
        m["NM"] = sb(attn, f"NM{n}", [128, 2, TILES])
        attn.close()
        m["W1"] = sb(frame, f"W1_{n}", [CK, 2, FF])
        m["W2"] = sb(frame, f"W2_{n}", [128, FM, C])
        m["HT"] = sb(frame, f"HT{n}", [128, FM, NT])
        frame.close()
        mem.append(m)
    spectral = ExitStack()
    spectral.enter_context(nc.sbuf_tensor("under_mlp", [128, 11000], F32))
    FW = sb(spectral, "FW", [128, 2, 2 * MODES])
    GI = sb(spectral, "GI", [MT, 2, 2, TOK])
    WS = sb(spectral, "WS", [CK, 2, 2, 2, CK])
    W1N = sb(spectral, "W1N", [CK, 2, CK])
    W2S = sb(spectral, "W2S", [CK, 2, 2, 2, CK])
    SB1 = sb(spectral, "SB1", [CK, 2, 2])
    SB2 = sb(spectral, "SB2", [MT, 2, 2, CK])
    XF = sb(spectral, "XF", [CK, 2, 2, NB * MODES])
    O1 = sb(spectral, "O1", [CK, 2, 2, NB * MODES])
    O2 = sb(spectral, "O2", [MT, 2, NB, 2, 2, CK])
    SH = sb(spectral, "SH", [MT, 2, 2, 2 * C])
    Y = sb(spectral, "Y", [128, TILES, C])
    spectral.close()

    def per(f):
        return [f(L) for L in LAYERS] + [0]

    dve_step = ctx.enter_context(nc.semaphore("dve_step"))
    x_in = count("x_in", [1, 0, 0, 0], 16)
    first_in = count("first_in", [3, 0, 0, 0], 16)
    const_in = count("const_in", [4 * 3 - 1, 0, 0, 0], 16)
    wqkv_in = count("wqkv_in", [1, 1, 1, 0], 16)
    wp_in = count("wp_in", [1, 1, 1, 0], 16)
    mlp_in = count("mlp_in", [2, 2, 2, 0], 16)
    masks_in = count("masks_in", per(lambda L: 2 if L.split else 0), 16)
    spectral_in = count("spectral_in", [0, 0, 0, 5], 16)
    const_rows = per(lambda L: RING * (3 if L.split else 1))
    aug_const = count("aug_const", const_rows, 16)
    masks_cast = count("masks_cast", per(lambda L: 2 if L.split else 0))
    v_ones = count("v_ones", [1, 1, 1, 0])
    pad_values = count("pad_values", per(lambda L: 1 if L.pads else 0))
    pad_keys = count("pad_keys", per(lambda L: L.chunks if L.pads else 0))
    skb_done = count("skb_done", [1, 1, 1, 0])
    mean_var = count("mean_var", [4, 4, 4, 0])
    std_done = count("std_done", [4, 4, 4, 0])
    xn_done = count("xn_done", [2 * TILES] * 3 + [0])
    xt_psum = count("xt_psum", [8, 8, 8, 0])
    xt_done = count("xt_done", [8, 8, 8, 0])
    v_psum = count("v_psum", [TILES] * 3 + [0])
    v_done = count("v_done", [TILES] * 3 + [0])
    two = per(lambda L: 2 * L.chunks)
    two_split = per(lambda L: 2 * L.chunks if L.split else 0)
    psum_of = {kind: count(kind + "_psum", two) for kind in ("q", "k", "rh", "rw")}
    q_done, k_done = count("q_done", two), count("k_done", two)
    rh_done, rw_done = count("rh_done", two), count("rw_done", two)
    rh_hi_done, rw_hi_done = count("rh_hi_done", two_split), count("rw_hi_done", two_split)
    split_hi, split_lo = count("split_hi", two_split), count("split_lo", two_split)
    aug_in = [count(f"aug_in{r}", per(lambda L: L.aug_dmas * (HEADS // RING)), 16) for r in range(RING)]
    max_psum = count("max_psum", [HEADS * TILES] * 3 + [0])
    max_done = count("max_done", [HEADS * TILES] * 3 + [0])
    maxT_psum = count("maxT_psum", [HEADS] * 3 + [0])
    maxT_hi_done = count("maxT_hi_done", per(lambda L: HEADS if L.split else 0))
    maxT_done = count("maxT_done", [HEADS] * 3 + [0])
    max_row_in = [count(f"max_row_in{p}", per(lambda L: HEADS // 2 * (2 if L.split else 1)), 16)
                  for p in (0, 1)]
    scores_psum = count("scores_psum", per(lambda L: HEADS * L.units))
    probs_done = count("probs_done", per(lambda L: HEADS * L.units))
    pv_done = count("pv_done", per(lambda L: HEADS // 2 * L.units))
    o_copied = count("o_copied", per(lambda L: 2 * L.groups))
    one_group = per(lambda L: L.groups)
    sums_in, inv_stored, inv_in = (count(x, one_group, 16) for x in ("sums_in", "inv_stored", "inv_in"))
    sums_inv = count("sums_inv", one_group)
    o_done = count("o_done", per(lambda L: 2 * L.groups))
    proj_psum = count("proj_psum", [TILES] * 3 + [0])
    x_mid = count("x_mid", [TILES] * 3 + [0])
    x_biased = count("x_biased", [2] * 3 + [0])
    up_psum = count("up_psum", [2 * FM] * 3 + [0])
    gelu_done = count("gelu_done", [2 * FM] * 3 + [0])
    down_psum = count("down_psum", [TILES] * 3 + [0])
    x_end = count("x_end", [TILES] * 3 + [0])
    w_prep = count("w_prep", [0, 0, 0, 3])
    fwd_psum, fwd_done = count("fwd_psum", [0, 0, 0, 8]), count("fwd_done", [0, 0, 0, 4])
    fwd_done_odd = count("fwd_done_odd", [0, 0, 0, 4])
    s1_psum, s1_done = count("s1_psum", [0, 0, 0, 8]), count("s1_done", [0, 0, 0, 8])
    s2_psum, s2_biased = count("s2_psum", [0, 0, 0, 8]), count("s2_biased", [0, 0, 0, 8])
    s2_clamped, s2_done = count("s2_clamped", [0, 0, 0, 8]), count("s2_done", [0, 0, 0, 8])
    inv_psum = count("inv_psum", [0, 0, 0, TILES])
    y_done = count("y_done", [0, 0, 0, TILES])
    y_out = count("y_out", [0, 0, 0, 2], 16)

    def aug_at(L, h):
        return aug_in[h % RING].at(L.index, (h // RING + 1) * L.aug_dmas - 1)

    def max_row_at(L, h):
        k = 2 if L.split else 1
        return max_row_in[h % 2].at(L.index, (h // 2 + 1) * k - 1)

    def chunk_read(L, c):
        return [aug_at(L, h) for h in range(c * L.per_chunk, (c + 1) * L.per_chunk)]

    def inverses(L, g):
        return io["inverses"][g * L.per_group:(g + 1) * L.per_group, :]

    def values(L, t, h):
        return mem[L.index]["V"][:, t, h * L.vcol:h * L.vcol + L.slot]

    def image(ap):
        return ap.rearrange("r (b y x) -> r b y x", b=NB, y=IMG)

    def rel_views(L, m, step, c, u, bank, low):
        rows = L.per_chunk * L.win
        tile = m["REL"][c % L.bufs][:, 2 * low + (step == "rw"), :]
        part = slice(8 * u, 8 * u + 8)
        if step == "rh":
            return image(tile)[:, :, part, :], PS[0:rows, bank, :].rearrange("r (y b x) -> r b y x", b=NB, y=8)
        return image(tile)[:, :, :, part], PS[0:rows, bank, :].rearrange("r (x b y) -> r b y x", b=NB, x=8)

    def raw(ap):
        return ap.bitcast(F32) if ap.dtype == F32R else ap

    block = ctx.enter_context(nc.Block())

    @block.sync
    def _(sp):
        sp.dma_start(X[:, :, :], io["x"].rearrange("(t p) c -> p t c", p=128)).then_inc(x_in.sem, 16)
        for dst, src in ((IDN[:, :], io["idn"]), (EPS[:, :], io["eps"]), (COL[0][:, :], io["col0"])):
            sp.dma_start(dst, src).then_inc(first_in.sem, 16)

        def load_wqkv(n):
            sp.dma_start(WQKV[:, :, 0:3 * LAYERS[n].dim], io[f"wqkv{n}"]).then_inc(wqkv_in.sem, 16)

        def load_attention(L):
            n, m = L.index, mem[L.index]
            rows = L.rows - L.rel_row
            if L.split:
                sp.dma_start(m["KC32"][:, :], io[f"kc{n}"]).then_inc(masks_in.sem, 16)
                sp.dma_start(m["QM32"][:, :], io["qm"]).then_inc(masks_in.sem, 16)
            if n:
                sp.wait_ge(*x_end.at(n - 1, TILES - 1))
            sp.dma_start(m["WP"][:, :, :], io[f"wp{n}"]).then_inc(wp_in.sem, 16)
            if L.split:
                sp.wait_ge(*masks_cast.at(n, 1))
            for s in range(RING):
                kdst = raw(m["KA"][L.rel_row:L.rows, s, :])
                ksrc = raw(m["KC"][:, :]) if L.split else io[f"kc{n}"]
                sp.dma_start(kdst[:, 0:NT].rearrange("r (b t) -> r b t", b=NB),
                             ksrc[:, 0:TOK].unsqueeze(1).broadcast_to([rows, NB, TOK])).then_inc(aug_const.sem, 16)
                if L.split:
                    sp.dma_start(kdst[:, NT:], ksrc[:, TOK:]).then_inc(aug_const.sem, 16)
                    sp.dma_start(raw(m["QA"][L.mask_row:L.max_row, s, :]).rearrange("r (b t) -> r b t", b=NB),
                                 raw(m["QM"][:, :]).unsqueeze(1).broadcast_to([5, NB, TOK]))\
                        .then_inc(aug_const.sem, 16)

        load_wqkv(0)
        for L in LAYERS:
            n = L.index
            for dst, src in ((RB[n][:, :, :, :], io[f"rb{n}"]), (VB[n][:, :], io[f"vb{n}"].partition_broadcast(128)),
                             (B2[n][:, :], io[f"b2_{n}"].partition_broadcast(128)),
                             (COL[n][:, :], io[f"col{n}"]))[:3 if n == 0 else 4]:
                sp.dma_start(dst, src).then_inc(const_in.sem, 16)
        load_attention(LAYERS[0])
        for L, step, h, u, bank in all_steps():
            n, m = L.index, mem[L.index]
            if step == "aug":
                s, c, i = h % RING, h // L.per_chunk, h % L.per_chunk
                buf = c % L.bufs
                if h >= RING:
                    sp.wait_ge(*scores_psum.at(n, L.units * (h - RING + 1) - 1))
                elif n:
                    sp.wait_ge(*x_end.at(n - 1, TILES - 1))
                qa, ka, hd = m["QA"][:, s, :], m["KA"][:, s, :], L.hd
                mine = slice(i * hd, (i + 1) * hd)
                if L.split:
                    sp.wait_ge(*split_lo.at(n, 2 * c))
                    moves = [(qa[0:2 * hd, :], m["QHL"][mine, :, :]), (qa[2 * hd:3 * hd, :], m["QHL"][mine, 0, :])]
                    for dst, src in moves:
                        sp.dma_start(raw(dst), raw(src)).then_inc(aug_in[s].sem, 16)
                    sp.wait_ge(*split_lo.at(n, 2 * c + 1))
                    twice = m["KHL"][mine, 0, :].unsqueeze(1).broadcast_to([hd, 2, L.keys])
                    moves = [(ka[0:2 * hd, :], twice), (ka[2 * hd:3 * hd, :], m["KHL"][mine, 1, :])]
                else:
                    sp.wait_ge(*q_done.at(n, 2 * c + 1))
                    sp.wait_ge(*k_done.at(n, 2 * c + 1))
                    moves = [(qa[0:hd, :], m["q"][buf][mine, :]), (ka[0:hd, :], m["k"][buf][mine, :])]
                for dst, src in moves:
                    sp.dma_start(raw(dst), raw(src)).then_inc(aug_in[s].sem, 16)
                sp.wait_ge(*rh_done.at(n, 2 * c + 1))
                sp.wait_ge(*rw_done.at(n, 2 * c + 1))
                sp.dma_start(raw(qa[L.rel_row:L.mask_row, :]), raw(m["REL"][buf][i::L.per_chunk, :, :]))\
                    .then_inc(aug_in[s].sem, 16)
            elif step == "maxT":
                s, p = h % RING, h % 2
                sp.wait_ge(*maxT_done.at(n, h))
                for r, part in enumerate((m["NRH"], m["NRL"]) if L.split else (m["NR"],)):
                    sp.dma_start(raw(m["QA"][L.max_row + r:L.max_row + r + 1, s, :]), raw(part[:, p, :]))\
                        .then_inc(max_row_in[p].sem, 16)
            elif step == "sums":
                sp.wait_ge(*o_copied.at(n, 2 * h + 1))
                if h:
                    sp.wait_ge(*sums_inv.at(n, h - 1))
                sp.dma_start(m["SUMS"][:, 0, :], m["OS"][L.hd::L.slot, :, :]).then_inc(sums_in.sem, 16)
            elif step == "inverse":
                sp.wait_ge(*sums_inv.at(n, h))
                sp.dma_start(inverses(L, h).rearrange("g (p c) -> (g p) c", p=L.slot), m["SUMS"][:, 1, :])\
                    .then_inc(inv_stored.sem, 16)
            elif step == "divide":
                sp.wait_ge(*inv_stored.at(n, h))
                sp.dma_start(m["OT"][:, h, :], inverses(L, h).unsqueeze(1).broadcast_to([L.per_group, L.slot, NT]))\
                    .then_inc(inv_in.sem, 16)
            elif step == "scores" and h == HEADS - 1 and u == L.units - 1:
                sp.wait_ge(*scores_psum.at(n, L.units * HEADS - 1))
                sp.dma_start(m["W1"][:, :, :], io[f"w1_{n}"]).then_inc(mlp_in.sem, 16)
                sp.dma_start(m["W2"][:, :, :], io[f"w2_{n}"]).then_inc(mlp_in.sem, 16)
                if n + 1 < len(LAYERS):
                    sp.wait_ge(*rw_done.at(n, 2 * L.chunks - 1))
                    load_wqkv(n + 1)
            elif step == "ln" and h == 1 and u == 1:
                sp.wait_ge(*x_mid.at(n, TILES - 1))
                if n + 1 == len(LAYERS):
                    for dst, src in ((FW[:, :, :], io["fwd"]), (GI[:, :, :, :], io["inv"]),
                                     (WS[:, :, :, :, :], io["ws"]), (SB1[:, :, :], io["sb1"]),
                                     (SB2[:, :, :, :], io["sb2"].partition_broadcast(MT))):
                        sp.dma_start(dst, src).then_inc(spectral_in.sem, 16)
            elif step == "up" and h == FM - 1 and u == 1 and n + 1 < len(LAYERS):
                load_attention(LAYERS[n + 1])
        for half in range(2):
            t = TILES // 2
            sp.wait_ge(*y_done.at(3, (half + 1) * t - 1))
            sp.dma_start(out[half * t * 128:(half + 1) * t * 128, :].rearrange("(t p) c -> p t c", p=128),
                         Y[:, half * t:(half + 1) * t, :]).then_inc(y_out.sem, 16)
        sp.wait_ge(*y_out.at(3, 1))

    @block.gpsimd
    def _(pool):
        def prepare(L):
            n, m = L.index, mem[L.index]
            if n:
                pool.wait_ge(*x_mid.at(n - 1, TILES - 1))
            v = m["V"][:, :, 0:HEADS * L.vcol].rearrange("p t (h d) -> p t h d", h=HEADS)
            for t in range(TILES):
                nc.gpsimd.memset(v[:, t, :, L.hd + 1:], 0.0)
                if L.slot > L.vcol:
                    nc.gpsimd.memset(m["V"][:, t, HEADS * L.vcol:], 0.0)
                ins = nc.gpsimd.memset(v[:, t, :, L.hd:L.hd + 1], 1.0)
            ins.then_inc(v_ones.sem, 1)
            if L.pads:
                pool.wait_ge(*const_in.at(0, 10))
                nc.gpsimd.memset(m["BV"][:, :, L.hd + 1:], 0.0)
                nc.gpsimd.memset(m["BV"][:, :, L.hd:L.hd + 1], 1.0)
                nc.gpsimd.tensor_copy(m["BV"][:, :, 0:L.hd],
                                      VB[n][0:L.pc, :].rearrange("p (h d) -> p h d", h=HEADS))\
                    .then_inc(pad_values.sem, 1)
            if L.split:
                pool.wait_ge(*masks_in.at(n, 1))
                nc.gpsimd.tensor_copy(m["KC"][:, :], m["KC32"][:, :]).then_inc(masks_cast.sem, 1)
                nc.gpsimd.tensor_copy(m["QM"][:, :], m["QM32"][:, :]).then_inc(masks_cast.sem, 1)

        prepare(LAYERS[0])
        for L, step, i, u, bank in all_steps():
            n, m = L.index, mem[L.index]
            if step in ("q", "k") and u == 1 and L.split:
                part, done = (m["QHL"], q_done) if step == "q" else (m["KHL"], k_done)
                at = 2 * i + (step == "k")
                if i:
                    for wait in chunk_read(L, i - 1):
                        pool.wait_ge(*wait)
                pool.wait_ge(*done.at(n, 2 * i + 1))
                if step == "k":
                    pool.wait_ge(*pad_keys.at(n, i))
                src = m[step][0][:, :]
                nc.gpsimd.tensor_copy(part[:, 0, :], src).then_inc(split_hi.sem, 1)
                pool.wait_ge(*split_hi.at(n, at))
                nc.gpsimd.tensor_tensor(part[:, 1, :], src, part[:, 0, :].bitcast(F32), ALU.subtract)\
                    .then_inc(split_lo.sem, 1)
            elif step == "divide":
                pool.wait_ge(*inv_in.at(n, i))
                for k in range(2):
                    o = m["OT"][:, i, k * 512:(k + 1) * 512]
                    nc.gpsimd.tensor_tensor(o, m["OS"][:, k, :], o, ALU.mult).then_inc(o_done.sem, 1)
            elif step == "ln" and i == 1:
                pool.wait_ge(*xn_done.at(n, TILES + 4 * u + 3))
                for t in range(4 * u, 4 * u + 4):
                    ins = nc.gpsimd.tensor_tensor(X[:, t, :], X[:, t, :], B2[n][:, :], ALU.add)
                ins.then_inc(x_biased.sem, 1)
            elif step == "down" and i == 0 and n + 1 < len(LAYERS):
                prepare(LAYERS[n + 1])
        pool.wait_ge(*spectral_in.at(3, 4))
        nc.gpsimd.tensor_scalar(W1N[:, :, :], WS[:, 0, :, 1, :], -1.0, None, ALU.mult).then_inc(w_prep.sem, 1)
        nc.gpsimd.tensor_copy(W2S[:, :, 0, :, :], WS[:, 1, :, :, :])
        nc.gpsimd.tensor_copy(W2S[:, :, 1, 1, :], WS[:, 1, :, 0, :]).then_inc(w_prep.sem, 1)
        nc.gpsimd.tensor_scalar(W2S[:, :, 1, 0, :], WS[:, 1, :, 1, :], -1.0, None, ALU.mult).then_inc(w_prep.sem, 1)
        for u in range(8):
            pool.wait_ge(*s2_biased.at(3, u))
            if u >= 2:
                pool.wait_ge(*s2_done.at(3, u - 2))
            nc.gpsimd.tensor_scalar(SH[:, 1, u % 2, :], SH[:, 0, u % 2, :], SHRINK, -SHRINK, ALU.min, ALU.max)\
                .then_inc(s2_clamped.sem, 1)

    @block.scalar
    def _(act):
        act.wait_ge(*first_in.at(0, 2))
        for L, step, i, u, bank in all_steps():
            n, m = L.index, mem[L.index]
            if step == "ln":
                s, tiles = i, slice(4 * u, 4 * u + 4)
                e = 1 if L.eps == 1e-6 else 0
                act.wait_ge(*mean_var.at(n, 2 * s + u))
                nc.scalar.activation(STD[:, tiles], MV[:, tiles, 1], ACT.Sqrt, bias=EPS[:, e:e + 1])\
                    .then_inc(std_done.sem, 1)
                g = COL[n][0:CK, 4 * s:4 * s + 4]
                for k in range(2):
                    act.wait_ge(*xt_psum.at(n, 4 * s + 2 * u + k))
                    nc.scalar.activation(XT[:, k, u * 512:(u + 1) * 512], PS[0:CK, bank + k, :], ACT.Identity,
                                         scale=g[:, k:k + 1], bias=g[:, 2 + k:3 + k]).then_inc(xt_done.sem, 1)
            elif step in ("q", "k"):
                if i >= L.bufs and u == 0:
                    act.wait_ge(*psum_of["rw"].at(n, 2 * (i - L.bufs) + 1))
                    if L.split:
                        act.wait_ge(*split_lo.at(n, 2 * (i - 1) + 1))
                    else:
                        for wait in chunk_read(L, i - L.bufs):
                            act.wait_ge(*wait)
                act.wait_ge(*psum_of[step].at(n, 2 * i + u))
                dst = m[step][i % L.bufs][:, u * 512:(u + 1) * 512]
                if step == "q":
                    nc.scalar.activation(dst, PS[0:CK, bank, :], ACT.Identity, bias=COL[n][0:CK, 8 + i:9 + i])\
                        .then_inc(q_done.sem, 1)
                else:
                    if i == 0 and u == 0:
                        act.wait_ge(*skb_done.at(n, 0))
                    nc.scalar.activation(dst, PS[0:CK, bank, :], ACT.Identity, bias=SKB[n][:, i:i + 1],
                                         scale=L.scale).then_inc(k_done.sem, 1)
            elif step == "rh" or (step == "rw" and L.split):
                act.wait_ge(*psum_of[step].at(n, 2 * i + u))
                if i >= L.bufs and u == 0:
                    for wait in chunk_read(L, i - L.bufs):
                        act.wait_ge(*wait)
                dst, src = rel_views(L, m, step, i, u, bank, 0)
                nc.scalar.activation(dst, src, ACT.Copy)\
                    .then_inc((rh_hi_done if step == "rh" else rw_hi_done).sem if L.split else rh_done.sem, 1)
            elif step == "scores":
                h, k = i, u
                if h >= 2:
                    act.wait_ge(*pv_done.at(n, L.units * (h // 2 - 1) + (2 * (k // 2) + 1 if k < 4 else 4)))
                j = L.units * h + k
                act.wait_ge(*scores_psum.at(n, j))
                if k < 4:
                    dst, src = m["PT"][:, h % 2, k % 2, (k // 2) * 512:(k // 2 + 1) * 512], \
                        PS[:, SCORE_BANK[j % 3], :]
                else:
                    dst, src = m["PP"][:, h % 2, :, :], PS[0:L.pc, SCORE_BANK[j % 3], 0:2 * NE]
                nc.scalar.activation(dst, src, ACT.Exp).then_inc(probs_done.sem, 1)
            elif step == "copy_o":
                act.wait_ge(*pv_done.at(n, (i + 1) * L.per_group // 2 * L.units - 1))
                if i:
                    act.wait_ge(*o_done.at(n, 2 * i - 1))
                for k in range(2):
                    nc.scalar.activation(m["OS"][:, k, :], PS[:, O_BANK[k], :], ACT.Copy).then_inc(o_copied.sem, 1)
            elif step == "up":
                j = FM * u + i
                act.wait_ge(*up_psum.at(n, j))
                b1 = 8 + 2 * L.chunks + i
                nc.scalar.activation(m["HT"][:, i, u * 512:(u + 1) * 512], PS[:, bank, :], L.gelu,
                                     bias=COL[n][:, b1:b1 + 1]).then_inc(gelu_done.sem, 1)
        act.wait_ge(*spectral_in.at(3, 4))
        for u in range(0, 8, 2):
            b, cc = divmod(u, 2)
            act.wait_ge(*fwd_psum.at(3, u))
            nc.scalar.activation(XF[:, cc, :, b * MODES:(b + 1) * MODES],
                                 PS[0:CK, u, 0:2 * MODES].rearrange("p (r m) -> p r m", r=2), ACT.Copy)\
                .then_inc(fwd_done.sem, 1)
        for u in range(8):
            cc, r, half = u // 4, u // 2 % 2, u % 2
            act.wait_ge(*s1_psum.at(3, u))
            nc.scalar.activation(O1[:, cc, r, half * 2 * MODES:(half + 1) * 2 * MODES], PS[0:CK, u, 0:2 * MODES],
                                 ACT.Relu, bias=SB1[:, cc, r:r + 1]).then_inc(s1_done.sem, 1)

    @block.vector
    def _(dve):
        steps = [0]

        def link(ins):
            steps[0] += 1
            ins.then_inc(dve_step, 1)
            dve.wait_ge(dve_step, steps[0])

        dve.wait_ge(*x_in.at(0, 0))
        dve.wait_ge(*first_in.at(0, 2))
        for L, step, i, u, bank in all_steps():
            n, m = L.index, mem[L.index]
            if step == "ln":
                s, tiles = i, range(4 * u, 4 * u + 4)
                for t in tiles:
                    if s == 1:
                        dve.wait_ge(*x_mid.at(n, t))
                    elif n:
                        dve.wait_ge(*x_end.at(n - 1, t))
                    ins = nc.vector.bn_stats(STAT[:, t, :], X[:, t, :])
                link(ins)
                for t in tiles:
                    ins = nc.vector.bn_aggr(MV[:, t, :], STAT[:, t, :])
                ins.then_inc(mean_var.sem, 1)
                dve.wait_ge(*mean_var.at(n, 2 * s + u))
                dve.wait_ge(*std_done.at(n, 2 * s + u))
                link(nc.vector.reciprocal(RSTD[:, 4 * u:4 * u + 4], STD[:, 4 * u:4 * u + 4]))
                if 2 * n + s:
                    last = 4 * s + 2 * u + 1 - 4
                    dve.wait_ge(*(xt_psum.at(n, last) if s else xt_psum.at(n - 1, last + 8)))
                for t in tiles:
                    nc.vector.tensor_scalar(XN[:, t, :], X[:, t, :], MV[:, t, 0:1], RSTD[:, t:t + 1],
                                            ALU.subtract, ALU.mult).then_inc(xn_done.sem, 1)
            elif step == "v":
                t = i
                if t == 0:
                    dve.wait_ge(*v_ones.at(n, 0))
                    dve.wait_ge(*const_in.at(0, 10))
                dve.wait_ge(*v_psum.at(n, t))
                nh = HEADS if L.hd == 16 else HEADS // 2
                v = m["V"][:, t, 0:HEADS * L.vcol].rearrange("p (h d) -> p h d", h=HEADS)
                for g in range(HEADS // nh):
                    ins = nc.vector.tensor_tensor(
                        v[:, g * nh:(g + 1) * nh, 0:L.hd],
                        PS[:, bank + g, 0:nh * L.hd].rearrange("p (h d) -> p h d", h=nh),
                        VB[n][:, g * nh * L.hd:(g + 1) * nh * L.hd].rearrange("p (h d) -> p h d", h=nh), ALU.add)
                ins.then_inc(v_done.sem, 1)
            elif step == "q" and i == 0 and u == 0:
                if n:
                    dve.wait_ge(*const_in.at(0, 10))
                nc.vector.tensor_scalar(SKB[n][:, :], COL[n][0:CK, 8 + L.chunks:8 + 2 * L.chunks], L.scale,
                                        None, ALU.mult).then_inc(skb_done.sem, 1)
            elif step == "k" and u == 0 and L.pads:
                if i:
                    dve.wait_ge(*split_lo.at(n, 2 * (i - 1) + 1))
                nc.vector.tensor_scalar(m["k"][0][:, NT:],
                                        COL[n][0:CK, 8 + L.chunks + i:9 + L.chunks + i].broadcast_to([CK, L.pad_cols]),
                                        L.scale, None, ALU.mult).then_inc(pad_keys.sem, 1)
            elif step in ("rh", "rw") and L.split:
                hi_done, done = (rh_hi_done, rh_done) if step == "rh" else (rw_hi_done, rw_done)
                dve.wait_ge(*hi_done.at(n, 2 * i + u))
                lo, src = rel_views(L, m, step, i, u, bank, 1)
                hi, _ = rel_views(L, m, step, i, u, bank, 0)
                nc.vector.tensor_tensor(lo, src, hi.bitcast(F32), ALU.subtract).then_inc(done.sem, 1)
            elif step == "rw":
                if i >= L.bufs and u == 0:
                    for wait in chunk_read(L, i - L.bufs):
                        dve.wait_ge(*wait)
                dve.wait_ge(*psum_of["rw"].at(n, 2 * i + u))
                dst, src = rel_views(L, m, step, i, u, bank, 0)
                nc.vector.tensor_copy(dst, src).then_inc(rw_done.sem, 1)
            elif step == "max":
                h = i
                if h >= 2 and u == 0:
                    dve.wait_ge(*maxT_psum.at(n, h - 2))
                for k in range(2 * u, 2 * u + 2):
                    j = TILES * h + k
                    dve.wait_ge(*max_psum.at(n, j))
                    nc.vector.tensor_reduce(m["NM"][:, h % 2, k:k + 1], PS[:, MAX_BANK[j % 2], 0:TOK + L.npad],
                                            AX.X, ALU.max, negate=True).then_inc(max_done.sem, 1)
            elif step == "maxT":
                h = i
                dve.wait_ge(*maxT_psum.at(n, h))
                if h >= 2:
                    dve.wait_ge(*max_row_at(L, h - 2))
                src = PS[0:TILES, TR_BANK, 0:128]
                if L.split:
                    nc.vector.tensor_copy(m["NRH"][:, h % 2, :], src).then_inc(maxT_hi_done.sem, 1)
                    dve.wait_ge(*maxT_hi_done.at(n, h))
                    nc.vector.tensor_tensor(m["NRL"][:, h % 2, :], src, m["NRH"][:, h % 2, :].bitcast(F32),
                                            ALU.subtract).then_inc(maxT_done.sem, 1)
                else:
                    nc.vector.tensor_copy(m["NR"][:, h % 2, :], src).then_inc(maxT_done.sem, 1)
            elif step == "inverse":
                dve.wait_ge(*sums_in.at(n, i))
                if i:
                    dve.wait_ge(*inv_stored.at(n, i - 1))
                nc.vector.reciprocal(m["SUMS"][:, 1, :], m["SUMS"][:, 0, :]).then_inc(sums_inv.sem, 1)
            elif step == "proj" and u == 1:
                dve.wait_ge(*proj_psum.at(n, i))
                nc.vector.tensor_tensor(X[:, i, :], X[:, i, :], PS[:, bank, 0:C], ALU.add).then_inc(x_mid.sem, 1)
            elif step == "down":
                if i % 4 == 0:
                    dve.wait_ge(*x_biased.at(n, i // 4))
                dve.wait_ge(*down_psum.at(n, i))
                nc.vector.tensor_tensor(X[:, i, :], X[:, i, :], PS[:, bank, 0:C], ALU.add).then_inc(x_end.sem, 1)
        for u in range(1, 8, 2):
            b, cc = divmod(u, 2)
            dve.wait_ge(*fwd_psum.at(3, u))
            nc.vector.tensor_copy(XF[:, cc, :, b * MODES:(b + 1) * MODES],
                                  PS[0:CK, u, 0:2 * MODES].rearrange("p (r m) -> p r m", r=2))\
                .then_inc(fwd_done_odd.sem, 1)

        def shrink(u):
            b, mt = divmod(u, 2)
            dve.wait_ge(*s2_clamped.at(3, u))
            view = "p (c r k) -> p r c k"
            nc.vector.tensor_tensor(O2[:, mt, b, :, :, :], SH[:, 0, u % 2, :].rearrange(view, c=2, r=2),
                                    SH[:, 1, u % 2, :].rearrange(view, c=2, r=2), ALU.subtract)\
                .then_inc(s2_done.sem, 1)

        for u in range(8):
            dve.wait_ge(*s2_psum.at(3, u))
            if u >= 2:
                dve.wait_ge(*s2_done.at(3, u - 2))
            nc.vector.tensor_tensor(SH[:, 0, u % 2, :], PS[0:MT, u, 0:2 * C],
                                    SB2[:, :, :, :].rearrange("p a b c -> p (a b c)"), ALU.add)\
                .then_inc(s2_biased.sem, 1)
            if u:
                shrink(u - 1)
        shrink(7)
        for t in range(TILES):
            dve.wait_ge(*inv_psum.at(3, t))
            nc.vector.tensor_tensor(Y[:, t, :], X[:, t, :], PS[:, t, 0:C], ALU.add).then_inc(y_done.sem, 1)

    @block.tensor
    def _(pe):
        free_by = {}

        def claim(bank, event):
            if bank in free_by:
                pe.wait_ge(*free_by[bank])
            free_by[bank] = event

        def mm(dst, lhsT, rhs, start, stop, loose=False):
            return nc.tensor.matmul(dst, lhsT, rhs, start=start, stop=stop, skip_group_check=loose)

        pe.wait_ge(*first_in.at(0, 2))
        for L, step, i, u, bank in all_steps():
            n, m, D = L.index, mem[L.index], L.dim
            if step == "ln":
                s = i
                for k in range(2):
                    claim(bank + k, xt_done.at(n, 4 * s + 2 * u + k))
                    for t in range(4):
                        pe.wait_ge(*xn_done.at(n, TILES * s + 4 * u + t))
                        last = nc.tensor.transpose(PS[0:CK, bank + k, t * 128:(t + 1) * 128],
                                                   XN[:, 4 * u + t, k * CK:(k + 1) * CK], IDN[:, :])
                    last.then_inc(xt_psum.sem, 1)
            elif step == "v":
                t = i
                pe.wait_ge(*xt_done.at(n, 2 * (t // 4) + 1))
                wide = min(D, 288)
                for g in range(D // wide):
                    claim(bank + g, v_done.at(n, t))
                    for k in range(2):
                        last = mm(PS[:, bank + g, 0:wide], XT[:, k, t * 128:(t + 1) * 128],
                                  WQKV[:, k, 2 * D + g * wide:2 * D + (g + 1) * wide], k == 0, k == 1)
                last.then_inc(v_psum.sem, 1)
            elif step in ("q", "k"):
                c, part = i, int(step == "k")
                pe.wait_ge(*wqkv_in.at(n, 0))
                pe.wait_ge(*xt_done.at(n, 2 * u + 1))
                claim(bank, (k_done if part else q_done).at(n, 2 * c + u))
                for k in range(2):
                    last = mm(PS[0:CK, bank, :], WQKV[:, k, part * D + c * CK:part * D + (c + 1) * CK],
                              XT[:, k, u * 512:(u + 1) * 512], k == 0, k == 1)
                last.then_inc(psum_of[step].sem, 1)
            elif step in ("rh", "rw"):
                c, axis = i, int(step == "rw")
                if n + i + u == 0:
                    pe.wait_ge(*const_in.at(0, 10))
                claim(bank, (rw_done if axis else rh_done).at(n, 2 * c + u))
                pe.wait_ge(*q_done.at(n, 2 * c + 1))
                rows = L.per_chunk * L.win
                qd = image(m["q"][c % L.bufs][:, :])
                for y in range(8):
                    at = 8 * u + y
                    last = mm(PS[0:rows, bank, y * 64:(y + 1) * 64],
                              RB[n][:, axis, at % L.win:at % L.win + L.win, :],
                              qd[:, :, :, at] if axis else qd[:, :, at, :], True, True)
                last.then_inc(psum_of[step].sem, 1)
            elif step == "max":
                h, s = i, i % RING
                pe.wait_ge(*aug_at(L, h))
                pe.wait_ge(*aug_const.at(n, const_rows[n] - 1))
                for k in range(2 * u, 2 * u + 2):
                    j, b = TILES * h + k, k // 2
                    claim(MAX_BANK[j % 2], max_done.at(n, j))
                    keys, wide = m["KA"][0:L.max_row, s, b * TOK:(b + 1) * TOK], TOK
                    if L.pads:
                        keys = bass.AP(m["KA"], s * L.keys + b * TOK,
                                       [[RING * L.keys, L.max_row], [NT - b * TOK, 2], [1, TOK]])
                        wide = 2 * TOK
                    mm(PS[:, MAX_BANK[j % 2], 0:wide], m["QA"][0:L.max_row, s, k * 128:(k + 1) * 128], keys,
                       True, True).then_inc(max_psum.sem, 1)
            elif step == "maxT":
                h = i
                pe.wait_ge(*max_done.at(n, TILES * h + TILES - 1))
                claim(TR_BANK, maxT_done.at(n, h))
                nc.tensor.transpose(PS[0:TILES, TR_BANK, 0:128], m["NM"][:, h % 2, :], IDN[:, :])\
                    .then_inc(maxT_psum.sem, 1)
            elif step == "scores":
                h, k, s = i, u, i % RING
                pe.wait_ge(*max_row_at(L, h))
                j = L.units * h + k
                claim(SCORE_BANK[j % 3], probs_done.at(n, j))
                if k < 4:
                    for b in (2 * (k // 2), 2 * (k // 2) + 1):
                        k0 = b * TOK + (k % 2) * 128
                        last = mm(PS[:, SCORE_BANK[j % 3], (b % 2) * TOK:(b % 2 + 1) * TOK],
                                  m["KA"][:, s, k0:k0 + 128], m["QA"][:, s, b * TOK:(b + 1) * TOK], True, True)
                else:
                    q = image(m["QA"][:, s, :])
                    for pc in range(2):
                        keys = m["KA"][:, s, NT + pc * L.pc:NT + (pc + 1) * L.pc]
                        dst = PS[0:L.pc, SCORE_BANK[j % 3], pc * NE:(pc + 1) * NE]
                        mm(dst[:, 0:STRIP_A], keys, q[:, :, :, EDGE:], True, True)
                        last = mm(dst[:, STRIP_A:], keys, q[:, :, EDGE:, 0:EDGE], True, True)
                last.then_inc(scores_psum.sem, 1)
            elif step == "pv":
                pair = (i, i + 1)
                if i % L.per_group == 0 and u == 0:
                    for k in range(2):
                        claim(O_BANK[k], o_copied.at(n, 2 * (i // L.per_group) + k))
                pe.wait_ge(*probs_done.at(n, L.units * (i + 1) + (2 * (u // 2) + 1 if u < 4 else 4)))
                o = {(h, k): PS[h % L.per_group * L.slot:(h % L.per_group + 1) * L.slot, O_BANK[k], :]
                     for h in pair for k in range(2)}
                if u < NB:
                    b = u
                    if i == 0 and u == 0:
                        pe.wait_ge(*v_done.at(n, TILES - 1))
                    for kc in range(2):
                        for h in pair:
                            last = mm(o[h, b // 2][:, (b % 2) * TOK:(b % 2 + 1) * TOK], values(L, 2 * b + kc, h),
                                      m["PT"][:, h % 2, kc, b * TOK:(b + 1) * TOK],
                                      b % 2 == 0 and kc == 0, kc == 1, True)
                else:
                    if i == 0:
                        pe.wait_ge(*pad_values.at(n, 0))
                    na, nb = STRIP_A // 2, STRIP_B // 2
                    for k in range(2):
                        for pc in range(2):
                            for h in pair:
                                p = m["PP"][:, h % 2, pc, :]
                                edge = o[h, k].rearrange("r (b y x) -> r b y x", b=2, y=IMG)
                                mm(edge[:, :, :, EDGE:], m["BV"][:, h, :],
                                   p[:, k * na:(k + 1) * na].rearrange("p (b y x) -> p b y x", b=2, y=IMG),
                                   False, False, True)
                            for h in pair:
                                p = m["PP"][:, h % 2, pc, :]
                                edge = o[h, k].rearrange("r (b y x) -> r b y x", b=2, y=IMG)
                                at = STRIP_A + k * nb
                                last = mm(edge[:, :, EDGE:, 0:EDGE], m["BV"][:, h, :],
                                          p[:, at:at + nb].rearrange("p (b y x) -> p b y x", b=2, y=2),
                                          False, True, True)
                last.then_inc(pv_done.sem, 1)
            elif step == "proj":
                t = i
                if t == 0 and u == 0:
                    pe.wait_ge(*wp_in.at(n, 0))
                if u == 0:
                    claim(bank, x_mid.at(n, t))
                groups = (L.groups - 1,) if u else range(L.groups - 1)
                pe.wait_ge(*o_done.at(n, 2 * groups[-1] + t // 4))
                for g in groups:
                    last = mm(PS[:, bank, 0:C], m["OT"][:, g, t * 128:(t + 1) * 128], m["WP"][:, g, :],
                              g == 0, g == L.groups - 1)
                if u:
                    last.then_inc(proj_psum.sem, 1)
            elif step == "up":
                if i == 0 and u == 0:
                    pe.wait_ge(*mlp_in.at(n, 1))
                pe.wait_ge(*xt_done.at(n, 4 + 2 * u + 1))
                claim(bank, gelu_done.at(n, FM * u + i))
                for k in range(2):
                    last = mm(PS[:, bank, :], m["W1"][:, k, i * 128:(i + 1) * 128],
                              XT[:, k, u * 512:(u + 1) * 512], k == 0, k == 1)
                last.then_inc(up_psum.sem, 1)
            elif step == "down":
                t = i
                pe.wait_ge(*gelu_done.at(n, FM * (t // 4 + 1) - 1))
                claim(bank, x_end.at(n, t))
                for g in range(FM):
                    last = mm(PS[:, bank, 0:C], m["HT"][:, g, t * 128:(t + 1) * 128], m["W2"][:, g, :],
                              g == 0, g == FM - 1)
                last.then_inc(down_psum.sem, 1)
        pe.wait_ge(*spectral_in.at(3, 4))
        pe.wait_ge(*x_end.at(2, TILES - 1))
        for bank in range(8):
            claim(bank, x_end.at(2, TILES - 1))
        for u in range(8):
            b, cc = divmod(u, 2)
            for kt in range(2):
                last = mm(PS[0:CK, u, 0:2 * MODES], X[:, 2 * b + kt, cc * CK:(cc + 1) * CK], FW[:, kt, :],
                          kt == 0, kt == 1)
            last.then_inc(fwd_psum.sem, 1)
        pe.wait_ge(*fwd_done.at(3, 3))
        pe.wait_ge(*fwd_done_odd.at(3, 3))
        pe.wait_ge(*w_prep.at(3, 2))
        for u in range(8):
            cc, r, half = u // 4, u // 2 % 2, u % 2
            cols = slice(half * 2 * MODES, (half + 1) * 2 * MODES)
            own, other = (WS[:, 0, cc, 0, :], W1N[:, cc, :] if r == 0 else WS[:, 0, cc, 1, :])
            mm(PS[0:CK, u, 0:2 * MODES], own, XF[:, cc, r, cols], True, False)
            mm(PS[0:CK, u, 0:2 * MODES], other, XF[:, cc, 1 - r, cols], False, True).then_inc(s1_psum.sem, 1)
        pe.wait_ge(*s1_done.at(3, 7))
        for u in range(8):
            b, mt = divmod(u, 2)
            for cc in range(2):
                for r in range(2):
                    m0 = b * MODES + mt * MT
                    last = mm(PS[0:MT, u, cc * C:(cc + 1) * C], O1[:, cc, r, m0:m0 + MT],
                              W2S[:, cc, r, :, :], r == 0, r == 1)
            last.then_inc(s2_psum.sem, 1)
        for t in range(TILES):
            b, half = divmod(t, 2)
            pe.wait_ge(*s2_done.at(3, 2 * b + 1))
            pe.wait_ge(*s2_biased.at(3, 7))
            for i in range(4):
                mt, r = divmod(i, 2)
                last = mm(PS[:, t, 0:C], GI[:, mt, r, half * 128:(half + 1) * 128],
                          O2[:, mt, b, r, :, :], i == 0, i == 3)
            last.then_inc(inv_psum.sem, 1)


def _pack(inputs):
    def f(name):
        return np.asarray(inputs[name])

    def cols(v, parts):
        return v.reshape(-1, parts).T

    def rows(w, parts):
        return w.reshape(-1, parts, w.shape[-1]).transpose(1, 0, 2)

    names = [("L0_conv_", "norm1_g norm1_b norm2_g norm2_b rel_pos_h rel_pos_w proj_w proj_b mlp_w1 mlp_b1 mlp_w2 mlp_b2"),
             ("L1_conv_", "ln1_scale ln1_offset ln2_scale ln2_offset rel_pos_0 rel_pos_1 wo bo w1 b1 w2 b2"),
             ("L2_conv_", "g1 beta1 g2 beta2 rel_pos_h rel_pos_w w_proj b_proj w_fc1 b_fc1 w_fc2 b_fc2")]
    arrays = {"x": f("x").reshape(NT, C)}
    for L, (prefix, keys) in zip(LAYERS, names):
        n = L.index
        g1, o1, g2, o2, rh, rw, wp, bp, w1, b1, w2, b2 = (f(prefix + k) for k in keys.split())
        if n == 1:
            wqkv = np.concatenate([f(prefix + k) for k in ("wq", "wk", "wv")], 1)
            bqkv = np.concatenate([f(prefix + k) for k in ("bq", "bk", "bv")])
        else:
            wqkv, bqkv = (f(prefix + k) for k in (("qkv_w", "qkv_b") if n == 0 else ("w_qkv", "b_qkv")))
        col = np.zeros((128, 8 + 2 * L.chunks + FM), np.float32)
        at = 0
        for v, parts in ((g1, CK), (o1, CK), (g2, CK), (o2, CK), (bqkv[:2 * L.dim], CK), (b1, 128)):
            c = cols(v, parts)
            col[:parts, at:at + c.shape[1]] = c
            at += c.shape[1]
        place = np.zeros((L.per_group, L.slot, L.groups, C), np.float32)
        place[:, :L.hd] = wp.reshape(L.groups, L.per_group, L.hd, C).transpose(1, 2, 0, 3)
        place[0, L.hd, 0] = bp
        rb = np.zeros((L.per_chunk, L.hd, 2, L.rel, L.per_chunk), np.float32)
        for i in range(L.per_chunk):
            rb[i, :, 0, :, i] = rh.T
            rb[i, :, 1, :, i] = rw.T
        arrays |= {f"col{n}": col, f"wqkv{n}": rows(wqkv, CK), f"wp{n}": place.reshape(128, L.groups, C),
                   f"rb{n}": rb.reshape(CK, 2, L.rel, L.per_chunk), f"w1_{n}": rows(w1, CK),
                   f"w2_{n}": rows(w2, 128), f"vb{n}": bqkv[2 * L.dim:], f"b2_{n}": b2,
                   f"kc{n}": key_constants(L)}
    arrays["qm"] = query_masks()
    arrays["idn"] = np.eye(128, dtype=np.float32)
    arrays["eps"] = np.tile(np.array([1e-5, 1e-6], np.float32), (128, 1))
    arrays["fwd"], arrays["inv"] = fourier()
    per = CK // BS
    ws = np.zeros((per, BS, 2, 2, 2, per, BS), np.float32)
    for layer, name in enumerate(("w1", "w2")):
        w = f("L3_conv_" + name).reshape(2, 2, per, BS, BS)
        for i in range(per):
            ws[i, :, layer, :, :, i] = w[:, :, i].transpose(2, 1, 0, 3)
    arrays["ws"] = ws.reshape(CK, 2, 2, 2, CK)
    arrays["sb1"] = f("L3_conv_b1").reshape(2, 2, CK).transpose(2, 1, 0)
    arrays["sb2"] = f("L3_conv_b2").reshape(2, 2, CK).transpose(1, 0, 2)
    return {k: np.ascontiguousarray(v) for k, v in arrays.items()}


def kernel(**inputs):
    import concourse.bacc as _bacc
    from concourse.bass_utils import run_bass_kernel_spmd as _run

    nc = _bacc.Bacc("TRN2", target_bir_lowering=False, num_devices=1)
    arrays = _pack(inputs)
    io = {k: nc.dram_tensor(f"in_{k}", v.shape, F32, kind="ExternalInput").ap() for k, v in arrays.items()}
    io["inverses"] = nc.dram_tensor("inverses", (HEADS, NT), F32).ap()
    out = nc.dram_tensor("out_y", (NT, C), F32, kind="ExternalOutput").ap()
    build(nc, io, out)
    r = _run(nc, [{f"in_{k}": v for k, v in arrays.items()}], core_ids=[0])
    return r.results[0]["out_y"].reshape(NB, IMG, IMG, C)
```

```python
from contextlib import ExitStack

import numpy as np
import concourse.bass as bass
from concourse import mybir

F32 = mybir.dt.float32
F32R = mybir.dt.float32r
ALU = mybir.AluOpType
ACT = mybir.ActivationFunctionType
AX = mybir.AxisListType

NB, IMG, C = 4, 16, 192
TOK = IMG * IMG
NT = NB * TOK
TILES = NT // 128
CK = C // 2
HEADS, HALF = 12, 6
FF = 4 * C
FM = FF // 128
BIG = 1e30
EDGE = 14
STRIP_A = NB * IMG * 2
STRIP_B = NB * 2 * EDGE
NE = STRIP_A + STRIP_B
FREQ = IMG // 2 + 1
MODES = IMG * FREQ
MT = MODES // 2
NBLK, BS = 8, C // 8
SHRINK = 0.01


class Layer:

    def __init__(self, index, head_dim, window, eps, gelu):
        self.index, self.hd, self.win, self.eps, self.gelu = index, head_dim, window, eps, gelu
        self.pads = IMG % window != 0
        self.dim = HEADS * head_dim
        self.scale = head_dim ** -0.5
        self.per_chunk = CK // head_dim
        self.chunks = HEADS // self.per_chunk
        self.slot = 32 if head_dim == 16 else 64
        self.vcol = 32 if head_dim == 16 else 49
        self.per_group = 128 // self.slot
        self.groups = HEADS // self.per_group
        self.rel = 2 * window - 1
        self.npad = window * window if self.pads else 0
        self.pad_cols = TOK if self.pads else 0
        self.keys = NT + self.pad_cols
        self.pc = self.npad // 2
        self.tiles = 1 if head_dim == 16 else 2
        self.ring = 6 if head_dim == 16 else 4
        parts = 2 if self.tiles == 1 else 1
        self.rel_row = 3 * head_dim if self.tiles == 1 else head_dim
        self.mask_row = self.rel_row + 2 * parts * window
        self.max_row = self.mask_row + (5 if self.pads else 0)
        self.rows = self.max_row + 2
        self.depth = (self.rows,) if self.tiles == 1 else (2 * head_dim + 2 * window, self.rows)
        self.aug_dmas = 5 if self.tiles == 1 else 6
        self.score_banks, self.unit_banks = ((2, 3, 4), (5,)) if self.tiles == 1 else ((2, 3), (4, 5))
        self.units = 5 if self.pads else 4
        self.per_pair = 4 if self.tiles == 1 else 8


LAYERS = [Layer(0, 16, 14, 1e-5, ACT.Gelu), Layer(1, 48, 16, 1e-5, ACT.Gelu_apprx_tanh),
          Layer(2, 16, 14, 1e-6, ACT.Gelu)]


def key_constants(L):
    w, parts = L.win, 2 if L.tiles == 1 else 1
    n = TOK + L.pad_cols
    hot = np.zeros((w, parts, 2, n), np.float32)
    masks = np.zeros((5 if L.pads else 0, n), np.float32)
    ones = np.ones((2, n), np.float32)
    for kh in range(IMG):
        for kw in range(IMG):
            j = kh * IMG + kw
            hot[w - 1 - kh % w, :, 0, j] = 1
            hot[w - 1 - kw % w, :, 1, j] = 1
            if L.pads:
                masks[kh // w, j] = 1
                masks[2 + kw // w, j] = 1
    for p in range(L.npad):
        kh, kw = divmod(p, w)
        j = TOK + p
        hot[w - 1 - kh, :, 0, j] = 1
        hot[w - 1 - kw, :, 1, j] = 1
        real_h, real_w = kh < IMG - w, kw < IMG - w
        if real_h and real_w:
            masks[0, j] = masks[1, j] = 1
        elif real_h:
            masks[3, j] = 1
        elif real_w:
            masks[1, j] = 1
        else:
            masks[4, j] = 1
    if L.tiles == 2:
        hot = hot.transpose(2, 0, 1, 3)
    return np.ascontiguousarray(np.concatenate([hot.reshape(-1, n), masks, ones]))


def query_masks():
    m = np.zeros((5, IMG, IMG), np.float32)
    low = np.arange(IMG) < EDGE
    m[0, ~low, :] = -BIG
    m[1, low, :] = -BIG
    m[2, :, ~low] = -BIG
    m[3, :, low] = -BIG
    m[4, :EDGE, :EDGE] = -BIG
    return m.reshape(5, TOK)


def fourier():
    pos = np.arange(IMG)
    h, w, kh, kw = np.meshgrid(pos, pos, pos, np.arange(FREQ), indexing="ij")
    ang = 2 * np.pi * ((h * kh + w * kw) % IMG) / IMG
    cos, sin = np.cos(ang).reshape(TOK, MODES) / IMG, np.sin(ang).reshape(TOK, MODES) / IMG
    weight = np.tile(np.where((np.arange(FREQ) == 0) | (np.arange(FREQ) == FREQ - 1), 1.0, 2.0), IMG)
    fwd = np.concatenate([cos, -sin], 1)
    inv = np.stack([(cos * weight).T, (-sin * weight).T])
    fwd = fwd.reshape(2, 128, 2 * MODES).transpose(1, 0, 2)
    inv = inv.reshape(2, 2, MT, TOK).transpose(2, 1, 0, 3)
    return np.ascontiguousarray(fwd, np.float32), np.ascontiguousarray(inv, np.float32)


class Count:

    def __init__(self, nc, ctx, name, per_layer, step=1):
        self.sem = ctx.enter_context(nc.semaphore(name))
        self.base = [sum(per_layer[:i]) for i in range(len(per_layer) + 1)]
        self.step = step

    def at(self, layer, i):
        return self.sem, self.step * (self.base[layer] + i + 1)


SLOTS = max(L.ring for L in LAYERS)
MAX_BANK, TR_BANK, O_BANK = (0, 1), 5, (6, 7)


def alternate(main, extra):
    taken = 0
    for i, step in enumerate(main):
        yield step, False
        while taken * len(main) < (i + 1) * len(extra):
            yield extra[taken], True
            taken += 1


def spread(main, extra):
    return [step for step, _ in alternate(main, extra)] if main else extra


def attention_steps(L):
    n = L.index
    out = []

    def chunk_units(c):
        return [(kind, c, u) for kind in ("q", "k", "rh", "rw") for u in range(2)]

    if n == 0:
        out += [("ln", 0, 0, 0), ("turn", 0, 0, 0), ("ln", 0, 1, 0)]
    upfront = L.tiles
    early = [("q", 0, 0), ("k", 0, 0)]
    out += [(*unit, 4 + k) for k, unit in enumerate(early)]
    out.append(("turn", 0, 1, 2))
    out += [(*unit, k % 4) for k, unit in enumerate(u for u in chunk_units(0) if u not in early)]
    out += [("aug", h, 0, 0) for h in range(L.per_chunk)]
    out += [("v", t, 0, 4 + 2 * (t % 2)) for t in range(TILES)]
    units = [unit for c in range(1, L.chunks) for unit in chunk_units(c)]
    beside = [(*unit, 2 + k % 2) for k, unit in enumerate(units[:4 * L.tiles])]
    units = units[4 * L.tiles:]
    out += beside[:2 * L.tiles]
    out += [("max", 0, k, 0) for k in range(4)] + [("max", 1, 0, 0), ("maxT", 0, 0, 0)]
    out += [("max", 1, k, 0) for k in range(1, 4)] + [beside[2 * L.tiles], ("maxT", 1, 0, 0)]
    out += beside[2 * L.tiles + 1:]
    if L.tiles == 2:
        out += [("aug", h, 0, 0) for h in range(L.per_chunk, 2 * L.per_chunk)]
    waiting = list(range(upfront * L.per_chunk, HEADS))
    ready, scored = upfront * L.per_chunk, 0

    def lay_out_heads():
        while waiting and waiting[0] < ready and waiting[0] - L.ring < scored:
            out.append(("aug", waiting.pop(0), 0, 0))

    finished = []
    for h in range(0, HEADS, 2):
        main = [("scores", a, k, 0) for a in (h, h + 1) for k in range(L.units)]
        main += [("pv", h, k, 0) for k in range(L.units if L.pads else NB)]
        maxima = []
        if h + 2 < HEADS:
            maxima = [("max", a, k, 0) for a in (h + 2, h + 3) for k in range(4)] + [("maxT", h + 3, 0, 0)]
            maxima.insert(5, ("maxT", h + 2, 0, 0))
        mine, units = units[:L.per_pair], units[L.per_pair:]
        extra = [(*unit, L.unit_banks[k % len(L.unit_banks)]) for k, unit in enumerate(mine)]
        first = L.tiles - 1 if h else 4
        fill = extra[:first] + spread(maxima[:6], extra[first:]) + maxima[6:]
        for k, part in enumerate(finished):
            fill.insert(min(1 + 3 * k, len(fill)), part)
        for step, filled in alternate(main, fill):
            if not filled:
                out.append(step)
                if step[0] == "scores" and step[2] == L.units - 1:
                    scored = step[1] + 1
                    lay_out_heads()
            else:
                out.append(step)
                if step[0] == "rw" and step[2] == 1:
                    ready = (step[1] + 1) * L.per_chunk
                    lay_out_heads()
        if (h + 2) % L.per_group == 0:
            g = h // L.per_group
            out.append(("copy_o", g, 0, 0))
            out.append(("sums", g, 0, 0))
            finished = [("inverse", g, 0, 0), ("divide", g, 0, 0)]
        else:
            finished = []
    out += finished
    assert not units and not waiting
    out += [("proj", t, 0, t) for t in range(TILES)]
    out += [("proj", t, 1, t) for t in range(4)] + [("ln", 1, 0, 0)]
    out += [("proj", t, 1, t) for t in range(4, TILES)] + [("turn", 1, 0, 0), ("ln", 1, 1, 0)]
    out += [("up", m, 0, 4 + m) for m in range(2)] + [("turn", 1, 1, 2)]
    out += [("gelu", m, 0, 4 + m) for m in range(2)]
    out += [(step, m, 0, (m + 2) % 4) for m in range(2, FM) for step in ("up", "gelu")]
    out += [("down", t, 0, 4 + t % 4) for t in range(4)]
    out += [(step, m, 1, m % 4) for m in range(FM) for step in ("up", "gelu")]
    down = [("down", t, 0, 4 + t % 4) for t in range(4, TILES)]
    if n + 1 < len(LAYERS):
        out += [("next_ln", 0, 0, 0), *down[:3], ("next_turn", 0, 0, 0), down[3], ("next_ln", 0, 1, 0)]
    else:
        out += down
    return out


def all_steps():
    for L in LAYERS:
        for step, i, u, bank in attention_steps(L):
            if step in ("next_ln", "next_turn"):
                yield LAYERS[L.index + 1], step[5:], i, u, bank
            else:
                yield L, step, i, u, bank


def build(nc, io, out):
    with ExitStack() as ctx:
        _build(nc, ctx, io, out)


def _build(nc, ctx, io, out):
    def sb(where, name, shape, dt=F32):
        return where.enter_context(nc.sbuf_tensor(name, shape, dt))

    def count(name, per_layer, step=1):
        return Count(nc, ctx, name, per_layer, step)

    X = sb(ctx, "X", [128, TILES, C])
    XNOS = sb(ctx, "XNOS", [128, TILES * C])
    XN = XNOS[:, :].rearrange("p (t c) -> p t c", t=TILES)
    OS = XNOS[:, 0:NT].rearrange("p (k t) -> p k t", k=2)
    XT = sb(ctx, "XT", [CK, 2, NT])
    IDN = sb(ctx, "IDN", [128, 128])
    STAT = sb(ctx, "STAT", [128, TILES, 6])
    MV = sb(ctx, "MV", [128, TILES, 2])
    STD = sb(ctx, "STD", [128, TILES])
    RSTD = sb(ctx, "RSTD", [128, TILES])
    EPS = sb(ctx, "EPS", [128, 2])
    WQKV = sb(ctx, "WQKV", [CK, 2, 3 * max(L.dim for L in LAYERS)])
    COL = [sb(ctx, f"COL{L.index}", [128, 8 + 2 * L.chunks + FM]) for L in LAYERS]
    SKB = [sb(ctx, f"SKB{L.index}", [CK, L.chunks]) for L in LAYERS]
    VB = [sb(ctx, f"VB{L.index}", [128, L.dim]) for L in LAYERS]
    B2 = [sb(ctx, f"B2_{L.index}", [128, C]) for L in LAYERS]
    RB = [sb(ctx, f"RB{L.index}", [CK, 2, L.rel, L.per_chunk]) for L in LAYERS]
    PS = ctx.enter_context(nc.psum_tensor("PS", [128, 8, 512], F32))

    mem = []
    for L in LAYERS:
        n = L.index
        m = {}
        frame = ExitStack()
        m["WP"] = sb(frame, f"WP{n}", [128, L.groups, C])
        attn = ExitStack()
        m["QA"] = sb(attn, f"QA{n}", [max(L.depth), L.tiles, L.ring, NT], F32R)
        m["KA"] = sb(attn, f"KA{n}", [max(L.depth), L.tiles, L.ring, L.keys], F32R)
        m["q"] = sb(attn, f"QD{n}", [CK, NT])
        m["k"] = sb(attn, f"KD{n}", [CK, L.keys])
        m["QHL"] = sb(attn, f"QHL{n}", [CK, 2, NT], F32R)
        m["KHL"] = sb(attn, f"KHL{n}", [CK, 2, L.keys], F32R)
        rw = L.per_chunk * L.win
        m["REL"] = sb(attn, f"REL{n}", [rw, 2, 2, NT] if L.tiles == 1 else [2 * rw, 2, NT], F32R)
        m["KC32"] = sb(attn, f"KC32_{n}", [L.rows - L.rel_row, TOK + L.pad_cols])
        m["KC"] = sb(attn, f"KC{n}", [L.rows - L.rel_row, TOK + L.pad_cols], F32R)
        if L.pads:
            m["QM32"] = sb(attn, f"QM32_{n}", [5, TOK])
            m["QM"] = sb(attn, f"QM{n}", [5, TOK], F32R)
            m["BV"] = sb(attn, f"BV{n}", [L.pc, HEADS, L.slot])
            m["PP"] = sb(attn, f"PP{n}", [L.pc, 2, 2, NE])
        m["NRH"] = sb(attn, f"NRH{n}", [TILES, 2, 128], F32R)
        m["NRL"] = sb(attn, f"NRL{n}", [TILES, 2, 128], F32R)
        m["V"] = sb(attn, f"V{n}", [128, TILES, HEADS * L.vcol + L.slot - L.vcol])
        m["OT"] = sb(attn, f"OT{n}", [128, L.groups, NT])
        m["SUMS"] = sb(attn, f"SUMS{n}", [128, 2, L.per_group * NT // 128])
        m["PT"] = sb(attn, f"PT{n}", [128, 2, 2, NT])
        m["NM"] = sb(attn, f"NM{n}", [128, 2, TILES])
        attn.close()
        m["W1"] = sb(frame, f"W1_{n}", [CK, 2, FF])
        m["W2"] = sb(frame, f"W2_{n}", [128, FM, C])
        m["HT"] = sb(frame, f"HT{n}", [128, FM, NT])
        frame.close()
        mem.append(m)
    spectral = ExitStack()
    spectral.enter_context(nc.sbuf_tensor("under_mlp", [128, 11000], F32))
    FW = sb(spectral, "FW", [128, 2, 2 * MODES])
    GI = sb(spectral, "GI", [MT, 2, 2, TOK])
    WS = sb(spectral, "WS", [CK, 2, 2, 2, CK])
    W1N = sb(spectral, "W1N", [CK, 2, CK])
    W2S = sb(spectral, "W2S", [CK, 2, 2, 2, CK])
    SB1 = sb(spectral, "SB1", [CK, 2, 2])
    SB2 = sb(spectral, "SB2", [MT, 2, 2, CK])
    XF = sb(spectral, "XF", [CK, 2, 2, NB * MODES])
    O1 = sb(spectral, "O1", [CK, 2, 2, NB * MODES])
    O2 = sb(spectral, "O2", [MT, 2, NB, 2, 2, CK])
    SH = sb(spectral, "SH", [MT, 2, 2, 2 * C])
    Y = sb(spectral, "Y", [128, TILES, C])
    spectral.close()

    def per(f):
        return [f(L) for L in LAYERS] + [0]

    dve_step = ctx.enter_context(nc.semaphore("dve_step"))
    x_in = [count(f"x_in{half}", [1, 0, 0, 0], 16) for half in range(2)]
    first_in = count("first_in", [3, 0, 0, 0], 16)
    const_in = count("const_in", [4 * 3 - 1, 0, 0, 0], 16)
    wqkv_in = count("wqkv_in", [1, 1, 1, 0], 16)
    wp_in = count("wp_in", [1, 1, 1, 0], 16)
    mlp_in = count("mlp_in", [2, 2, 2, 0], 16)
    masks_in = count("masks_in", per(lambda L: 2 if L.pads else 1), 16)
    spectral_in = count("spectral_in", [0, 0, 0, 5], 16)
    const_rows = per(lambda L: L.ring * (3 if L.pads else 2))
    aug_const = count("aug_const", const_rows, 16)
    masks_cast = count("masks_cast", per(lambda L: 2 if L.pads else 1))
    v_ones = count("v_ones", [1, 1, 1, 0])
    pad_values = count("pad_values", per(lambda L: 1 if L.pads else 0))
    pad_keys = count("pad_keys", per(lambda L: L.chunks if L.pads else 0))
    skb_done = count("skb_done", [1, 1, 1, 0])
    mean_var = count("mean_var", [4, 4, 4, 0])
    std_done = count("std_done", [4, 4, 4, 0])
    xn_done = count("xn_done", [2 * TILES] * 3 + [0])
    xt_psum = count("xt_psum", [8, 8, 8, 0])
    xt_done = count("xt_done", [8, 8, 8, 0])
    v_psum = count("v_psum", [TILES] * 3 + [0])
    v_done = count("v_done", [TILES] * 3 + [0])
    two = per(lambda L: 2 * L.chunks)
    psum_of = {kind: count(kind + "_psum", two) for kind in ("q", "k", "rh", "rw")}
    q_done, k_done = count("q_done", two), count("k_done", two)
    rh_done, rw_done = count("rh_done", two), count("rw_done", two)
    rh_hi_done, rw_hi_done = count("rh_hi_done", two), count("rw_hi_done", two)
    split_hi, split_lo = count("split_hi", two), count("split_lo", two)
    aug_in = [count(f"aug_in{r}", per(lambda L: L.aug_dmas * len(range(r, HEADS, L.ring)) * (r < L.ring)), 16)
              for r in range(SLOTS)]
    max_psum = count("max_psum", [HEADS * TILES] * 3 + [0])
    max_done = count("max_done", [HEADS * TILES] * 3 + [0])
    maxT_psum = count("maxT_psum", [HEADS] * 3 + [0])
    maxT_hi_done = count("maxT_hi_done", [HEADS] * 3 + [0])
    maxT_done = count("maxT_done", [HEADS] * 3 + [0])
    max_row_in = [count(f"max_row_in{p}", [HEADS] * 3 + [0], 16)
                  for p in (0, 1)]
    scores_psum = count("scores_psum", per(lambda L: HEADS * L.units))
    probs_done = count("probs_done", per(lambda L: HEADS * L.units))
    pv_done = count("pv_done", per(lambda L: HEADS // 2 * L.units))
    o_copied = count("o_copied", per(lambda L: 2 * L.groups))
    one_group = per(lambda L: L.groups)
    sums_in, inv_stored, inv_in = (count(x, one_group, 16) for x in ("sums_in", "inv_stored", "inv_in"))
    sums_inv = count("sums_inv", one_group)
    o_done = count("o_done", per(lambda L: 2 * L.groups))
    proj_psum = count("proj_psum", [TILES] * 3 + [0])
    x_mid = count("x_mid", [TILES] * 3 + [0])
    x_biased = count("x_biased", [2] * 3 + [0])
    up_psum = count("up_psum", [2 * FM] * 3 + [0])
    gelu_done = count("gelu_done", [2 * FM] * 3 + [0])
    down_psum = count("down_psum", [TILES] * 3 + [0])
    x_end = count("x_end", [TILES] * 3 + [0])
    w_prep = count("w_prep", [0, 0, 0, 3])
    fwd_psum, fwd_done = count("fwd_psum", [0, 0, 0, 8]), count("fwd_done", [0, 0, 0, 4])
    fwd_done_odd = count("fwd_done_odd", [0, 0, 0, 4])
    s1_psum, s1_done = count("s1_psum", [0, 0, 0, 8]), count("s1_done", [0, 0, 0, 8])
    s2_psum, s2_biased = count("s2_psum", [0, 0, 0, 8]), count("s2_biased", [0, 0, 0, 8])
    s2_clamped, s2_done = count("s2_clamped", [0, 0, 0, 8]), count("s2_done", [0, 0, 0, 8])
    inv_psum = count("inv_psum", [0, 0, 0, TILES])
    y_done = count("y_done", [0, 0, 0, TILES])
    y_out = count("y_out", [0, 0, 0, 2], 16)

    def aug_at(L, h):
        return aug_in[h % L.ring].at(L.index, (h // L.ring + 1) * L.aug_dmas - 1)

    def max_row_at(L, h):
        return max_row_in[h % 2].at(L.index, (h // 2 + 1) * 2 - 1)

    def chunk_read(L, c):
        return [aug_at(L, h) for h in range(c * L.per_chunk, (c + 1) * L.per_chunk)]

    def inverses(L, g):
        return io["inverses"][g * L.per_group:(g + 1) * L.per_group, :]

    def values(L, t, h):
        return mem[L.index]["V"][:, t, h * L.vcol:h * L.vcol + L.slot]

    def image(ap):
        return ap.rearrange("r (b y x) -> r b y x", b=NB, y=IMG)

    def rel_views(L, m, step, c, u, bank, low):
        axis, rows = int(step == "rw"), L.per_chunk * L.win
        if L.tiles == 1:
            tile, p = m["REL"][:, low, axis, :], slice(0, rows)
        else:
            p = slice(axis * rows, (axis + 1) * rows)
            tile = m["REL"][p, low, :]
        part = slice(8 * u, 8 * u + 8)
        if step == "rh":
            return image(tile)[:, :, part, :], PS[p, bank, :].rearrange("r (y b x) -> r b y x", b=NB, y=8)
        return image(tile)[:, :, :, part], PS[p, bank, :].rearrange("r (x b y) -> r b y x", b=NB, x=8)

    def raw(ap):
        return ap.bitcast(F32) if ap.dtype == F32R else ap

    block = ctx.enter_context(nc.Block())

    @block.sync
    def _(sp):
        for tiles in (slice(0, TILES // 2), slice(TILES // 2, TILES)):
            sp.dma_start(X[:, tiles, :], io["x"].rearrange("(t p) c -> p t c", p=128)[:, tiles, :])\
                .then_inc(x_in[tiles.start > 0].sem, 16)
        for dst, src in ((IDN[:, :], io["idn"]), (EPS[:, :], io["eps"]), (COL[0][:, :], io["col0"])):
            sp.dma_start(dst, src).then_inc(first_in.sem, 16)

        def load_wqkv(n):
            sp.dma_start(WQKV[:, :, 0:3 * LAYERS[n].dim], io[f"wqkv{n}"]).then_inc(wqkv_in.sem, 16)

        def load_attention(L):
            n, m = L.index, mem[L.index]
            rows = L.rows - L.rel_row
            sp.dma_start(m["KC32"][:, :], io[f"kc{n}"]).then_inc(masks_in.sem, 16)
            if L.pads:
                sp.dma_start(m["QM32"][:, :], io["qm"]).then_inc(masks_in.sem, 16)
            if n:
                sp.wait_ge(*x_end.at(n - 1, TILES - 1))
            sp.dma_start(m["WP"][:, :, :], io[f"wp{n}"]).then_inc(wp_in.sem, 16)
            sp.wait_ge(*masks_cast.at(n, 1 if L.pads else 0))
            ksrc = raw(m["KC"][:, :])
            places = [(L.tiles - 1, L.rel_row, rows)] + ([(0, 2 * L.hd, 2 * L.win)] if L.tiles == 2 else [])
            for s in range(L.ring):
                for tile, row, size in places:
                    kdst = raw(m["KA"][row:row + size, tile, s, :])
                    sp.dma_start(kdst[:, 0:NT].rearrange("r (b t) -> r b t", b=NB),
                                 ksrc[0:size, 0:TOK].unsqueeze(1).broadcast_to([size, NB, TOK]))\
                        .then_inc(aug_const.sem, 16)
                if L.pads:
                    sp.dma_start(kdst[:, NT:], ksrc[:, TOK:]).then_inc(aug_const.sem, 16)
                    sp.dma_start(raw(m["QA"][L.mask_row:L.max_row, 0, s, :]).rearrange("r (b t) -> r b t", b=NB),
                                 raw(m["QM"][:, :]).unsqueeze(1).broadcast_to([5, NB, TOK]))\
                        .then_inc(aug_const.sem, 16)

        load_wqkv(0)
        for L in LAYERS:
            n = L.index
            for dst, src in ((RB[n][:, :, :, :], io[f"rb{n}"]), (VB[n][:, :], io[f"vb{n}"].partition_broadcast(128)),
                             (B2[n][:, :], io[f"b2_{n}"].partition_broadcast(128)),
                             (COL[n][:, :], io[f"col{n}"]))[:3 if n == 0 else 4]:
                sp.dma_start(dst, src).then_inc(const_in.sem, 16)
        load_attention(LAYERS[0])
        for L, step, h, u, bank in all_steps():
            n, m = L.index, mem[L.index]
            if step == "aug":
                s, c, i = h % L.ring, h // L.per_chunk, h % L.per_chunk
                if h >= L.ring:
                    sp.wait_ge(*scores_psum.at(n, L.units * (h - L.ring + 1) - 1))
                elif n:
                    sp.wait_ge(*x_end.at(n - 1, TILES - 1))
                hd, end = L.hd, L.tiles - 1
                mine = slice(i * hd, (i + 1) * hd)
                again = slice(2 * hd, 3 * hd) if end == 0 else slice(0, hd)
                sp.wait_ge(*split_lo.at(n, 2 * c))
                for dst, src in ((m["QA"][0:2 * hd, 0, s, :], m["QHL"][mine, :, :]),
                                 (m["QA"][again, end, s, :], m["QHL"][mine, 0, :])):
                    sp.dma_start(raw(dst), raw(src)).then_inc(aug_in[s].sem, 16)
                sp.wait_ge(*split_lo.at(n, 2 * c + 1))
                twice = m["KHL"][mine, 0, :].unsqueeze(1).broadcast_to([hd, 2, L.keys])
                for dst, src in ((m["KA"][0:2 * hd, 0, s, :], twice),
                                 (m["KA"][again, end, s, :], m["KHL"][mine, 1, :])):
                    sp.dma_start(raw(dst), raw(src)).then_inc(aug_in[s].sem, 16)
                sp.wait_ge(*rh_done.at(n, 2 * c + 1))
                sp.wait_ge(*rw_done.at(n, 2 * c + 1))
                if end == 0:
                    moves = [(m["QA"][L.rel_row:L.mask_row, 0, s, :],
                              m["REL"][i::L.per_chunk, :, :, :].rearrange("r a b t -> r (a b) t"))]
                else:
                    moves = [(m["QA"][2 * hd:2 * hd + 2 * L.win, 0, s, :], m["REL"][i::L.per_chunk, 0, :]),
                             (m["QA"][L.rel_row:L.mask_row, 1, s, :], m["REL"][i::L.per_chunk, 1, :])]
                for dst, src in moves:
                    sp.dma_start(raw(dst), raw(src)).then_inc(aug_in[s].sem, 16)
            elif step == "maxT":
                s, p = h % L.ring, h % 2
                sp.wait_ge(*maxT_done.at(n, h))
                for r, part in enumerate((m["NRH"], m["NRL"])):
                    sp.dma_start(raw(m["QA"][L.max_row + r:L.max_row + r + 1, L.tiles - 1, s, :]), raw(part[:, p, :]))\
                        .then_inc(max_row_in[p].sem, 16)
            elif step == "sums":
                sp.wait_ge(*o_copied.at(n, 2 * h + 1))
                if h:
                    sp.wait_ge(*sums_inv.at(n, h - 1))
                sp.dma_start(m["SUMS"][:, 0, :], OS[L.hd::L.slot, :, :]).then_inc(sums_in.sem, 16)
            elif step == "inverse":
                sp.wait_ge(*sums_inv.at(n, h))
                sp.dma_start(inverses(L, h).rearrange("g (p c) -> (g p) c", p=L.slot), m["SUMS"][:, 1, :])\
                    .then_inc(inv_stored.sem, 16)
            elif step == "divide":
                sp.wait_ge(*inv_stored.at(n, h))
                sp.dma_start(m["OT"][:, h, :], inverses(L, h).unsqueeze(1).broadcast_to([L.per_group, L.slot, NT]))\
                    .then_inc(inv_in.sem, 16)
            elif step == "proj" and h == 0 and u == 0:
                sp.wait_ge(*scores_psum.at(n, L.units * HEADS - 1))
                sp.dma_start(m["W1"][:, :, :], io[f"w1_{n}"]).then_inc(mlp_in.sem, 16)
                sp.dma_start(m["W2"][:, :, :], io[f"w2_{n}"]).then_inc(mlp_in.sem, 16)
                if n + 1 < len(LAYERS):
                    sp.wait_ge(*rw_done.at(n, 2 * L.chunks - 1))
                    load_wqkv(n + 1)
            elif step == "ln" and h == 1 and u == 1:
                sp.wait_ge(*x_mid.at(n, TILES - 1))
                if n + 1 == len(LAYERS):
                    for dst, src in ((FW[:, :, :], io["fwd"]), (GI[:, :, :, :], io["inv"]),
                                     (WS[:, :, :, :, :], io["ws"]), (SB1[:, :, :], io["sb1"]),
                                     (SB2[:, :, :, :], io["sb2"].partition_broadcast(MT))):
                        sp.dma_start(dst, src).then_inc(spectral_in.sem, 16)
            elif step == "up" and h == FM - 1 and u == 1 and n + 1 < len(LAYERS):
                load_attention(LAYERS[n + 1])
        for half in range(2):
            t = TILES // 2
            sp.wait_ge(*y_done.at(3, (half + 1) * t - 1))
            sp.dma_start(out[half * t * 128:(half + 1) * t * 128, :].rearrange("(t p) c -> p t c", p=128),
                         Y[:, half * t:(half + 1) * t, :]).then_inc(y_out.sem, 16)
        sp.wait_ge(*y_out.at(3, 1))

    @block.gpsimd
    def _(pool):
        def prepare(L):
            n, m = L.index, mem[L.index]
            if n:
                pool.wait_ge(*x_mid.at(n - 1, TILES - 1))
            v = m["V"][:, :, 0:HEADS * L.vcol].rearrange("p t (h d) -> p t h d", h=HEADS)
            for t in range(TILES):
                if L.vcol > L.hd + 1:
                    nc.gpsimd.memset(v[:, t, :, L.hd + 1:], 0.0)
                if L.slot > L.vcol:
                    nc.gpsimd.memset(m["V"][:, t, HEADS * L.vcol:], 0.0)
                ins = nc.gpsimd.memset(v[:, t, :, L.hd:L.hd + 1], 1.0)
            ins.then_inc(v_ones.sem, 1)
            if L.pads:
                pool.wait_ge(*const_in.at(0, 10))
                nc.gpsimd.memset(m["BV"][:, :, L.hd + 1:], 0.0)
                nc.gpsimd.memset(m["BV"][:, :, L.hd:L.hd + 1], 1.0)
                nc.gpsimd.tensor_copy(m["BV"][:, :, 0:L.hd],
                                      VB[n][0:L.pc, :].rearrange("p (h d) -> p h d", h=HEADS))\
                    .then_inc(pad_values.sem, 1)
            pool.wait_ge(*masks_in.at(n, 1 if L.pads else 0))
            nc.gpsimd.tensor_copy(m["KC"][:, :], m["KC32"][:, :]).then_inc(masks_cast.sem, 1)
            if L.pads:
                nc.gpsimd.tensor_copy(m["QM"][:, :], m["QM32"][:, :]).then_inc(masks_cast.sem, 1)

        prepare(LAYERS[0])
        for L, step, i, u, bank in all_steps():
            n, m = L.index, mem[L.index]
            if step in ("q", "k") and u == 1:
                part, done = (m["QHL"], q_done) if step == "q" else (m["KHL"], k_done)
                at = 2 * i + (step == "k")
                if i:
                    for wait in chunk_read(L, i - 1):
                        pool.wait_ge(*wait)
                pool.wait_ge(*done.at(n, 2 * i + 1))
                if step == "k" and L.pads:
                    pool.wait_ge(*pad_keys.at(n, i))
                src = m[step][:, :]
                nc.gpsimd.tensor_copy(part[:, 0, :], src).then_inc(split_hi.sem, 1)
                pool.wait_ge(*split_hi.at(n, at))
                nc.gpsimd.tensor_tensor(part[:, 1, :], src, part[:, 0, :].bitcast(F32), ALU.subtract)\
                    .then_inc(split_lo.sem, 1)
            elif step == "divide":
                pool.wait_ge(*inv_in.at(n, i))
                for k in range(2):
                    o = m["OT"][:, i, k * 512:(k + 1) * 512]
                    nc.gpsimd.tensor_tensor(o, OS[:, k, :], o, ALU.mult).then_inc(o_done.sem, 1)
            elif step == "ln" and i == 1:
                pool.wait_ge(*xn_done.at(n, TILES + 4 * u + 3))
                for t in range(4 * u, 4 * u + 4):
                    ins = nc.gpsimd.tensor_tensor(X[:, t, :], X[:, t, :], B2[n][:, :], ALU.add)
                ins.then_inc(x_biased.sem, 1)
            elif step == "down" and i == 0 and n + 1 < len(LAYERS):
                prepare(LAYERS[n + 1])
        pool.wait_ge(*spectral_in.at(3, 4))
        nc.gpsimd.tensor_scalar(W1N[:, :, :], WS[:, 0, :, 1, :], -1.0, None, ALU.mult).then_inc(w_prep.sem, 1)
        nc.gpsimd.tensor_copy(W2S[:, :, 0, :, :], WS[:, 1, :, :, :])
        nc.gpsimd.tensor_copy(W2S[:, :, 1, 1, :], WS[:, 1, :, 0, :]).then_inc(w_prep.sem, 1)
        nc.gpsimd.tensor_scalar(W2S[:, :, 1, 0, :], WS[:, 1, :, 1, :], -1.0, None, ALU.mult).then_inc(w_prep.sem, 1)
        for u in range(8):
            pool.wait_ge(*s2_biased.at(3, u))
            if u >= 2:
                pool.wait_ge(*s2_done.at(3, u - 2))
            nc.gpsimd.tensor_scalar(SH[:, 1, u % 2, :], SH[:, 0, u % 2, :], SHRINK, -SHRINK, ALU.min, ALU.max)\
                .then_inc(s2_clamped.sem, 1)

    @block.scalar
    def _(act):
        act.wait_ge(*first_in.at(0, 2))
        for L, step, i, u, bank in all_steps():
            n, m = L.index, mem[L.index]
            if step == "ln":
                s, tiles = i, slice(4 * u, 4 * u + 4)
                e = 1 if L.eps == 1e-6 else 0
                act.wait_ge(*mean_var.at(n, 2 * s + u))
                nc.scalar.activation(STD[:, tiles], MV[:, tiles, 1], ACT.Sqrt, bias=EPS[:, e:e + 1])\
                    .then_inc(std_done.sem, 1)
            elif step == "turn":
                s = i
                g = COL[n][0:CK, 4 * s:4 * s + 4]
                for k in range(2):
                    act.wait_ge(*xt_psum.at(n, 4 * s + 2 * u + k))
                    nc.scalar.activation(XT[:, k, u * 512:(u + 1) * 512], PS[0:CK, bank + k, :], ACT.Identity,
                                         scale=g[:, k:k + 1], bias=g[:, 2 + k:3 + k]).then_inc(xt_done.sem, 1)
            elif step in ("q", "k"):
                if i and u == 0:
                    act.wait_ge(*psum_of["rw"].at(n, 2 * (i - 1) + 1))
                    act.wait_ge(*split_lo.at(n, 2 * (i - 1) + 1))
                act.wait_ge(*psum_of[step].at(n, 2 * i + u))
                dst = m[step][:, u * 512:(u + 1) * 512]
                if step == "q":
                    nc.scalar.activation(dst, PS[0:CK, bank, :], ACT.Identity, bias=COL[n][0:CK, 8 + i:9 + i])\
                        .then_inc(q_done.sem, 1)
                else:
                    if i == 0 and u == 0:
                        act.wait_ge(*skb_done.at(n, 0))
                    nc.scalar.activation(dst, PS[0:CK, bank, :], ACT.Identity, bias=SKB[n][:, i:i + 1],
                                         scale=L.scale).then_inc(k_done.sem, 1)
            elif step in ("rh", "rw"):
                act.wait_ge(*psum_of[step].at(n, 2 * i + u))
                if i and u == 0:
                    for wait in chunk_read(L, i - 1):
                        act.wait_ge(*wait)
                dst, src = rel_views(L, m, step, i, u, bank, 0)
                nc.scalar.activation(dst, src, ACT.Copy)\
                    .then_inc((rh_hi_done if step == "rh" else rw_hi_done).sem, 1)
            elif step == "scores":
                h, k = i, u
                if h >= 2:
                    act.wait_ge(*pv_done.at(n, L.units * (h // 2 - 1) + (2 * (k // 2) + 1 if k < 4 else 4)))
                j = L.units * h + k
                act.wait_ge(*scores_psum.at(n, j))
                if k < 4:
                    dst, src = m["PT"][:, h % 2, k % 2, (k // 2) * 512:(k // 2 + 1) * 512], \
                        PS[:, L.score_banks[j % len(L.score_banks)], :]
                else:
                    dst, src = m["PP"][:, h % 2, :, :], PS[0:L.pc, L.score_banks[j % len(L.score_banks)], 0:2 * NE]
                nc.scalar.activation(dst, src, ACT.Exp).then_inc(probs_done.sem, 1)
            elif step == "copy_o":
                act.wait_ge(*pv_done.at(n, (i + 1) * L.per_group // 2 * L.units - 1))
                if i:
                    act.wait_ge(*o_done.at(n, 2 * i - 1))
                for k in range(2):
                    nc.scalar.activation(OS[:, k, :], PS[:, O_BANK[k], :], ACT.Copy).then_inc(o_copied.sem, 1)
            elif step == "gelu":
                j = FM * u + i
                act.wait_ge(*up_psum.at(n, j))
                b1 = 8 + 2 * L.chunks + i
                nc.scalar.activation(m["HT"][:, i, u * 512:(u + 1) * 512], PS[:, bank, :], L.gelu,
                                     bias=COL[n][:, b1:b1 + 1]).then_inc(gelu_done.sem, 1)
        act.wait_ge(*spectral_in.at(3, 4))
        for u in range(0, 8, 2):
            b, cc = divmod(u, 2)
            act.wait_ge(*fwd_psum.at(3, u))
            nc.scalar.activation(XF[:, cc, :, b * MODES:(b + 1) * MODES],
                                 PS[0:CK, u, 0:2 * MODES].rearrange("p (r m) -> p r m", r=2), ACT.Copy)\
                .then_inc(fwd_done.sem, 1)
        for u in range(8):
            cc, r, half = u // 4, u // 2 % 2, u % 2
            act.wait_ge(*s1_psum.at(3, u))
            nc.scalar.activation(O1[:, cc, r, half * 2 * MODES:(half + 1) * 2 * MODES], PS[0:CK, u, 0:2 * MODES],
                                 ACT.Relu, bias=SB1[:, cc, r:r + 1]).then_inc(s1_done.sem, 1)

    @block.vector
    def _(dve):
        steps = [0]

        def link(ins):
            steps[0] += 1
            ins.then_inc(dve_step, 1)
            dve.wait_ge(dve_step, steps[0])

        dve.wait_ge(*first_in.at(0, 2))
        for L, step, i, u, bank in all_steps():
            n, m = L.index, mem[L.index]
            if step == "ln":
                s, tiles = i, range(4 * u, 4 * u + 4)
                if n + s == 0:
                    dve.wait_ge(*x_in[u].at(0, 0))
                for t in tiles:
                    if s == 1:
                        dve.wait_ge(*x_mid.at(n, t))
                    elif n:
                        dve.wait_ge(*x_end.at(n - 1, t))
                    ins = nc.vector.bn_stats(STAT[:, t, :], X[:, t, :])
                link(ins)
                for t in tiles:
                    ins = nc.vector.bn_aggr(MV[:, t, :], STAT[:, t, :])
                ins.then_inc(mean_var.sem, 1)
                dve.wait_ge(*mean_var.at(n, 2 * s + u))
                dve.wait_ge(*std_done.at(n, 2 * s + u))
                link(nc.vector.reciprocal(RSTD[:, 4 * u:4 * u + 4], STD[:, 4 * u:4 * u + 4]))
                if s == 1 and u == 0:
                    dve.wait_ge(*o_done.at(n, 2 * L.groups - 1))
                if 2 * n + s:
                    last = 4 * s + 2 * u + 1 - 4
                    dve.wait_ge(*(xt_psum.at(n, last) if s else xt_psum.at(n - 1, last + 8)))
                for t in tiles:
                    nc.vector.tensor_scalar(XN[:, t, :], X[:, t, :], MV[:, t, 0:1], RSTD[:, t:t + 1],
                                            ALU.subtract, ALU.mult).then_inc(xn_done.sem, 1)
            elif step == "v":
                t = i
                if t == 0:
                    dve.wait_ge(*v_ones.at(n, 0))
                    dve.wait_ge(*const_in.at(0, 10))
                dve.wait_ge(*v_psum.at(n, t))
                nh = HEADS if L.hd == 16 else HEADS // 2
                v = m["V"][:, t, 0:HEADS * L.vcol].rearrange("p (h d) -> p h d", h=HEADS)
                for g in range(HEADS // nh):
                    ins = nc.vector.tensor_tensor(
                        v[:, g * nh:(g + 1) * nh, 0:L.hd],
                        PS[:, bank + g, 0:nh * L.hd].rearrange("p (h d) -> p h d", h=nh),
                        VB[n][:, g * nh * L.hd:(g + 1) * nh * L.hd].rearrange("p (h d) -> p h d", h=nh), ALU.add)
                ins.then_inc(v_done.sem, 1)
            elif step == "q" and i == 0 and u == 0:
                if n:
                    dve.wait_ge(*const_in.at(0, 10))
                nc.vector.tensor_scalar(SKB[n][:, :], COL[n][0:CK, 8 + L.chunks:8 + 2 * L.chunks], L.scale,
                                        None, ALU.mult).then_inc(skb_done.sem, 1)
            elif step == "k" and u == 0 and L.pads:
                if i:
                    dve.wait_ge(*split_lo.at(n, 2 * (i - 1) + 1))
                nc.vector.tensor_scalar(m["k"][:, NT:],
                                        COL[n][0:CK, 8 + L.chunks + i:9 + L.chunks + i].broadcast_to([CK, L.pad_cols]),
                                        L.scale, None, ALU.mult).then_inc(pad_keys.sem, 1)
            elif step in ("rh", "rw"):
                hi_done, done = (rh_hi_done, rh_done) if step == "rh" else (rw_hi_done, rw_done)
                dve.wait_ge(*hi_done.at(n, 2 * i + u))
                lo, src = rel_views(L, m, step, i, u, bank, 1)
                hi, _ = rel_views(L, m, step, i, u, bank, 0)
                nc.vector.tensor_tensor(lo, src, hi.bitcast(F32), ALU.subtract).then_inc(done.sem, 1)
            elif step == "max":
                h = i
                if h >= 2 and u == 0:
                    dve.wait_ge(*maxT_psum.at(n, h - 2))
                for k in range(2 * u, 2 * u + 2):
                    j = TILES * h + k
                    dve.wait_ge(*max_psum.at(n, j))
                    nc.vector.tensor_reduce(m["NM"][:, h % 2, k:k + 1], PS[:, MAX_BANK[j % 2], 0:TOK + L.npad],
                                            AX.X, ALU.max, negate=True).then_inc(max_done.sem, 1)
            elif step == "maxT":
                h = i
                dve.wait_ge(*maxT_psum.at(n, h))
                if h >= 2:
                    dve.wait_ge(*max_row_at(L, h - 2))
                src = PS[0:TILES, TR_BANK, 0:128]
                nc.vector.tensor_copy(m["NRH"][:, h % 2, :], src).then_inc(maxT_hi_done.sem, 1)
                dve.wait_ge(*maxT_hi_done.at(n, h))
                nc.vector.tensor_tensor(m["NRL"][:, h % 2, :], src, m["NRH"][:, h % 2, :].bitcast(F32),
                                        ALU.subtract).then_inc(maxT_done.sem, 1)
            elif step == "inverse":
                dve.wait_ge(*sums_in.at(n, i))
                if i:
                    dve.wait_ge(*inv_stored.at(n, i - 1))
                nc.vector.reciprocal(m["SUMS"][:, 1, :], m["SUMS"][:, 0, :]).then_inc(sums_inv.sem, 1)
            elif step == "proj" and u == 1:
                dve.wait_ge(*proj_psum.at(n, i))
                nc.vector.tensor_tensor(X[:, i, :], X[:, i, :], PS[:, bank, 0:C], ALU.add).then_inc(x_mid.sem, 1)
            elif step == "down":
                if i % 4 == 0:
                    dve.wait_ge(*x_biased.at(n, i // 4))
                dve.wait_ge(*down_psum.at(n, i))
                nc.vector.tensor_tensor(X[:, i, :], X[:, i, :], PS[:, bank, 0:C], ALU.add).then_inc(x_end.sem, 1)
        for u in range(1, 8, 2):
            b, cc = divmod(u, 2)
            dve.wait_ge(*fwd_psum.at(3, u))
            nc.vector.tensor_copy(XF[:, cc, :, b * MODES:(b + 1) * MODES],
                                  PS[0:CK, u, 0:2 * MODES].rearrange("p (r m) -> p r m", r=2))\
                .then_inc(fwd_done_odd.sem, 1)

        def shrink(u):
            b, mt = divmod(u, 2)
            dve.wait_ge(*s2_clamped.at(3, u))
            view = "p (c r k) -> p r c k"
            nc.vector.tensor_tensor(O2[:, mt, b, :, :, :], SH[:, 0, u % 2, :].rearrange(view, c=2, r=2),
                                    SH[:, 1, u % 2, :].rearrange(view, c=2, r=2), ALU.subtract)\
                .then_inc(s2_done.sem, 1)

        for u in range(8):
            dve.wait_ge(*s2_psum.at(3, u))
            if u >= 2:
                dve.wait_ge(*s2_done.at(3, u - 2))
            nc.vector.tensor_tensor(SH[:, 0, u % 2, :], PS[0:MT, u, 0:2 * C],
                                    SB2[:, :, :, :].rearrange("p a b c -> p (a b c)"), ALU.add)\
                .then_inc(s2_biased.sem, 1)
            if u:
                shrink(u - 1)
        shrink(7)
        for t in range(TILES):
            dve.wait_ge(*inv_psum.at(3, t))
            nc.vector.tensor_tensor(Y[:, t, :], X[:, t, :], PS[:, t, 0:C], ALU.add).then_inc(y_done.sem, 1)

    @block.tensor
    def _(pe):
        free_by = {}

        def claim(bank, event):
            if bank in free_by:
                pe.wait_ge(*free_by[bank])
            free_by[bank] = event

        def mm(dst, lhsT, rhs, start, stop, loose=False):
            return nc.tensor.matmul(dst, lhsT, rhs, start=start, stop=stop, skip_group_check=loose)

        pe.wait_ge(*first_in.at(0, 2))
        for L, step, i, u, bank in all_steps():
            n, m, D = L.index, mem[L.index], L.dim
            if step == "turn":
                s = i
                for k in range(2):
                    claim(bank + k, xt_done.at(n, 4 * s + 2 * u + k))
                    for t in range(4):
                        pe.wait_ge(*xn_done.at(n, TILES * s + 4 * u + t))
                        last = nc.tensor.transpose(PS[0:CK, bank + k, t * 128:(t + 1) * 128],
                                                   XN[:, 4 * u + t, k * CK:(k + 1) * CK], IDN[:, :])
                    last.then_inc(xt_psum.sem, 1)
            elif step == "v":
                t = i
                pe.wait_ge(*xt_done.at(n, 2 * (t // 4) + 1))
                wide = min(D, 288)
                for g in range(D // wide):
                    claim(bank + g, v_done.at(n, t))
                    for k in range(2):
                        last = mm(PS[:, bank + g, 0:wide], XT[:, k, t * 128:(t + 1) * 128],
                                  WQKV[:, k, 2 * D + g * wide:2 * D + (g + 1) * wide], k == 0, k == 1)
                last.then_inc(v_psum.sem, 1)
            elif step in ("q", "k"):
                c, part = i, int(step == "k")
                pe.wait_ge(*wqkv_in.at(n, 0))
                pe.wait_ge(*xt_done.at(n, 2 * u + 1))
                claim(bank, (k_done if part else q_done).at(n, 2 * c + u))
                for k in range(2):
                    last = mm(PS[0:CK, bank, :], WQKV[:, k, part * D + c * CK:part * D + (c + 1) * CK],
                              XT[:, k, u * 512:(u + 1) * 512], k == 0, k == 1)
                last.then_inc(psum_of[step].sem, 1)
            elif step in ("rh", "rw"):
                c, axis = i, int(step == "rw")
                if n + i + u == 0:
                    pe.wait_ge(*const_in.at(0, 10))
                claim(bank, (rw_done if axis else rh_done).at(n, 2 * c + u))
                pe.wait_ge(*q_done.at(n, 2 * c + 1))
                rows = L.per_chunk * L.win
                qd = image(m["q"][:, :])
                row0 = rows * axis if L.tiles == 2 else 0
                for y in range(8):
                    at = 8 * u + y
                    last = mm(PS[row0:row0 + rows, bank, y * 64:(y + 1) * 64],
                              RB[n][:, axis, at % L.win:at % L.win + L.win, :],
                              qd[:, :, :, at] if axis else qd[:, :, at, :], True, True)
                last.then_inc(psum_of[step].sem, 1)
            elif step == "max":
                h, s = i, i % L.ring
                pe.wait_ge(*aug_at(L, h))
                pe.wait_ge(*aug_const.at(n, const_rows[n] - 1))
                for k in range(2 * u, 2 * u + 2):
                    j, b = TILES * h + k, k // 2
                    claim(MAX_BANK[j % 2], max_done.at(n, j))
                    for tile in range(L.tiles):
                        deep = L.depth[tile] if tile < L.tiles - 1 else L.max_row
                        keys, wide = m["KA"][0:deep, tile, s, b * TOK:(b + 1) * TOK], TOK
                        if L.pads:
                            keys = bass.AP(m["KA"], s * L.keys + b * TOK,
                                           [[L.ring * L.keys, deep], [NT - b * TOK, 2], [1, TOK]])
                            wide = 2 * TOK
                        last = mm(PS[:, MAX_BANK[j % 2], 0:wide], m["QA"][0:deep, tile, s, k * 128:(k + 1) * 128],
                                  keys, tile == 0, tile == L.tiles - 1)
                    last.then_inc(max_psum.sem, 1)
            elif step == "maxT":
                h = i
                pe.wait_ge(*max_done.at(n, TILES * h + TILES - 1))
                claim(TR_BANK, maxT_done.at(n, h))
                nc.tensor.transpose(PS[0:TILES, TR_BANK, 0:128], m["NM"][:, h % 2, :], IDN[:, :])\
                    .then_inc(maxT_psum.sem, 1)
            elif step == "scores":
                h, k, s = i, u, i % L.ring
                pe.wait_ge(*max_row_at(L, h))
                j = L.units * h + k
                claim(L.score_banks[j % len(L.score_banks)], probs_done.at(n, j))
                if k < 4:
                    for b in (2 * (k // 2), 2 * (k // 2) + 1):
                        k0 = b * TOK + (k % 2) * 128
                        for tile, deep in enumerate(L.depth):
                            last = mm(PS[:, L.score_banks[j % len(L.score_banks)], (b % 2) * TOK:(b % 2 + 1) * TOK],
                                      m["KA"][0:deep, tile, s, k0:k0 + 128],
                                      m["QA"][0:deep, tile, s, b * TOK:(b + 1) * TOK],
                                      tile == 0, tile == L.tiles - 1)
                else:
                    q = image(m["QA"][:, 0, s, :])
                    for pc in range(2):
                        keys = m["KA"][:, 0, s, NT + pc * L.pc:NT + (pc + 1) * L.pc]
                        dst = PS[0:L.pc, L.score_banks[j % len(L.score_banks)], pc * NE:(pc + 1) * NE]
                        mm(dst[:, 0:STRIP_A], keys, q[:, :, :, EDGE:], True, True)
                        last = mm(dst[:, STRIP_A:], keys, q[:, :, EDGE:, 0:EDGE], True, True)
                last.then_inc(scores_psum.sem, 1)
            elif step == "pv":
                pair = (i, i + 1)
                if i % L.per_group == 0 and u == 0:
                    for k in range(2):
                        claim(O_BANK[k], o_copied.at(n, 2 * (i // L.per_group) + k))
                pe.wait_ge(*probs_done.at(n, L.units * (i + 1) + (2 * (u // 2) + 1 if u < 4 else 4)))
                o = {(h, k): PS[h % L.per_group * L.slot:(h % L.per_group + 1) * L.slot, O_BANK[k], :]
                     for h in pair for k in range(2)}
                if u < NB:
                    b = u
                    if i == 0 and u == 0:
                        pe.wait_ge(*v_done.at(n, TILES - 1))
                    for kc in range(2):
                        for h in pair:
                            last = mm(o[h, b // 2][:, (b % 2) * TOK:(b % 2 + 1) * TOK], values(L, 2 * b + kc, h),
                                      m["PT"][:, h % 2, kc, b * TOK:(b + 1) * TOK],
                                      b % 2 == 0 and kc == 0, kc == 1, True)
                else:
                    if i == 0:
                        pe.wait_ge(*pad_values.at(n, 0))
                    na, nb = STRIP_A // 2, STRIP_B // 2
                    for k in range(2):
                        for pc in range(2):
                            for h in pair:
                                p = m["PP"][:, h % 2, pc, :]
                                edge = o[h, k].rearrange("r (b y x) -> r b y x", b=2, y=IMG)
                                mm(edge[:, :, :, EDGE:], m["BV"][:, h, :],
                                   p[:, k * na:(k + 1) * na].rearrange("p (b y x) -> p b y x", b=2, y=IMG),
                                   False, False, True)
                            for h in pair:
                                p = m["PP"][:, h % 2, pc, :]
                                edge = o[h, k].rearrange("r (b y x) -> r b y x", b=2, y=IMG)
                                at = STRIP_A + k * nb
                                last = mm(edge[:, :, EDGE:, 0:EDGE], m["BV"][:, h, :],
                                          p[:, at:at + nb].rearrange("p (b y x) -> p b y x", b=2, y=2),
                                          False, True, True)
                last.then_inc(pv_done.sem, 1)
            elif step == "proj":
                t = i
                if t == 0 and u == 0:
                    pe.wait_ge(*wp_in.at(n, 0))
                if u == 0:
                    claim(bank, x_mid.at(n, t))
                groups = (L.groups - 1,) if u else range(L.groups - 1)
                pe.wait_ge(*o_done.at(n, 2 * groups[-1] + t // 4))
                for g in groups:
                    last = mm(PS[:, bank, 0:C], m["OT"][:, g, t * 128:(t + 1) * 128], m["WP"][:, g, :],
                              g == 0, g == L.groups - 1)
                if u:
                    last.then_inc(proj_psum.sem, 1)
            elif step == "up":
                if i == 0 and u == 0:
                    pe.wait_ge(*mlp_in.at(n, 1))
                pe.wait_ge(*xt_done.at(n, 4 + 2 * u + 1))
                claim(bank, gelu_done.at(n, FM * u + i))
                for k in range(2):
                    last = mm(PS[:, bank, :], m["W1"][:, k, i * 128:(i + 1) * 128],
                              XT[:, k, u * 512:(u + 1) * 512], k == 0, k == 1)
                last.then_inc(up_psum.sem, 1)
            elif step == "down":
                t = i
                pe.wait_ge(*gelu_done.at(n, FM * (t // 4 + 1) - 1))
                claim(bank, x_end.at(n, t))
                for g in range(FM):
                    last = mm(PS[:, bank, 0:C], m["HT"][:, g, t * 128:(t + 1) * 128], m["W2"][:, g, :],
                              g == 0, g == FM - 1)
                last.then_inc(down_psum.sem, 1)
        pe.wait_ge(*spectral_in.at(3, 4))
        pe.wait_ge(*x_end.at(2, TILES - 1))
        for bank in range(8):
            claim(bank, x_end.at(2, TILES - 1))
        for u in range(8):
            b, cc = divmod(u, 2)
            for kt in range(2):
                last = mm(PS[0:CK, u, 0:2 * MODES], X[:, 2 * b + kt, cc * CK:(cc + 1) * CK], FW[:, kt, :],
                          kt == 0, kt == 1)
            last.then_inc(fwd_psum.sem, 1)
        pe.wait_ge(*fwd_done.at(3, 3))
        pe.wait_ge(*fwd_done_odd.at(3, 3))
        pe.wait_ge(*w_prep.at(3, 2))
        for u in range(8):
            cc, r, half = u // 4, u // 2 % 2, u % 2
            cols = slice(half * 2 * MODES, (half + 1) * 2 * MODES)
            own, other = (WS[:, 0, cc, 0, :], W1N[:, cc, :] if r == 0 else WS[:, 0, cc, 1, :])
            mm(PS[0:CK, u, 0:2 * MODES], own, XF[:, cc, r, cols], True, False)
            mm(PS[0:CK, u, 0:2 * MODES], other, XF[:, cc, 1 - r, cols], False, True).then_inc(s1_psum.sem, 1)
        pe.wait_ge(*s1_done.at(3, 7))
        for u in range(8):
            b, mt = divmod(u, 2)
            for cc in range(2):
                for r in range(2):
                    m0 = b * MODES + mt * MT
                    last = mm(PS[0:MT, u, cc * C:(cc + 1) * C], O1[:, cc, r, m0:m0 + MT],
                              W2S[:, cc, r, :, :], r == 0, r == 1)
            last.then_inc(s2_psum.sem, 1)
        for t in range(TILES):
            b, half = divmod(t, 2)
            pe.wait_ge(*s2_done.at(3, 2 * b + 1))
            pe.wait_ge(*s2_biased.at(3, 7))
            for i in range(4):
                mt, r = divmod(i, 2)
                last = mm(PS[:, t, 0:C], GI[:, mt, r, half * 128:(half + 1) * 128],
                          O2[:, mt, b, r, :, :], i == 0, i == 3)
            last.then_inc(inv_psum.sem, 1)


def _pack(inputs):
    def f(name):
        return np.asarray(inputs[name])

    def cols(v, parts):
        return v.reshape(-1, parts).T

    def rows(w, parts):
        return w.reshape(-1, parts, w.shape[-1]).transpose(1, 0, 2)

    names = [("L0_conv_", "norm1_g norm1_b norm2_g norm2_b rel_pos_h rel_pos_w proj_w proj_b "
                          "mlp_w1 mlp_b1 mlp_w2 mlp_b2"),
             ("L1_conv_", "ln1_scale ln1_offset ln2_scale ln2_offset rel_pos_0 rel_pos_1 wo bo w1 b1 w2 b2"),
             ("L2_conv_", "g1 beta1 g2 beta2 rel_pos_h rel_pos_w w_proj b_proj w_fc1 b_fc1 w_fc2 b_fc2")]
    arrays = {"x": f("x").reshape(NT, C)}
    for L, (prefix, keys) in zip(LAYERS, names):
        n = L.index
        g1, o1, g2, o2, rh, rw, wp, bp, w1, b1, w2, b2 = (f(prefix + k) for k in keys.split())
        if n == 1:
            wqkv = np.concatenate([f(prefix + k) for k in ("wq", "wk", "wv")], 1)
            bqkv = np.concatenate([f(prefix + k) for k in ("bq", "bk", "bv")])
        else:
            wqkv, bqkv = (f(prefix + k) for k in (("qkv_w", "qkv_b") if n == 0 else ("w_qkv", "b_qkv")))
        col = np.zeros((128, 8 + 2 * L.chunks + FM), np.float32)
        at = 0
        for v, parts in ((g1, CK), (o1, CK), (g2, CK), (o2, CK), (bqkv[:2 * L.dim], CK), (b1, 128)):
            c = cols(v, parts)
            col[:parts, at:at + c.shape[1]] = c
            at += c.shape[1]
        place = np.zeros((L.per_group, L.slot, L.groups, C), np.float32)
        place[:, :L.hd] = wp.reshape(L.groups, L.per_group, L.hd, C).transpose(1, 2, 0, 3)
        place[0, L.hd, 0] = bp
        rb = np.zeros((L.per_chunk, L.hd, 2, L.rel, L.per_chunk), np.float32)
        for i in range(L.per_chunk):
            rb[i, :, 0, :, i] = rh.T
            rb[i, :, 1, :, i] = rw.T
        arrays |= {f"col{n}": col, f"wqkv{n}": rows(wqkv, CK), f"wp{n}": place.reshape(128, L.groups, C),
                   f"rb{n}": rb.reshape(CK, 2, L.rel, L.per_chunk), f"w1_{n}": rows(w1, CK),
                   f"w2_{n}": rows(w2, 128), f"vb{n}": bqkv[2 * L.dim:], f"b2_{n}": b2,
                   f"kc{n}": key_constants(L)}
    arrays["qm"] = query_masks()
    arrays["idn"] = np.eye(128, dtype=np.float32)
    arrays["eps"] = np.tile(np.array([1e-5, 1e-6], np.float32), (128, 1))
    arrays["fwd"], arrays["inv"] = fourier()
    per = CK // BS
    ws = np.zeros((per, BS, 2, 2, 2, per, BS), np.float32)
    for layer, name in enumerate(("w1", "w2")):
        w = f("L3_conv_" + name).reshape(2, 2, per, BS, BS)
        for i in range(per):
            ws[i, :, layer, :, :, i] = w[:, :, i].transpose(2, 1, 0, 3)
    arrays["ws"] = ws.reshape(CK, 2, 2, 2, CK)
    arrays["sb1"] = f("L3_conv_b1").reshape(2, 2, CK).transpose(2, 1, 0)
    arrays["sb2"] = f("L3_conv_b2").reshape(2, 2, CK).transpose(1, 0, 2)
    return {k: np.ascontiguousarray(v) for k, v in arrays.items()}


def kernel(**inputs):
    import concourse.bacc as _bacc
    from concourse.bass_utils import run_bass_kernel_spmd as _run

    nc = _bacc.Bacc("TRN2", target_bir_lowering=False, num_devices=1)
    arrays = _pack(inputs)
    io = {k: nc.dram_tensor(f"in_{k}", v.shape, F32, kind="ExternalInput").ap() for k, v in arrays.items()}
    io["inverses"] = nc.dram_tensor("inverses", (HEADS, NT), F32).ap()
    out = nc.dram_tensor("out_y", (NT, C), F32, kind="ExternalOutput").ap()
    build(nc, io, out)
    r = _run(nc, [{f"in_{k}": v for k, v in arrays.items()}], core_ids=[0])
    return r.results[0]["out_y"].reshape(NB, IMG, IMG, C)
```
